# Optimizing a Trainium2 kernel written in Bass

```python
import numpy as np
import jax
import jax.numpy as jnp

def _softmax(x, axis=-1):
    return jax.nn.softmax(x, axis=axis)

def _gelu(x):
    return jax.nn.gelu(x, approximate=True)

def _silu(x):
    return jax.nn.silu(x)

def _sigmoid(x):
    return jax.nn.sigmoid(x)

def _layernorm(x, axis=-1, eps=1e-05):
    m = jnp.mean(x, axis=axis, keepdims=True)
    v = jnp.var(x, axis=axis, keepdims=True)
    return (x - m) / jnp.sqrt(v + eps)

def _scatter_add(tgt, idx, src, axis=0):
    return tgt.at[idx].add(src)

def _segment_sum(src, seg, n):
    return jax.ops.segment_sum(src, seg, n)
kernel_name = 'mk_seq_postln_d2_jaxref_r8_272728'

def setup_inputs(seed: int=0):
    np.random.seed(seed)
    _w = jnp.asarray

    def _L0_attn_setup():
        import math
        import jax, jax.numpy as jnp
        import numpy as np
        B, S, D, H, DH = (2, 256, 256, 16, 128)

        def _alibi_slopes(n):

            def pow2(m):
                start = 2 ** (-2 ** (-(math.log2(m) - 3)))
                return [start * start ** i for i in range(m)]
            if math.log2(n).is_integer():
                return pow2(n)
            c = 2 ** math.floor(math.log2(n))
            return pow2(c) + _alibi_slopes(2 * c)[0::2][:n - c]

        def _alibi_mask(n_heads, q_len, kv_len):
            slopes = jnp.asarray(np.array(_alibi_slopes(n_heads), dtype=np.float32))
            bias = slopes[:, None, None] * jnp.arange(kv_len, dtype=jnp.float32)[None, None, :]
            i = jnp.arange(q_len)[:, None]
            j = jnp.arange(kv_len)[None, :]
            causal = jnp.where(j > i, -jnp.inf, 0.0).astype(jnp.float32)
            return causal[None, :, :] + bias
        key = jax.random.key(seed)
        k1, k2, k3, k4, k5 = jax.random.split(key, 5)
        scale = 1.0 / math.sqrt(D)
        return {'resid_pre': jax.random.normal(k1, (B, S, D), dtype=jnp.float32), 'Wq': jax.random.normal(k2, (H * DH, D), dtype=jnp.float32) * scale, 'Wk': jax.random.normal(k3, (H * DH, D), dtype=jnp.float32) * scale, 'Wv': jax.random.normal(k4, (H * DH, D), dtype=jnp.float32) * scale, 'Wo': jax.random.normal(k5, (D, H * DH), dtype=jnp.float32) * scale}
    _L0_attn_in = _L0_attn_setup()

    def _L0_ffn_setup():
        import jax, jax.numpy as jnp
        import numpy as np
        EPS = 1e-07
        CURVATURE = 1.0
        MAX_NORM_RATIO = 0.99
        B, L, N, K = (4, 256, 256, 256)

        def _ternary_init(key, n, k):
            rand = jax.random.normal(key, (n, k), dtype=jnp.float32)
            threshold = 0.5 * jnp.mean(jnp.abs(rand))
            return jnp.where(rand > threshold, 1.0, jnp.where(rand < -threshold, -1.0, 0.0)).astype(jnp.float32)
        key = jax.random.key(seed)
        kx, kw = jax.random.split(key)
        x = jax.random.normal(kx, (B, L, N), dtype=jnp.float32)
        weight = _ternary_init(kw, N, K)
        scale = jnp.full((K,), 1.0 / np.sqrt(N), dtype=jnp.float32)
        return {'x': x, 'weight': weight, 'scale': scale}
    _L0_ffn_in = _L0_ffn_setup()

    def _L1_attn_setup():
        import math
        import jax, jax.numpy as jnp
        import numpy as np
        EMBED_DIM = 256
        NUM_HEADS = 16
        HEAD_DIM = EMBED_DIM // NUM_HEADS
        CHUNK = 128
        RMS_EPS = 1e-05

        def _build_slopes(n):

            def pow2(n):
                start = 2.0 ** (-2.0 ** (-(math.log2(n) - 3)))
                return [start * start ** i for i in range(n)]
            if math.log2(n).is_integer():
                s = pow2(n)
            else:
                closest = 2 ** math.floor(math.log2(n))
                s = pow2(closest) + pow2(2 * closest)[0::2][:n - closest]
            return jnp.asarray(s, dtype=jnp.float32)

        def _rotary(x_BTHD, offset=0):
            T, D = (x_BTHD.shape[1], x_BTHD.shape[-1])
            freq = (1.0 / 1024.0) ** jnp.linspace(0.0, 1.0, D // 4, dtype=jnp.float32)
            freq = jnp.concatenate([freq, jnp.zeros(D // 4, dtype=jnp.float32)])
            t = jnp.arange(offset, offset + T, dtype=jnp.float32)
            theta = t[:, None] * freq[None, :]
            cos = jnp.cos(theta)[None, :, None, :]
            sin = jnp.sin(theta)[None, :, None, :]
            x1, x2 = jnp.split(x_BTHD.astype(jnp.float32), 2, axis=-1)
            y1 = x1 * cos + x2 * sin
            y2 = -x1 * sin + x2 * cos
            return jnp.concatenate([y1, y2], axis=-1).astype(x_BTHD.dtype)

        def _lightning_attn(q, k, v, slopes):
            B, H, T, D = q.shape
            C = CHUNK
            NC = T // C
            r = jnp.exp(-slopes)
            i = jnp.arange(C, dtype=jnp.float32)
            q_decay = r[:, None] ** (i[None, :] + 1.0)
            k_decay = r[:, None] ** (C - 1.0 - i[None, :])
            diff = i[:, None] - i[None, :]
            mask = diff >= 0
            dmask = jnp.where(mask[None], r[:, None, None] ** jnp.where(mask, diff, 0.0)[None], 0.0)
            r_C = r ** float(C)

            def reshape_chunks(x):
                return x.reshape(B, H, NC, C, D).transpose(2, 0, 1, 3, 4)
            qc, kc, vc = (reshape_chunks(q), reshape_chunks(k), reshape_chunks(v))

            def step(kv, qkv):
                qi, ki, vi = qkv
                inter = jnp.einsum('bhcd,bhde->bhce', qi * q_decay[None, :, :, None], kv)
                scores = jnp.einsum('bhcd,bhsd->bhcs', qi, ki) * dmask[None]
                intra = jnp.einsum('bhcs,bhse->bhce', scores, vi)
                kv_new = r_C[None, :, None, None] * kv + jnp.einsum('bhcd,bhce->bhde', ki * k_decay[None, :, :, None], vi)
                return (kv_new, inter + intra)
            kv0 = jnp.zeros((B, H, D, D), dtype=q.dtype)
            _, out = jax.lax.scan(step, kv0, (qc, kc, vc))
            return out.transpose(1, 2, 0, 3, 4).reshape(B, H, T, D)

        def _rms_norm(x, w):
            var = jnp.mean(jnp.square(x), axis=-1, keepdims=True)
            return x * jax.lax.rsqrt(var + RMS_EPS) * w
        key = jax.random.key(seed)
        ks = jax.random.split(key, 6)
        sc = 1.0 / math.sqrt(EMBED_DIM)
        return {'x': jax.random.normal(ks[0], (4, 512, EMBED_DIM), dtype=jnp.float32), 'Wq': jax.random.normal(ks[1], (EMBED_DIM, EMBED_DIM), dtype=jnp.float32) * sc, 'Wk': jax.random.normal(ks[2], (EMBED_DIM, EMBED_DIM), dtype=jnp.float32) * sc, 'Wv': jax.random.normal(ks[3], (EMBED_DIM, EMBED_DIM), dtype=jnp.float32) * sc, 'Wo': jax.random.normal(ks[4], (EMBED_DIM, EMBED_DIM), dtype=jnp.float32) * sc, 'rms_w': jnp.ones((EMBED_DIM,), dtype=jnp.float32)}
    _L1_attn_in = _L1_attn_setup()

    def _L1_ffn_setup():
        import jax, jax.numpy as jnp
        import numpy as np
        E = 8
        TOP_K = 2
        H = 256
        I_MOE = 176
        I_SH = 704
        B, S = (2, 256)

        def _moe_forward(hidden_states, router_weight, gate_up_proj, down_proj, sh_gate_w, sh_up_w, sh_down_w, shared_gate_w):
            b, s, h = hidden_states.shape
            x = hidden_states.reshape(-1, h)
            shared = jnp.einsum('ti,hi->th', jax.nn.silu(x @ sh_gate_w.T) * (x @ sh_up_w.T), sh_down_w)
            logits = x @ router_weight.T
            probs = jax.nn.softmax(logits.astype(jnp.float32), axis=-1)
            top_v, top_i = jax.lax.top_k(probs, TOP_K)
            top_v = top_v / top_v.sum(axis=-1, keepdims=True)
            combine = (jax.nn.one_hot(top_i, E, dtype=top_v.dtype) * top_v[..., None]).sum(axis=1)
            out = jnp.zeros_like(x)
            for e in range(E):
                gu = x @ gate_up_proj[e].T
                gate, up = (gu[:, :I_MOE], gu[:, I_MOE:])
                cur = jax.nn.silu(gate) * up @ down_proj[e].T
                out = out + cur * combine[:, e:e + 1]
            out = out + jax.nn.sigmoid(x @ shared_gate_w.T) * shared
            return out.reshape(b, s, h)
        key = jax.random.key(seed)
        ks = jax.random.split(key, 8)
        scale = 0.02
        return {'hidden_states': jax.random.normal(ks[0], (B, S, H), dtype=jnp.float32), 'router_weight': jax.random.normal(ks[1], (E, H), dtype=jnp.float32) * scale, 'gate_up_proj': jax.random.normal(ks[2], (E, 2 * I_MOE, H), dtype=jnp.float32) * scale, 'down_proj': jax.random.normal(ks[3], (E, H, I_MOE), dtype=jnp.float32) * scale, 'sh_gate_w': jax.random.normal(ks[4], (I_SH, H), dtype=jnp.float32) * scale, 'sh_up_w': jax.random.normal(ks[5], (I_SH, H), dtype=jnp.float32) * scale, 'sh_down_w': jax.random.normal(ks[6], (H, I_SH), dtype=jnp.float32) * scale, 'shared_gate_w': jax.random.normal(ks[7], (1, H), dtype=jnp.float32) * scale}
    _L1_ffn_in = _L1_ffn_setup()
    _d = {'L0_attn_resid_pre': _L0_attn_in['resid_pre'], 'L0_attn_Wq': _L0_attn_in['Wq'], 'L0_attn_Wk': _L0_attn_in['Wk'], 'L0_attn_Wv': _L0_attn_in['Wv'], 'L0_attn_Wo': _L0_attn_in['Wo'], 'L0_ffn_weight': _L0_ffn_in['weight'], 'L0_ffn_scale': _L0_ffn_in['scale'], 'L1_attn_Wq': _L1_attn_in['Wq'], 'L1_attn_Wk': _L1_attn_in['Wk'], 'L1_attn_Wv': _L1_attn_in['Wv'], 'L1_attn_Wo': _L1_attn_in['Wo'], 'L1_attn_rms_w': _L1_attn_in['rms_w'], 'L1_ffn_router_weight': _L1_ffn_in['router_weight'], 'L1_ffn_gate_up_proj': _L1_ffn_in['gate_up_proj'], 'L1_ffn_down_proj': _L1_ffn_in['down_proj'], 'L1_ffn_sh_gate_w': _L1_ffn_in['sh_gate_w'], 'L1_ffn_sh_up_w': _L1_ffn_in['sh_up_w'], 'L1_ffn_sh_down_w': _L1_ffn_in['sh_down_w'], 'L1_ffn_shared_gate_w': _L1_ffn_in['shared_gate_w']}
    _x0 = _d['L0_attn_resid_pre']
    _d['L0_attn_resid_pre'] = jax.random.normal(jax.random.fold_in(jax.random.key(seed), 1), (8, 512, 256), dtype=_x0.dtype)
    del _x0
    return _d

def reference(L0_attn_resid_pre, L0_attn_Wq, L0_attn_Wk, L0_attn_Wv, L0_attn_Wo, L0_ffn_weight, L0_ffn_scale, L1_attn_Wq, L1_attn_Wk, L1_attn_Wv, L1_attn_Wo, L1_attn_rms_w, L1_ffn_router_weight, L1_ffn_gate_up_proj, L1_ffn_down_proj, L1_ffn_sh_gate_w, L1_ffn_sh_up_w, L1_ffn_sh_down_w, L1_ffn_shared_gate_w):

    def _L0_attn_ref(resid_pre, Wq, Wk, Wv, Wo):
        import math
        import jax, jax.numpy as jnp
        import numpy as np
        B, S, D, H, DH = (2, 256, 256, 16, 128)

        def _alibi_slopes(n):

            def pow2(m):
                start = 2 ** (-2 ** (-(math.log2(m) - 3)))
                return [start * start ** i for i in range(m)]
            if math.log2(n).is_integer():
                return pow2(n)
            c = 2 ** math.floor(math.log2(n))
            return pow2(c) + _alibi_slopes(2 * c)[0::2][:n - c]

        def _alibi_mask(n_heads, q_len, kv_len):
            slopes = jnp.asarray(np.array(_alibi_slopes(n_heads), dtype=np.float32))
            bias = slopes[:, None, None] * jnp.arange(kv_len, dtype=jnp.float32)[None, None, :]
            i = jnp.arange(q_len)[:, None]
            j = jnp.arange(kv_len)[None, :]
            causal = jnp.where(j > i, -jnp.inf, 0.0).astype(jnp.float32)
            return causal[None, :, :] + bias
        b, s, d = resid_pre.shape
        q = (resid_pre @ Wq.T).reshape(b, s, H, DH)
        k = (resid_pre @ Wk.T).reshape(b, s, H, DH)
        v = (resid_pre @ Wv.T).reshape(b, s, H, DH)
        scores = jnp.einsum('bqhd,bkhd->bhqk', q, k) / math.sqrt(DH)
        scores = jnp.clip(scores, -1024.0, 1024.0)
        scores = scores + _alibi_mask(H, s, s)[None]
        attn = jax.nn.softmax(scores.astype(jnp.float32), axis=-1).astype(q.dtype)
        z = jnp.einsum('bhqk,bkhd->bqhd', attn, v)
        out = jnp.einsum('bqhd,ohd->bqo', z, Wo.reshape(d, H, DH))
        return out

    def _L0_ffn_ref(x, weight, scale):
        import jax, jax.numpy as jnp
        import numpy as np
        EPS = 1e-07
        CURVATURE = 1.0
        MAX_NORM_RATIO = 0.99
        B, L, N, K = (4, 256, 256, 256)

        def _ternary_init(key, n, k):
            rand = jax.random.normal(key, (n, k), dtype=jnp.float32)
            threshold = 0.5 * jnp.mean(jnp.abs(rand))
            return jnp.where(rand > threshold, 1.0, jnp.where(rand < -threshold, -1.0, 0.0)).astype(jnp.float32)
        sqrt_c = jnp.sqrt(jnp.float32(CURVATURE))
        out = jnp.einsum('bln,nk->blk', x, weight) * scale
        v_norm = jnp.maximum(jnp.linalg.norm(out, axis=-1, keepdims=True), EPS)
        scaled_norm = sqrt_c * v_norm
        out = out * (jnp.tanh(scaled_norm) / (scaled_norm + EPS))
        max_norm = MAX_NORM_RATIO / sqrt_c
        o_norm = jnp.maximum(jnp.linalg.norm(out, axis=-1, keepdims=True), EPS)
        out = out * jnp.minimum(max_norm / o_norm, 1.0)
        return out.astype(x.dtype)

    def _L1_attn_ref(x, Wq, Wk, Wv, Wo, rms_w):
        import math
        import jax, jax.numpy as jnp
        import numpy as np
        EMBED_DIM = 256
        NUM_HEADS = 16
        HEAD_DIM = EMBED_DIM // NUM_HEADS
        CHUNK = 128
        RMS_EPS = 1e-05

        def _build_slopes(n):

            def pow2(n):
                start = 2.0 ** (-2.0 ** (-(math.log2(n) - 3)))
                return [start * start ** i for i in range(n)]
            if math.log2(n).is_integer():
                s = pow2(n)
            else:
                closest = 2 ** math.floor(math.log2(n))
                s = pow2(closest) + pow2(2 * closest)[0::2][:n - closest]
            return jnp.asarray(s, dtype=jnp.float32)

        def _rotary(x_BTHD, offset=0):
            T, D = (x_BTHD.shape[1], x_BTHD.shape[-1])
            freq = (1.0 / 1024.0) ** jnp.linspace(0.0, 1.0, D // 4, dtype=jnp.float32)
            freq = jnp.concatenate([freq, jnp.zeros(D // 4, dtype=jnp.float32)])
            t = jnp.arange(offset, offset + T, dtype=jnp.float32)
            theta = t[:, None] * freq[None, :]
            cos = jnp.cos(theta)[None, :, None, :]
            sin = jnp.sin(theta)[None, :, None, :]
            x1, x2 = jnp.split(x_BTHD.astype(jnp.float32), 2, axis=-1)
            y1 = x1 * cos + x2 * sin
            y2 = -x1 * sin + x2 * cos
            return jnp.concatenate([y1, y2], axis=-1).astype(x_BTHD.dtype)

        def _lightning_attn(q, k, v, slopes):
            B, H, T, D = q.shape
            C = CHUNK
            NC = T // C
            r = jnp.exp(-slopes)
            i = jnp.arange(C, dtype=jnp.float32)
            q_decay = r[:, None] ** (i[None, :] + 1.0)
            k_decay = r[:, None] ** (C - 1.0 - i[None, :])
            diff = i[:, None] - i[None, :]
            mask = diff >= 0
            dmask = jnp.where(mask[None], r[:, None, None] ** jnp.where(mask, diff, 0.0)[None], 0.0)
            r_C = r ** float(C)

            def reshape_chunks(x):
                return x.reshape(B, H, NC, C, D).transpose(2, 0, 1, 3, 4)
            qc, kc, vc = (reshape_chunks(q), reshape_chunks(k), reshape_chunks(v))

            def step(kv, qkv):
                qi, ki, vi = qkv
                inter = jnp.einsum('bhcd,bhde->bhce', qi * q_decay[None, :, :, None], kv)
                scores = jnp.einsum('bhcd,bhsd->bhcs', qi, ki) * dmask[None]
                intra = jnp.einsum('bhcs,bhse->bhce', scores, vi)
                kv_new = r_C[None, :, None, None] * kv + jnp.einsum('bhcd,bhce->bhde', ki * k_decay[None, :, :, None], vi)
                return (kv_new, inter + intra)
            kv0 = jnp.zeros((B, H, D, D), dtype=q.dtype)
            _, out = jax.lax.scan(step, kv0, (qc, kc, vc))
            return out.transpose(1, 2, 0, 3, 4).reshape(B, H, T, D)

        def _rms_norm(x, w):
            var = jnp.mean(jnp.square(x), axis=-1, keepdims=True)
            return x * jax.lax.rsqrt(var + RMS_EPS) * w
        B, T, E = x.shape
        H, D = (NUM_HEADS, HEAD_DIM)
        q = (x @ Wq).reshape(B, T, H, D)
        k = (x @ Wk).reshape(B, T, H, D)
        v = (x @ Wv).reshape(B, T, H, D)
        q = _rotary(q)
        k = _rotary(k)
        q, k, v = (t.transpose(0, 2, 1, 3) for t in (q, k, v))
        slopes = _build_slopes(H)
        attn = _lightning_attn(q, k, v, slopes)
        attn = attn.transpose(0, 2, 1, 3).reshape(B, T, E)
        attn = _rms_norm(attn, rms_w)
        return attn @ Wo

    def _L1_ffn_ref(hidden_states, router_weight, gate_up_proj, down_proj, sh_gate_w, sh_up_w, sh_down_w, shared_gate_w):
        import jax, jax.numpy as jnp
        import numpy as np
        E = 8
        TOP_K = 2
        H = 256
        I_MOE = 176
        I_SH = 704
        B, S = (2, 256)

        def _moe_forward(hidden_states, router_weight, gate_up_proj, down_proj, sh_gate_w, sh_up_w, sh_down_w, shared_gate_w):
            b, s, h = hidden_states.shape
            x = hidden_states.reshape(-1, h)
            shared = jnp.einsum('ti,hi->th', jax.nn.silu(x @ sh_gate_w.T) * (x @ sh_up_w.T), sh_down_w)
            logits = x @ router_weight.T
            probs = jax.nn.softmax(logits.astype(jnp.float32), axis=-1)
            top_v, top_i = jax.lax.top_k(probs, TOP_K)
            top_v = top_v / top_v.sum(axis=-1, keepdims=True)
            combine = (jax.nn.one_hot(top_i, E, dtype=top_v.dtype) * top_v[..., None]).sum(axis=1)
            out = jnp.zeros_like(x)
            for e in range(E):
                gu = x @ gate_up_proj[e].T
                gate, up = (gu[:, :I_MOE], gu[:, I_MOE:])
                cur = jax.nn.silu(gate) * up @ down_proj[e].T
                out = out + cur * combine[:, e:e + 1]
            out = out + jax.nn.sigmoid(x @ shared_gate_w.T) * shared
            return out.reshape(b, s, h)
        return _moe_forward(hidden_states, router_weight, gate_up_proj, down_proj, sh_gate_w, sh_up_w, sh_down_w, shared_gate_w)
    x = L0_attn_resid_pre
    x = _layernorm(x + _L0_attn_ref(x, L0_attn_Wq, L0_attn_Wk, L0_attn_Wv, L0_attn_Wo), axis=-1)
    x = _layernorm(x + _L0_ffn_ref(x, L0_ffn_weight, L0_ffn_scale), axis=-1)
    x = _layernorm(x + _L1_attn_ref(x, L1_attn_Wq, L1_attn_Wk, L1_attn_Wv, L1_attn_Wo, L1_attn_rms_w), axis=-1)
    x = _layernorm(x + _L1_ffn_ref(x, L1_ffn_router_weight, L1_ffn_gate_up_proj, L1_ffn_down_proj, L1_ffn_sh_gate_w, L1_ffn_sh_up_w, L1_ffn_sh_down_w, L1_ffn_shared_gate_w), axis=-1)
    return x

_drawn_inputs = setup_inputs


def setup_inputs(seed=0):
    import zlib

    import numpy as np

    out = dict(_drawn_inputs(seed))
    spreads = {'L0_ffn_scale': (0.0625, 0.6), 'L1_attn_rms_w': (1.0, 0.2)}
    factors = {'L1_ffn_router_weight': 6.564,
     'L1_ffn_gate_up_proj': 5.688,
     'L1_ffn_down_proj': 5.691,
     'L1_ffn_sh_gate_w': 3.869,
     'L1_ffn_sh_up_w': 3.642,
     'L1_ffn_sh_down_w': 3.645,
     'L1_ffn_shared_gate_w': 8.0}
    for name, (base, spread) in spreads.items():
        noise = np.random.default_rng([zlib.crc32(name.encode()), seed]).standard_normal(out[name].shape)
        drawn = base * np.exp(spread * noise) if base else spread * noise
        out[name] = jnp.asarray(drawn.astype(out[name].dtype))
    for name, factor in factors.items():
        out[name] = (out[name] * factor).astype(out[name].dtype)
    return out
```

```python
from contextlib import ExitStack

import numpy as np

import concourse.bass as bass
from concourse import mybir

F32 = mybir.dt.float32
F32R = mybir.dt.float32r
ALU = mybir.AluOpType
ACT = mybir.ActivationFunctionType
AX = mybir.AxisListType

P = 128
D = 256
KC = D // P
S = 512
T = S // P

H0 = 16
DH = 128
PAIRS = H0 // 2
CLIP = 1024.0
MASKED = 1e30
BIG = 3e38

PASSES = ((1, 0), (0, 1), (0, 0))
HI, LO = 0, 1


class Space:

    def __init__(self, nc, stack, prefix):
        self.nc, self.stack, self.prefix = nc, stack, prefix

    def sb(self, name, shape, dt=F32):
        return self.stack.enter_context(self.nc.sbuf_tensor(self.prefix + name, shape, dt))

    def ps(self, name, shape, dt=F32):
        return self.stack.enter_context(self.nc.psum_tensor(self.prefix + name, shape, dt))

    def sem(self, name):
        return self.stack.enter_context(self.nc.semaphore(self.prefix + name))


def softmax_attention(nc, x_tokens, x_t, w_heads, slopes, y_scratch):
    batches = x_tokens.shape[0] - 1
    with ExitStack() as stack:
        m = Space(nc, stack, "attention_")
        w_qk = m.sb("w_qk", [P, H0 * 2 * 2 * KC * DH], F32R)
        w_v = [m.sb(f"w_v_{x}", [P, KC, H0 * DH], F32R) for x in ("hi", "lo")]
        w_o = [m.sb(f"w_o_{x}", [P, H0 * D], F32R) for x in ("hi", "lo")]
        split_weights(nc, w_heads, w_qk, w_v, w_o)
        attend(nc, m, batches, x_tokens, x_t, slopes, y_scratch, w_qk, w_v, w_o)


def split_weights(nc, w_heads, w_qk, w_v, w_o):
    SLOTS = 4
    QK, V, O = 2 * KC * DH, KC * DH, D
    with ExitStack() as stack:
        m = Space(nc, stack, "attention_split_")
        raw = [m.sb(f"raw_{i}", [P, QK + V + O]) for i in range(SLOTS)]
        loaded = [m.sem(f"raw_loaded_{i}") for i in range(SLOTS)]
        high_done = m.sem("w_high_done")
        low_done = m.sem("w_low_done")
        block = stack.enter_context(nc.Block())

        def parts(h, part):
            yield w_qk[:, (2 * h + part) * QK:(2 * h + part + 1) * QK], 0, QK
            yield w_v[part][:, :, h * DH:(h + 1) * DH], QK, V
            yield w_o[part][:, h * O:(h + 1) * O], QK + V, O

        def piece(i, at, n):
            r = raw[i][:, at:at + n]
            return r.rearrange("p (c n) -> p c n", c=KC) if n == V and at == QK else r

        @block.sync
        def _(sp):
            for h in range(H0):
                if h >= SLOTS:
                    sp.wait_ge(low_done, h - SLOTS + 1)
                sp.dma_start(raw[h % SLOTS][:], w_heads[h]).then_inc(loaded[h % SLOTS], 16)

        @block.scalar
        def _(act):
            for h in range(H0):
                act.wait_ge(loaded[h % SLOTS], 16 * (h // SLOTS + 1))
                for n, (dst, at, size) in enumerate(parts(h, HI)):
                    last = act.activation(dst, piece(h % SLOTS, at, size), ACT.Copy)
                last.then_inc(high_done, 1)

        @block.vector
        def _(dve):
            for h in range(H0):
                dve.wait_ge(high_done, h + 1)
                for (dst, at, size), (high, _, _) in zip(parts(h, LO), parts(h, HI)):
                    last = dve.tensor_tensor(dst, piece(h % SLOTS, at, size), high.bitcast(F32), ALU.subtract)
                last.then_inc(low_done, 1)


def attend(nc, m, batches, x_tokens, x_t, slopes, y_scratch, w_qk, w_v, w_o):
    QK = 2 * KC * DH
    stage = [m.sb(f"w_stage_{s}", [P, 2, 2, KC, DH], F32R) for s in "ab"]
    xt_raw = m.sb("xt_raw", [P, KC, S])
    xt = [m.sb(f"xt_{x}", [P, KC, S], F32R) for x in ("hi", "lo")]
    y = m.sb("y_tokens", [P, T, D])
    q = [[m.sb(f"q_{s}_{x}", [P, S], F32R) for x in ("hi", "lo")] for s in "ab"]
    k = [[m.sb(f"k_{s}_{x}", [P, S], F32R) for x in ("hi", "lo")] for s in "ab"]
    v = [m.sb(f"v_{x}", [P, T, 2 * DH], F32R) for x in ("hi", "lo")]
    z = [m.sb(f"z_{x}", [P, S], F32R) for x in ("hi", "lo")]
    pt = [m.sb(f"probs_t_{x}", [P, T, S], F32R) for x in ("hi", "lo")]
    WIDTH = [(t + 1) * P for t in range(T)]
    AT = [sum(WIDTH[:t]) for t in range(T)]
    probs = m.sb("probs", [P, sum(WIDTH)])
    distance = m.sb("distance", [P, S])
    bias = [m.sb(f"bias_{s}", [P, S]) for s in "ab"]
    slope = m.sb("slope", [P, H0])
    ident = m.sb("ident", [P, P])
    count = bias[0][:].bitcast(mybir.dt.int32)
    zeros = m.sb("zeros", [P, 2], F32R)
    low = m.sb("lowest", [P, 2 * T])
    total = m.sb("total", [P, 2 * T])
    inverse = m.sb("inverse", [P, 2 * T])
    scores = [m.ps(f"scores_{i}", [P, S]) for i in range(2)]
    turned = [m.ps(f"turned_{i}", [P, S]) for i in range(2)]
    proj = [m.ps(f"proj_{i}", [P, S]) for i in range(2)]
    out = [m.ps(f"out_{i}", [P, 2, D]) for i in range(2)]

    consts = m.sem("consts")
    stage_in = [m.sem(f"stage_{s}_in") for s in "ab"]
    xt_in, x_in = m.sem("xt_in"), m.sem("x_in")
    xt_high, xt_split = m.sem("xt_high"), m.sem("xt_split")
    proj_ready, proj_high, proj_low = m.sem("proj_ready"), m.sem("proj_high"), m.sem("proj_low")
    scores_ready, scores_clipped = m.sem("scores_ready"), m.sem("scores_clipped")
    biased, exp_done, inverse_done = m.sem("biased"), m.sem("exp_done"), m.sem("inverse_done")
    dve_passed, pool_passed = m.sem("dve_passed"), m.sem("pool_passed")
    bias_ready, probs_ready = m.sem("bias_ready"), m.sem("probs_ready")
    turned_ready, turned_high, turned_low = m.sem("turned_ready"), m.sem("turned_high"), m.sem("turned_low")
    out_ready, y_ready, y_stored = m.sem("out_ready"), m.sem("y_ready"), m.sem("y_stored")

    STEP = 8
    Q_B, K_B, Z_A, Q_A, K_A, Z_B, V_0, V_1 = range(STEP)
    AHEAD = 4
    FREE = 2
    HEAD_UNIT = STEP // 2

    block = m.stack.enter_context(nc.Block())

    def numbers(eng, b, i):
        return eng.snap(b * (PAIRS * STEP) + i * STEP)

    @block.sync
    def _(sp):
        def weights(head):
            return w_qk[:, bass.ds(head * (2 * QK), 2 * QK)]

        def load_stage(slot, src):
            dst = stage[slot][:].rearrange("p a b c d -> p (a b c d)")
            sp.dma_start(dst.bitcast(F32), src.bitcast(F32)).then_inc(stage_in[slot], 16)

        def tokens(dram):
            return dram.rearrange("(t p) d -> p t d", p=P)

        sp.dma_start(xt_raw[:], x_t[0]).then_inc(xt_in, 16)
        load_stage(0, weights(0))
        load_stage(1, weights(1))
        sp.dma_start(slope[:], slopes).then_inc(consts, 16)
        sp.dma_start(y[:], tokens(x_tokens[0])).then_inc(x_in, 16)

        def step(n, next_a, next_b):
            sp.wait_ge(proj_ready, n + 2)
            load_stage(0, weights(next_a))
            sp.wait_ge(proj_ready, n + AHEAD + K_B + 1)
            load_stage(1, weights(next_b))

        with sp.Fori(0, batches) as b:
            sp.wait_ge(xt_split, b + 1)
            sp.dma_start(xt_raw[:], x_t[b + 1]).then_inc(xt_in, 16)
            with sp.Fori(0, PAIRS - 1) as i:
                step(numbers(sp, b, i), 2 * i + 2, 2 * i + 3)
            step(numbers(sp, b, PAIRS - 1), 0, 1)
            sp.wait_ge(y_ready, b + 1)
            sp.dma_start(tokens(y_scratch[b]), y[:]).then_inc(y_stored, 16)
            sp.wait_ge(y_stored, 16 * b + 16)
            sp.dma_start(y[:], tokens(x_tokens[b + 1])).then_inc(x_in, 16)
        sp.wait_ge(xt_in, 16 * (batches + 1))
        sp.wait_ge(x_in, 16 * (batches + 1))
        for s in range(2):
            sp.wait_ge(stage_in[s], 16 * (batches * PAIRS + 1))

    @block.gpsimd
    def _(pool):
        pool.memset(ident[:], 0.0).then_inc(consts, 1)
        pool.memset(zeros[:].bitcast(F32), 0.0).then_inc(consts, 1)
        pool.iota(count[:], pattern=[[-1, S]], base=S - P, channel_multiplier=0).then_inc(consts, 1)
        pool.wait_ge(consts, 16 + 3)
        pool.affine_select(ident[:], ident[:], compare_op=ALU.not_equal, fill=1.0, base=0,
                           pattern=[[-1, P]], channel_multiplier=1).then_inc(consts, 1)
        pool.tensor_copy(distance[:], count[:]).then_inc(consts, 1)
        pool.wait_ge(consts, 16 + 5)
        pool.affine_select(distance[:], distance[:], compare_op=ALU.is_ge, fill=MASKED, base=S - P,
                           pattern=[[-1, S]], channel_multiplier=1).then_inc(consts, 1)
        pool.wait_ge(consts, 16 + 6)

        def head_bias(slot, head):
            s = slope[:, bass.ds(head, 1)].broadcast_to([P, S])
            pool.tensor_tensor(bias[slot][:], distance[:], s, ALU.mult).then_inc(bias_ready, HEAD_UNIT)

        def normalise(tile, slot):
            for t in range(T):
                pool.wait_ge(inverse_done, tile + t + 1)
                pool.sem_inc(pool_passed, 1)
                p = probs[:, AT[t]:AT[t] + WIDTH[t]]
                pool.tensor_scalar(p, p, inverse[:, slot * T + t:slot * T + t + 1], 1.0,
                                   ALU.mult, ALU.mult).then_inc(probs_ready, 1)

        head_bias(0, 0)
        head_bias(1, 1)
        normalise(0, 0)

        def step(n, next_a, next_b):
            pool.wait_ge(biased, n + T)
            head_bias(0, next_a)
            normalise(n + T, 1)
            pool.wait_ge(biased, n + 2 * T)
            head_bias(1, next_b)
            normalise(n + 2 * T, 0)

        with pool.Fori(0, batches) as b:
            with pool.Fori(0, PAIRS - 1) as i:
                step(numbers(pool, b, i), 2 * i + 2, 2 * i + 3)
            step(numbers(pool, b, PAIRS - 1), 0, 1)

    @block.tensor
    def _(pe):
        def projection(unit, slot, which):
            for n, (a, b) in enumerate((p, c) for c in range(KC) for p in PASSES):
                last = pe.matmul(proj[unit % 2][:], stage[slot][:, a[0], which, b], xt[a[1]][:, b],
                                 start=(n == 0), stop=(n == 3 * KC - 1))
            last.then_inc(proj_ready, 1)

        def values(half, col):
            for t in range(2):
                at = (2 * half + t) * P
                for n, (a, c) in enumerate((p, c) for c in range(KC) for p in PASSES):
                    last = pe.matmul(proj[half][:, t * 2 * DH:(t + 1) * 2 * DH], xt[a[0]][:, c, at:at + P],
                                     w_v[a[1]][:, c, bass.ds(col, 2 * DH)],
                                     start=(n == 0), stop=(n == 3 * KC - 1))
            last.then_inc(proj_ready, 1)

        def score_tile(slot, t):
            for n, a in enumerate(PASSES):
                last = pe.matmul(scores[t % 2][:, 0:WIDTH[t]], q[slot][a[0]][:, t * P:(t + 1) * P],
                                 k[slot][a[1]][:, 0:WIDTH[t]], start=(n == 0), stop=(n == 2))
            last.then_inc(scores_ready, 1)

        def turn(tile):
            for t in range(T):
                pe.wait_ge(probs_ready, tile + t + 1)
                pe.wait_ge(turned_low, tile + t - 1 + FREE)
                for c in range(t + 1):
                    last = pe.transpose(turned[t % 2][:, c * P:(c + 1) * P],
                                        probs[:, AT[t] + c * P:AT[t] + (c + 1) * P], ident[:])
                last.then_inc(turned_ready, 1)

        def attended(unit, slot):
            for c in range(T):
                for n, a in enumerate(PASSES):
                    last = pe.matmul(proj[unit % 2][:, c * P:S], v[a[0]][:, c, slot * DH:(slot + 1) * DH],
                                     pt[a[1]][:, c, c * P:S], start=(c == 0 and n == 0),
                                     stop=(c == T - 1 and n == 2))
            last.then_inc(proj_ready, 1)

        def project_out(col):
            for t in range(T):
                for a in PASSES:
                    last = pe.matmul(out[t // 2][:, t % 2], z[a[0]][:, t * P:(t + 1) * P],
                                     w_o[a[1]][:, bass.ds(col, D)], start=False, stop=False,
                                     skip_group_check=True)
            return last

        def clear_out():
            for bank in out:
                pe.matmul(bank[:, 0, 0:2], w_qk[:, 0:P], zeros[:], start=True, stop=True,
                          skip_group_check=True)

        def free_bank(n, unit):
            pe.wait_ge(proj_low, n + AHEAD + unit - 1)

        pe.wait_ge(consts, 16 + 6)
        pe.wait_ge(xt_split, 1)
        pe.wait_ge(stage_in[0], 16)
        projection(0, 0, 0)
        projection(1, 0, 1)
        for half in range(2):
            pe.wait_ge(proj_low, half + 1)
            values(half, 0)
        clear_out()
        for t in range(T):
            if t >= 2:
                pe.wait_ge(scores_clipped, t - 1)
            score_tile(0, t)

        def step(b, n, i, last_pair):
            pe.wait_ge(stage_in[1], 2 * n + 16)
            for unit, which in ((Q_B, 0), (K_B, 1)):
                free_bank(n, unit)
                projection(unit, 1, which)
            turn(n)
            pe.wait_ge(proj_low, n + AHEAD + K_B + 1)
            for t in range(T):
                pe.wait_ge(scores_clipped, n + T + t - 1)
                score_tile(1, t)
            free_bank(n, Z_A)
            pe.wait_ge(turned_low, n + T + FREE)
            attended(Z_A, 0)
            pe.wait_ge(stage_in[0], 2 * n + 32)
            if last_pair:
                pe.wait_ge(xt_split, b + 2)
            for unit, which in ((Q_A, 0), (K_A, 1)):
                free_bank(n, unit)
                projection(unit, 0, which)
            pe.wait_ge(proj_low, n + AHEAD + Z_A + 1)
            project_out(i * (2 * D))
            turn(n + T)
            free_bank(n, Z_B)
            pe.wait_ge(turned_low, n + 2 * T + FREE)
            attended(Z_B, 1)
            pe.wait_ge(proj_low, n + AHEAD + K_A + 1)
            for t in range(T):
                pe.wait_ge(scores_clipped, n + 2 * T + t - 1)
                score_tile(0, t)
            for half, unit in enumerate((V_0, V_1)):
                free_bank(n, unit)
                values(half, 0 if last_pair else i * (2 * DH) + 2 * DH)
            pe.wait_ge(proj_low, n + AHEAD + Z_B + 1)
            last = project_out(i * (2 * D) + D)
            if last_pair:
                last.then_inc(out_ready, 1)

        with pe.Fori(0, batches) as b:
            with pe.Fori(0, PAIRS - 1) as i:
                step(b, numbers(pe, b, i), i, False)
            step(b, numbers(pe, b, PAIRS - 1), PAIRS - 1, True)
            pe.wait_ge(y_ready, b + 1)
            clear_out()

    NEGATIVE_SCALE = -1.0 / DH ** 0.5

    def unit_target(number, unit):
        bank = proj[number % 2][:]
        if unit in (V_0, V_1):
            t = 2 * (unit - V_0)
            return bank.rearrange("p (t n) -> p t n", t=2), [x[:, t:t + 2] for x in v], 1.0
        if unit in (Q_A, Q_B):
            return bank, [x[:] for x in q[unit == Q_B]], NEGATIVE_SCALE
        if unit in (K_A, K_B):
            return bank, [x[:] for x in k[unit == K_B]], 1.0
        return bank, [x[:] for x in z], 1.0

    @block.scalar
    def _(act):
        def split_x(b):
            act.wait_ge(xt_in, 16 * b + 16)
            act.activation(xt[HI][:], xt_raw[:], ACT.Copy).then_inc(xt_high, 1)

        def unit_high(number, unit, before=0):
            bank, dst, scale = unit_target(number, unit)
            act.wait_ge(proj_ready, before + number + 1)
            act.activation(dst[HI], bank, ACT.Copy, scale=scale).then_inc(proj_high, 1)

        def exponentials(tile, slot, t):
            act.wait_ge(biased, tile + t + 1)
            p = probs[:, AT[t]:AT[t] + WIDTH[t]]
            c = slot * T + t
            act.activation(p, p, ACT.Exp, bias=low[:, c:c + 1], scale=-1.0,
                           accum_out=total[:, c:c + 1]).then_inc(exp_done, 1)

        def turned_to_high(tile):
            for t in range(T):
                act.wait_ge(turned_ready, tile + t + 1)
                act.activation(pt[HI][:, 0:t + 1, t * P:(t + 1) * P],
                               turned[t % 2][:, 0:WIDTH[t]].rearrange("p (c n) -> p c n", c=t + 1),
                               ACT.Copy).then_inc(turned_high, 1)

        split_x(0)
        for number, unit in enumerate((Q_A, K_A, V_0, V_1)):
            unit_high(number, unit)
        for t in range(T):
            exponentials(0, 0, t)

        def step(b, n, last_pair):
            unit_high(AHEAD + Q_B, Q_B, n)
            unit_high(AHEAD + K_B, K_B, n)
            if last_pair:
                split_x(b + 1)
            turned_to_high(n)
            exponentials(n + T, 1, 0)
            exponentials(n + T, 1, 1)
            unit_high(AHEAD + Z_A, Z_A, n)
            exponentials(n + T, 1, 2)
            unit_high(AHEAD + Q_A, Q_A, n)
            exponentials(n + T, 1, 3)
            unit_high(AHEAD + K_A, K_A, n)
            turned_to_high(n + T)
            unit_high(AHEAD + Z_B, Z_B, n)
            exponentials(n + 2 * T, 0, 0)
            exponentials(n + 2 * T, 0, 1)
            unit_high(AHEAD + V_0, V_0, n)
            exponentials(n + 2 * T, 0, 2)
            unit_high(AHEAD + V_1, V_1, n)
            exponentials(n + 2 * T, 0, 3)

        with act.Fori(0, batches) as b:
            with act.Fori(0, PAIRS - 1) as i:
                step(b, numbers(act, b, i), False)
            step(b, numbers(act, b, PAIRS - 1), True)

    @block.vector
    def _(dve):
        def split_x(b):
            dve.wait_ge(xt_high, b + 1)
            dve.tensor_tensor(xt[LO][:], xt_raw[:], xt[HI][:].bitcast(F32), ALU.subtract).then_inc(xt_split, 1)

        def unit_low(number, unit, before=0):
            bank, dst, scale = unit_target(number, unit)
            dve.wait_ge(proj_high, before + number + 1)
            high = dst[HI].bitcast(F32)
            if scale == 1.0:
                dve.tensor_tensor(dst[LO], bank, high, ALU.subtract).then_inc(proj_low, 1)
            else:
                dve.scalar_tensor_tensor(dst[LO], bank, scale, high, ALU.mult, ALU.subtract).then_inc(proj_low, 1)

        def clip(tile, t, first=False):
            dve.wait_ge(scores_ready, tile + t + 1)
            if not first:
                dve.wait_ge(turned_ready, tile + t - T + 1)
            dve.tensor_scalar(probs[:, AT[t]:AT[t] + WIDTH[t]], scores[t % 2][:, 0:WIDTH[t]], CLIP, -CLIP,
                              ALU.min, ALU.max).then_inc(scores_clipped, 1)

        def add_bias(tile, slot, t, biases):
            if t == 0:
                dve.wait_ge(bias_ready, biases)
            dve.wait_ge(scores_clipped, tile + t + 1)
            dve.sem_inc(dve_passed, 1)
            p = probs[:, AT[t]:AT[t] + WIDTH[t]]
            c = slot * T + t
            dve.tensor_tensor_reduce(p, p, bias[slot][:, S - WIDTH[t]:S], 1.0, BIG, ALU.add, ALU.min,
                                     low[:, c:c + 1]).then_inc(biased, 1)

        def invert(tile, slot, t):
            dve.wait_ge(exp_done, tile + t + 1)
            c = slot * T + t
            dve.reciprocal(inverse[:, c:c + 1], total[:, c:c + 1]).then_inc(inverse_done, 1)

        def turned_to_low(tile):
            for t in range(T):
                dve.wait_ge(turned_high, tile + t + 1)
                dst = [x[:, 0:t + 1, t * P:(t + 1) * P] for x in pt]
                dve.tensor_tensor(dst[LO], turned[t % 2][:, 0:WIDTH[t]].rearrange("p (c n) -> p c n", c=t + 1),
                                  dst[HI].bitcast(F32), ALU.subtract).then_inc(turned_low, 1)

        def softmax(tile, slot, biases, between, first=False):
            clip(tile, 0, first)
            clip(tile, 1, first)
            add_bias(tile, slot, 0, biases)
            clip(tile, 2, first)
            add_bias(tile, slot, 1, biases)
            clip(tile, 3, first)
            invert(tile, slot, 0)
            add_bias(tile, slot, 2, biases)
            invert(tile, slot, 1)
            between[0]()
            add_bias(tile, slot, 3, biases)
            invert(tile, slot, 2)
            between[1]()
            invert(tile, slot, 3)
            between[2]()

        def nothing():
            pass

        dve.engine_nop().then_inc(turned_low, FREE)
        split_x(0)
        for number, unit in enumerate((Q_A, K_A, V_0, V_1)):
            unit_low(number, unit)
        softmax(0, 0, HEAD_UNIT, (nothing, nothing, nothing), first=True)

        def step(b, n, last_pair):
            unit_low(AHEAD + Q_B, Q_B, n)
            unit_low(AHEAD + K_B, K_B, n)
            if last_pair:
                split_x(b + 1)
            turned_to_low(n)
            softmax(n + T, 1, n + 2 * HEAD_UNIT, (lambda: unit_low(AHEAD + Z_A, Z_A, n),
                                                  lambda: unit_low(AHEAD + Q_A, Q_A, n),
                                                  lambda: unit_low(AHEAD + K_A, K_A, n)))
            turned_to_low(n + T)
            unit_low(AHEAD + Z_B, Z_B, n)
            softmax(n + 2 * T, 0, n + 3 * HEAD_UNIT, (lambda: unit_low(AHEAD + V_0, V_0, n),
                                                      lambda: unit_low(AHEAD + V_1, V_1, n),
                                                      nothing))

        with dve.Fori(0, batches) as b:
            with dve.Fori(0, PAIRS - 1) as i:
                step(b, numbers(dve, b, i), False)
            step(b, numbers(dve, b, PAIRS - 1), True)
            dve.wait_ge(x_in, 16 * b + 16)
            dve.wait_ge(out_ready, b + 1)
            for half in range(2):
                part = y[:, 2 * half:2 * half + 2]
                last = dve.tensor_tensor(part, out[half][:], part, ALU.add)
            last.then_inc(y_ready, 1)


H1 = 16
E1 = D // H1
PAD = 32
BLOCKS = H1 * PAD // P
PER_BLOCK = H1 // BLOCKS
LN_EPS, RMS_EPS, NORM_EPS = 1e-5, 1e-5, 1e-7
MAX_NORM = 0.99
EXPERTS = 8
I_MOE, I_SHARED = 176, 704
ROWS = P // EXPERTS
E_CHUNKS = I_MOE // ROWS
S_CHUNKS = -(-I_SHARED // P)
CHUNKS = E_CHUNKS + S_CHUNKS
SHARED = [c % 3 == 2 or c == CHUNKS - 1 for c in range(CHUNKS)]
assert sum(SHARED) == S_CHUNKS
ROUTER = 10
GU = 2 * KC * P


def block_one(nc, y_scratch, weights, tables, result):
    with ExitStack() as stack:
        m = Space(nc, stack, "block_one_")
        resident = dict(
            gate_up=[m.sb(f"gate_up_{x}", [P, CHUNKS, 2, KC, P], F32R) for x in ("hi", "lo")],
            down=[m.sb(f"down_{x}", [P, CHUNKS, D], F32R) for x in ("hi", "lo")],
            qkv=[m.sb(f"qkv_{x}", [P, KC, 3 * D], F32R) for x in ("hi", "lo")],
            router=[m.sb(f"router_{x}", [P, KC, ROUTER], F32R) for x in ("hi", "lo")],
        )
        split_block_one(nc, weights, resident)
        block_one_layers(nc, m, y_scratch, weights, tables, resident, result)


def split_block_one(nc, weights, resident):
    SLOTS = 4
    pieces = []
    for c in range(CHUNKS):
        pieces.append((weights["gate_up"][c], *[x[:, c] for x in resident["gate_up"]]))
        pieces.append((weights["down"][c], *[x[:, c] for x in resident["down"]]))
    for c in range(KC):
        pieces.append((weights["qkv"][:, c], *[x[:, c] for x in resident["qkv"]]))
    pieces.append((weights["router"], *[x[:] for x in resident["router"]]))
    with ExitStack() as stack:
        m = Space(nc, stack, "block_one_split_")
        raw = [m.sb(f"raw_{i}", [P, 3 * D]) for i in range(SLOTS)]
        loaded = [m.sem(f"raw_loaded_{i}") for i in range(SLOTS)]
        high_done, low_done = m.sem("w_high_done"), m.sem("w_low_done")
        block = stack.enter_context(nc.Block())

        def flat(ap):
            names = "abcd"[:len(ap.shape) - 1]
            return ap if len(names) == 1 else ap.rearrange(f"p {' '.join(names)} -> p ({' '.join(names)})")

        @block.sync
        def _(sp):
            for n, (src, high, _) in enumerate(pieces):
                if n >= SLOTS:
                    sp.wait_ge(low_done, n - SLOTS + 1)
                src, size = flat(src), flat(high).shape[1]
                sp.dma_start(raw[n % SLOTS][:, 0:size], src).then_inc(loaded[n % SLOTS], 16)

        @block.scalar
        def _(act):
            for n, (_, high, _) in enumerate(pieces):
                high = flat(high)
                act.wait_ge(loaded[n % SLOTS], 16 * (n // SLOTS + 1))
                act.activation(high, raw[n % SLOTS][:, 0:high.shape[1]], ACT.Copy).then_inc(high_done, 1)

        @block.vector
        def _(dve):
            for n, (_, high, low) in enumerate(pieces):
                high, low = flat(high), flat(low)
                dve.wait_ge(high_done, n + 1)
                dve.tensor_tensor(low, raw[n % SLOTS][:, 0:high.shape[1]], high.bitcast(F32),
                                  ALU.subtract).then_inc(low_done, 1)


def block_one_layers(nc, m, y_scratch, weights, tables, resident, result):
    batches = result.shape[0]
    gate_up, down, qkv, router = (resident[x] for x in ("gate_up", "down", "qkv", "router"))
    ffn_w = m.sb("ffn_w", [P, KC, D])
    ffn_scale = m.sb("ffn_scale", [P, D])
    wo = m.sb("wo", [P, KC, D])
    rms_w = m.sb("rms_w", [P, KC])
    cos, sin = m.sb("cos", [P, T, E1]), m.sb("sin", [P, T, E1])
    decay = m.sb("decay", [P, PER_BLOCK, BLOCKS * P])
    q_decay, k_decay = m.sb("q_decay", [P, H1]), m.sb("k_decay", [P, H1])
    own_head = m.sb("own_head", [P, PER_BLOCK * E1])
    chunk_decay = m.sb("chunk_decay", [P, BLOCKS, PER_BLOCK * E1])
    spread = m.sb("spread", [P, 2, P])
    ident = m.sb("ident", [P, P])
    descending = m.sb("descending", [P, T, EXPERTS])
    power = m.sb("power", [P, 2, T])
    x1 = m.sb("x1", [P, T, D])
    x2 = m.sb("x2", [P, T, D])
    x3 = m.sb("x3", [P, T, D])
    masked = m.sb("masked_scores", [P, PER_BLOCK, BLOCKS * P])
    x1t = masked[:, 0:KC]
    x2_squares = masked[:, KC:].rearrange("p a (b d) -> p (a b) d", d=D)
    x2t = [m.sb(f"x2t_{x}", [P, KC, S], F32R) for x in ("hi", "lo")]
    x3t = [m.sb(f"x3t_{x}", [P, KC, S], F32R) for x in ("hi", "lo")]
    qk = m.sb("qk", [P, 2 * H1, E1])
    swapped = m.sb("swapped", [P, 2 * H1, E1])
    qk_pad = m.sb("qk_pad", [P, 2 * H1, PAD])
    kd_pad = m.sb("kd_pad", [P, H1, PAD])
    v = m.sb("v", [P, D])
    qt, kt = m.sb("qt", [P, BLOCKS * P]), m.sb("kt", [P, BLOCKS * P])
    state = m.sb("state", [P, BLOCKS, PER_BLOCK * E1])
    faded = m.sb("faded", [P, BLOCKS, PER_BLOCK * E1])
    update = m.sb("update", [P, BLOCKS, PER_BLOCK * E1])
    attn = m.sb("attn", [P, D])
    attn_t = m.sb("attn_t", [P, KC, P])
    junk = m.sb("junk", [P, D])
    stats, moments = m.sb("stats", [P, T, 6]), m.sb("moments", [P, T, 2])
    variance, inverse = m.sb("variance", [P, T]), m.sb("inverse", [P, T])
    squares = m.sb("squares", [P, T])
    norm = m.sb("norm", [P, 8, T])
    attn_squares, attn_inverse = m.sb("attn_squares", [P, T]), m.sb("attn_inverse", [P, T])
    logits = m.sb("logits", [P, T, ROUTER])
    pick = m.sb("pick", [P, 5, T, EXPERTS])
    best = m.sb("best", [P, 8, T])
    mix = m.sb("mix", [P, T, EXPERTS + 1])
    mix_t = m.sb("mix_t", [EXPERTS + 1, S])
    share = [m.sb(f"share_{x}", [P, S]) for x in ("experts", "shared")]
    SLOTS = 2
    hidden = [m.sb(f"hidden_{i}", [P, S]) for i in range(SLOTS)]
    hidden_split = [[m.sb(f"hidden_{x}_{i}", [P, S], F32R) for x in ("hi", "lo")] for i in range(SLOTS)]
    BANKS = 4
    bank = [m.ps(f"bank_{i}", [P, 512]) for i in range(BANKS)]
    gate_bank, up_bank = m.ps("gate_bank", [P, S]), m.ps("up_bank", [P, S])
    out = [m.ps(f"out_{i}", [P, 2, D]) for i in range(2)]

    loaded, consts = m.sem("loaded"), m.sem("consts")
    bank_ready = [m.sem(f"bank_{i}_ready") for i in range(BANKS)]
    bank_taken = [m.sem(f"bank_{i}_taken") for i in range(BANKS)]
    gate_ready, gate_taken = m.sem("gate_ready"), m.sem("gate_taken")
    up_ready, up_taken = m.sem("up_ready"), m.sem("up_taken")
    y_in, result_out = m.sem("y_in"), m.sem("result_out")
    stats_done, inverse_done = m.sem("stats_done"), m.sem("inverse_done")
    x1_done, x2_done, x3_done = m.sem("x1_done"), m.sem("x2_done"), m.sem("x3_done")
    turned_x1 = m.sem("turned_x1")
    x2t_high, x2t_split, x3t_high, x3t_split = (m.sem(x) for x in ("x2t_high", "x2t_split", "x3t_high", "x3t_split"))
    scaled, squares_done, norms_done, norm_floored, tanh_done = (
        m.sem(x) for x in ("scaled", "squares_done", "norms_done", "norm_floored", "tanh_done"))
    qk_copied, v_copied, swapped_done, rotated, kd_done = (
        m.sem(x) for x in ("qk_copied", "v_copied", "swapped_done", "rotated", "kd_done"))
    qt_done, kt_done, masked_done = m.sem("qt_done"), m.sem("kt_done"), m.sem("masked_done")
    state_ready, state_faded, update_done = m.sem("state_ready"), m.sem("state_faded"), m.sem("update_done")
    attn_done, attn_squared, attn_inverse_done, attn_t_done = (
        m.sem(x) for x in ("attn_done", "attn_squared", "attn_inverse_done", "attn_t_done"))
    gap_done, exp_done, mix_done, mix_t_done, share_done = (
        m.sem(x) for x in ("gap_done", "exp_done", "mix_done", "mix_t_done", "share_done"))
    tanh_gate, product_done, weighted, hidden_high, hidden_low = (
        m.sem(x) for x in ("tanh_gate", "product_done", "weighted", "hidden_high", "hidden_low"))
    down_done, moe_done, result_ready = m.sem("down_done"), m.sem("moe_done"), m.sem("result_ready")
    front_chain, back_chain, pool_chain = m.sem("front_chain"), m.sem("back_chain"), m.sem("pool_chain")
    final_stats, final_inverse = m.sem("final_stats"), m.sem("final_inverse")
    dve_passed, pool_passed = m.sem("dve_passed"), m.sem("pool_passed")

    X1T, FFN, X2T = 0, 2, 4
    TILE = 6
    QK_, V_, QT, KT, SCORES, MIXED, UPDATE, ATTN_T, OUT = 0, 1, 2, 3, 4, 8, 9, 10, 11
    PER_TILE = 12
    X3T = TILE + T * PER_TILE
    LOGITS, MIX_T, SHARE = X3T + 2, X3T + 3, X3T + 4
    USES = SHARE + 2
    PER_BANK = USES // BANKS
    assert USES % BANKS == 0

    def at(t, use):
        return TILE + t * PER_TILE + use

    def bank_of(use):
        return bank[use % BANKS]

    def wait_bank(eng, b, use):
        eng.wait_ge(bank_ready[use % BANKS], b * PER_BANK + (use // BANKS + 1))

    def wait_free(eng, b, use):
        eng.wait_ge(bank_taken[use % BANKS], b * PER_BANK + (use // BANKS + 1))

    def run(front, back):
        for part in (front, back):
            for _ in part or ():
                pass

    loads = [(ffn_w, weights["ffn_w"]), (ffn_scale, weights["ffn_scale"]), (wo, weights["wo"]),
             (rms_w, weights["rms_w"])] + \
            [(t, tables[x]) for x, t in dict(
                cos=cos, sin=sin, decay=decay, q_decay=q_decay, k_decay=k_decay, own_head=own_head,
                chunk_decay=chunk_decay, spread=spread, ident=ident, descending=descending,
                power=power).items()]
    LOADED = 16 * len(loads)

    block = m.stack.enter_context(nc.Block())

    @block.sync
    def _(sp):
        def tokens(dram):
            return dram.rearrange("(t p) d -> p t d", p=P)

        sp.dma_start(x1[:], tokens(y_scratch[0])).then_inc(y_in, 16)
        for dst, src in loads:
            sp.dma_start(dst[:], src).then_inc(loaded, 16)

        def store(b):
            sp.wait_ge(result_ready, b + 1)
            sp.dma_start(tokens(result[b]), x3[:]).then_inc(result_out, 16)

        with sp.Fori(0, batches - 1) as b:
            sp.wait_ge(x3_done, b + 1)
            sp.dma_start(x1[:], tokens(y_scratch[b + 1])).then_inc(y_in, 16)
            store(b)
        store(batches - 1)
        sp.wait_ge(result_out, 16 * batches + 1)


    @block.gpsimd
    def _(pool):
        pool.wait_ge(loaded, LOADED)
        pool.memset(qk_pad[:], 0.0).then_inc(consts, 1)
        pool.memset(kd_pad[:], 0.0).then_inc(consts, 1)
        pool.memset(state[:], 0.0).then_inc(state_ready, 1)

        def root(dst, src, which):
            return pool.tensor_tensor(dst, src, power[:, which, 0:dst.shape[1]], ALU.pow)

        def layer_inverse(stats_sem, count, chain_value, signal):
            pool.wait_ge(stats_sem, count)
            pool.sem_inc(pool_passed, 1)
            pool.tensor_scalar(variance[:], moments[:, :, 1], LN_EPS, 1.0, ALU.add, ALU.mult)\
                .then_inc(pool_chain, 1)
            pool.wait_ge(pool_chain, chain_value)
            root(inverse[:], variance[:], 0).then_inc(signal, 1)

        CHAIN = 3 + T + 1

        def front(b):
            layer_inverse(stats_done, 3 * b + 1, CHAIN * b + 1, inverse_done)
            pool.wait_ge(squares_done, b + 1)
            root(norm[:, 0], squares[:], 1).then_inc(norms_done, 1)
            layer_inverse(stats_done, 3 * b + 2, CHAIN * b + 2, inverse_done)
            yield
            for t in range(T):
                half = E1 // 2
                pool.wait_ge(qk_copied, T * b + t + 1)
                s = sin[:, t, None, :].broadcast_to([P, 2 * H1, E1])
                pool.tensor_tensor(swapped[:, :, 0:half], qk[:, :, half:E1], s[:, :, 0:half], ALU.mult)
                pool.tensor_tensor(swapped[:, :, half:E1], qk[:, :, 0:half], s[:, :, half:E1], ALU.mult)\
                    .then_inc(swapped_done, 1)
                pool.wait_ge(rotated, T * b + t + 1)
                pool.tensor_tensor(kd_pad[:, :, 0:E1], qk_pad[:, H1:, 0:E1],
                                   k_decay[:, :, None].broadcast_to([P, H1, E1]), ALU.mult).then_inc(kd_done, 1)
                wait_bank(pool, b, at(t, MIXED))
                pool.tensor_tensor(faded[:], state[:], chunk_decay[:], ALU.mult).then_inc(state_faded, 1)
                pool.wait_ge(state_faded, T * b + t + 1)
                pool.wait_ge(update_done, T * b + t + 1)
                if t < T - 1:
                    pool.tensor_tensor(state[:], faded[:], update[:], ALU.add).then_inc(state_ready, 1)
                else:
                    pool.sem_inc(pool_passed, 1)
                    pool.memset(state[:], 0.0).then_inc(state_ready, 1)
                pool.wait_ge(attn_squared, T * b + t + 1)
                pool.sem_inc(pool_passed, 1)
                pool.tensor_scalar(variance[:, 0:1], attn_squares[:, t:t + 1], 1.0 / D, RMS_EPS,
                                   ALU.mult, ALU.add).then_inc(pool_chain, 1)
                pool.wait_ge(pool_chain, CHAIN * b + 3 + t)
                root(attn_inverse[:, t:t + 1], variance[:, 0:1], 0).then_inc(attn_inverse_done, 1)
                yield
            layer_inverse(stats_done, 3 * b + 3, CHAIN * b + 3 + T, inverse_done)
            yield

        def back(b):
            pool.wait_ge(share_done, 2 * b + 2)
            for c in range(CHUNKS):
                pool.wait_ge(product_done, CHUNKS * b + c + 1)
                h = hidden[c % SLOTS][:]
                pool.tensor_tensor(h, h, share[SHARED[c]][:], ALU.mult).then_inc(weighted, 1)
                yield
            layer_inverse(final_stats, b + 1, CHAIN * b + CHAIN, final_inverse)

        with pool.Fori(0, batches) as b:
            run(front(b), back(b))

    @block.tensor
    def _(pe):
        def transposes(b, use, src, col):
            wait_free(pe, b, use)
            for t in range(T):
                last = pe.transpose(bank_of(use)[:, t * P:(t + 1) * P], src[:, t, col:col + P], ident[:])
            last.then_inc(bank_ready[use % BANKS], 1)

        def front(b):
            pe.wait_ge(x1_done, b + 1)
            for c in range(KC):
                transposes(b, X1T + c, x1, c * P)
            pe.wait_ge(turned_x1, 2 * b + 2)
            for half in range(2):
                wait_free(pe, b, FFN + half)
                for t in range(2):
                    row = (2 * half + t) * P
                    for c in range(KC):
                        last = pe.matmul(bank_of(FFN + half)[:, t * D:(t + 1) * D], x1t[:, c, row:row + P],
                                         ffn_w[:, c], start=(c == 0), stop=(c == KC - 1))
                last.then_inc(bank_ready[(FFN + half) % BANKS], 1)
            pe.wait_ge(x2_done, b + 1)
            for c in range(KC):
                transposes(b, X2T + c, x2, c * P)
            pe.wait_ge(x2t_split, 2 * b + 2)
            yield
            for t in range(T):
                row = t * P
                for use, lo, hi in ((QK_, 0, 2 * D), (V_, 2 * D, 3 * D)):
                    wait_free(pe, b, at(t, use))
                    for n, (p, c) in enumerate((p, c) for c in range(KC) for p in PASSES):
                        last = pe.matmul(bank_of(at(t, use))[:, 0:hi - lo], x2t[p[0]][:, c, row:row + P],
                                         qkv[p[1]][:, c, lo:hi], start=(n == 0), stop=(n == 3 * KC - 1))
                    last.then_inc(bank_ready[at(t, use) % BANKS], 1)
                pe.wait_ge(rotated, T * b + t + 1)
                for use, first in ((QT, 0), (KT, H1)):
                    wait_free(pe, b, at(t, use))
                    for g in range(BLOCKS):
                        heads = qk_pad[:, first + g * PER_BLOCK:first + (g + 1) * PER_BLOCK]
                        last = pe.transpose(bank_of(at(t, use))[:, g * P:(g + 1) * P],
                                            heads.rearrange("p a b -> p (a b)"), ident[:])
                    last.then_inc(bank_ready[at(t, use) % BANKS], 1)
                pe.wait_ge(qt_done, T * b + t + 1)
                pe.wait_ge(kt_done, T * b + t + 1)
                for j in range(PER_BLOCK):
                    wait_free(pe, b, at(t, SCORES + j))
                for g in range(BLOCKS):
                    for j in range(PER_BLOCK):
                        rows = slice(j * PAD, j * PAD + E1)
                        last = pe.matmul(bank_of(at(t, SCORES + j))[:, g * P:(g + 1) * P],
                                         kt[rows, g * P:(g + 1) * P], qt[rows, g * P:(g + 1) * P],
                                         start=True, stop=True)
                        if g == BLOCKS - 1:
                            last.then_inc(bank_ready[at(t, SCORES + j) % BANKS], 1)
                pe.wait_ge(v_copied, T * b + t + 1)
                pe.wait_ge(state_ready, T * b + t + 1)
                wait_free(pe, b, at(t, MIXED))
                for j in range(PER_BLOCK):
                    pe.wait_ge(masked_done, (T * b + t) * PER_BLOCK + j + 1)
                    for g in range(BLOCKS):
                        head = g * PER_BLOCK + j
                        pe.matmul(bank_of(at(t, MIXED))[:, head * E1:(head + 1) * E1],
                                  masked[:, j, g * P:(g + 1) * P], v[:, head * E1:(head + 1) * E1],
                                  start=True, stop=True)
                W = PER_BLOCK * E1
                for g in range(BLOCKS):
                    last = pe.matmul(bank_of(at(t, MIXED))[:, D + g * W:D + (g + 1) * W],
                                     qt[:, g * P:(g + 1) * P], state[:, g], start=True, stop=True)
                last.then_inc(bank_ready[at(t, MIXED) % BANKS], 1)
                pe.wait_ge(kd_done, T * b + t + 1)
                wait_free(pe, b, at(t, UPDATE))
                for g in range(BLOCKS):
                    keys = kd_pad[:, g * PER_BLOCK:(g + 1) * PER_BLOCK].rearrange("p a b -> p (a b)")
                    last = pe.matmul(bank_of(at(t, UPDATE))[:, g * W:(g + 1) * W], keys,
                                     v[:, g * W:(g + 1) * W], start=True, stop=True)
                last.then_inc(bank_ready[at(t, UPDATE) % BANKS], 1)
                pe.wait_ge(attn_done, T * b + t + 1)
                wait_free(pe, b, at(t, ATTN_T))
                for c in range(KC):
                    last = pe.transpose(bank_of(at(t, ATTN_T))[:, c * P:(c + 1) * P],
                                        attn[:, c * P:(c + 1) * P], ident[:])
                last.then_inc(bank_ready[at(t, ATTN_T) % BANKS], 1)
                pe.wait_ge(attn_t_done, T * b + t + 1)
                wait_free(pe, b, at(t, OUT))
                for c in range(KC):
                    last = pe.matmul(bank_of(at(t, OUT))[:, 0:D], attn_t[:, c], wo[:, c],
                                     start=(c == 0), stop=(c == KC - 1))
                last.then_inc(bank_ready[at(t, OUT) % BANKS], 1)
                yield
            pe.wait_ge(x3_done, b + 1)
            for c in range(KC):
                transposes(b, X3T + c, x3, c * P)
            pe.wait_ge(x3t_split, 2 * b + 2)
            wait_free(pe, b, LOGITS)
            for t in range(T):
                for n, (p, c) in enumerate((p, c) for c in range(KC) for p in PASSES):
                    last = pe.matmul(bank_of(LOGITS)[:, t * ROUTER:(t + 1) * ROUTER],
                                     x3t[p[0]][:, c, t * P:(t + 1) * P], router[p[1]][:, c],
                                     start=(n == 0), stop=(n == 3 * KC - 1))
            last.then_inc(bank_ready[LOGITS % BANKS], 1)
            pe.wait_ge(mix_done, b + 1)
            wait_free(pe, b, MIX_T)
            for t in range(T):
                last = pe.matmul(bank_of(MIX_T)[0:EXPERTS + 1, t * P:(t + 1) * P], mix[:, t], ident[:],
                                 start=True, stop=True)
            last.then_inc(bank_ready[MIX_T % BANKS], 1)
            pe.wait_ge(mix_t_done, b + 1)
            for which in range(2):
                wait_free(pe, b, SHARE + which)
                pe.matmul(bank_of(SHARE + which)[:], spread[0:EXPERTS + 1, which], mix_t[:],
                          start=True, stop=True).then_inc(bank_ready[(SHARE + which) % BANKS], 1)
            yield

        def back(b):
            def expand(c):
                for which, (target, taken, ready) in enumerate(((gate_bank, gate_taken, gate_ready),
                                                                (up_bank, up_taken, up_ready))):
                    pe.wait_ge(taken, CHUNKS * b + c + 1)
                    for n, (p, k) in enumerate((p, k) for k in range(KC) for p in PASSES):
                        last = pe.matmul(target[:], gate_up[p[0]][:, c, which, k], x3t[p[1]][:, k],
                                         start=(n == 0), stop=(n == 3 * KC - 1))
                    last.then_inc(ready, 1)

            def contract(c):
                pe.wait_ge(hidden_low, CHUNKS * b + c + 1)
                for t in range(T):
                    for n, p in enumerate(PASSES):
                        last = pe.matmul(out[t // 2][:, t % 2], hidden_split[c % SLOTS][p[0]][:, t * P:(t + 1) * P],
                                         down[p[1]][:, c], start=(c == 0 and n == 0 and t % 2 == 0),
                                         stop=(c == CHUNKS - 1 and n == 2), skip_group_check=True)
                last.then_inc(down_done, 1)

            for c in range(CHUNKS):
                expand(c)
                if c == 0:
                    pe.wait_ge(moe_done, b + 1)
                else:
                    contract(c - 1)
                yield
            contract(CHUNKS - 1)

        pe.wait_ge(loaded, LOADED)
        pe.wait_ge(consts, 3)
        with pe.Fori(0, batches) as b:
            run(front(b), back(b))

    @block.scalar
    def _(act):
        def front(b):
            wait_bank(act, b, X1T)
            act.activation(x1t[:, 0], bank_of(X1T)[:], ACT.Copy).then_inc(bank_taken[X1T % BANKS], 1)
            act.wait_ge(scaled, b + 1)
            for t in range(T):
                last = act.activation(x2_squares[:, t], x2[:, t], ACT.Square, accum_out=squares[:, t:t + 1])
            last.then_inc(squares_done, 1)
            act.wait_ge(norm_floored, b + 1)
            act.activation(norm[:, 2], norm[:, 1], ACT.Tanh).then_inc(tanh_done, 1)
            for c in range(KC):
                wait_bank(act, b, X2T + c)
                act.activation(x2t[HI][:, c], bank_of(X2T + c)[:], ACT.Copy).then_inc(x2t_high, 1)
            yield
            for t in range(T):
                wait_bank(act, b, at(t, QK_))
                act.activation(qk[:].rearrange("p a b -> p (a b)"), bank_of(at(t, QK_))[:], ACT.Copy)\
                    .then_inc(qk_copied, 1)
                wait_bank(act, b, at(t, V_))
                act.activation(v[:], bank_of(at(t, V_))[:, 0:D], ACT.Copy).then_inc(v_copied, 1)
                wait_bank(act, b, at(t, QT))
                act.activation(qt[:], bank_of(at(t, QT))[:], ACT.Copy).then_inc(qt_done, 1)
                act.wait_ge(attn_done, T * b + t + 1)
                act.activation(junk[:], attn[:], ACT.Square, accum_out=attn_squares[:, t:t + 1])\
                    .then_inc(attn_squared, 1)
                wait_bank(act, b, at(t, ATTN_T))
                act.activation(attn_t[:].rearrange("p a b -> p (a b)"), bank_of(at(t, ATTN_T))[:, 0:D], ACT.Copy)\
                    .then_inc(attn_t_done, 1)
                yield
            for c in range(KC):
                wait_bank(act, b, X3T + c)
                act.activation(x3t[HI][:, c], bank_of(X3T + c)[:], ACT.Copy).then_inc(x3t_high, 1)
            act.wait_ge(gap_done, b + 1)
            act.activation(best[:, 4], best[:, 3], ACT.Exp)
            act.activation(best[:, 5], logits[:, :, EXPERTS], ACT.Exp, scale=-1.0).then_inc(exp_done, 1)
            wait_bank(act, b, SHARE)
            act.activation(share[0][:], bank_of(SHARE)[:], ACT.Copy).then_inc(share_done, 1)
            yield

        def back(b):
            def high(c):
                act.wait_ge(weighted, CHUNKS * b + c + 1)
                act.activation(hidden_split[c % SLOTS][HI][:], hidden[c % SLOTS][:], ACT.Copy)\
                    .then_inc(hidden_high, 1)

            for c in range(CHUNKS):
                act.wait_ge(gate_ready, CHUNKS * b + c + 1)
                act.activation(hidden[c % SLOTS][:], gate_bank[:], ACT.Tanh, scale=0.5).then_inc(tanh_gate, 1)
                if c:
                    high(c - 1)
                yield
            high(CHUNKS - 1)

        act.wait_ge(loaded, LOADED)
        with act.Fori(0, batches) as b:
            run(front(b), back(b))

    @block.vector
    def _(dve):
        dve.wait_ge(loaded, LOADED)
        for c in range(KC):
            last = dve.tensor_scalar(wo[:, c], wo[:, c], rms_w[:, c:c + 1], None, ALU.mult)
        last.then_inc(consts, 1)
        for s in bank_taken + [gate_taken, up_taken, moe_done, result_out]:
            dve.sem_inc(s, 1)
        FRONT_LINKS, BACK_LINKS = 52, 19

        class Chain:

            def __init__(self, sem, base, links):
                self.sem, self.base, self.n, self.links = sem, base, 0, links

            def link(self, instruction):
                instruction.then_inc(self.sem, 1)
                self.n += 1
                dve.wait_ge(self.sem, self.base + self.n)

            def close(self):
                assert self.n == self.links, self.n

        def statistics(chain, src, signal):
            for t in range(T):
                last = dve.bn_stats(stats[:, t], src[:, t])
            chain.link(last)
            dve.sem_inc(dve_passed, 1)
            for t in range(T):
                last = dve.bn_aggr(moments[:, t], stats[:, t])
            last.then_inc(signal, 1)

        def normalise(src, dst, signal):
            for t in range(T):
                last = dve.tensor_scalar(dst[:, t], src[:, t], moments[:, t, 0:1], inverse[:, t:t + 1],
                                         ALU.subtract, ALU.mult)
            last.then_inc(signal, 1)

        def front(b):
            chain = Chain(front_chain, b * FRONT_LINKS, FRONT_LINKS)
            link = chain.link
            dve.wait_ge(y_in, 16 * b + 16)
            statistics(chain, x1, stats_done)
            dve.wait_ge(inverse_done, 3 * b + 1)
            normalise(x1, x1, x1_done)
            wait_bank(dve, b, X1T + 1)
            last = dve.tensor_copy(x1t[:, 1], bank_of(X1T + 1)[:])
            last.then_inc(turned_x1, 1)
            dve.wait_ge(bank_taken[X1T % BANKS], b * PER_BANK + 2)
            dve.sem_inc(turned_x1, 1)
            dve.wait_ge(turned_x1, 2 * b + 1)
            dve.sem_inc(bank_taken[(X1T + 1) % BANKS], 1)
            for half in range(2):
                wait_bank(dve, b, FFN + half)
                last = dve.tensor_tensor(x2[:, 2 * half:2 * half + 2],
                                         bank_of(FFN + half)[:].rearrange("p (t n) -> p t n", t=2),
                                         ffn_scale[:, None, :].broadcast_to([P, 2, D]), ALU.mult)
                link(last)
                dve.sem_inc(bank_taken[(FFN + half) % BANKS], 1)
            dve.sem_inc(scaled, 1)
            dve.wait_ge(norms_done, b + 1)
            root, floored, tanh, shrink = norm[:, 0], norm[:, 1], norm[:, 2], norm[:, 3]
            tmp, tmp2, factor = norm[:, 4], norm[:, 5], norm[:, 6]
            dve.tensor_scalar(floored, root, NORM_EPS, None, ALU.max).then_inc(norm_floored, 1)
            dve.wait_ge(norm_floored, b + 1)
            link(dve.tensor_scalar(tmp, floored, NORM_EPS, None, ALU.add))
            link(dve.reciprocal(tmp2, tmp))
            dve.wait_ge(tanh_done, b + 1)
            link(dve.tensor_tensor(shrink, tanh, tmp2, ALU.mult))
            link(dve.tensor_tensor(tmp, shrink, root, ALU.mult))
            link(dve.tensor_scalar(tmp2, tmp, NORM_EPS, None, ALU.max))
            link(dve.reciprocal(tmp, tmp2))
            link(dve.tensor_scalar(tmp2, tmp, MAX_NORM, 1.0, ALU.mult, ALU.min))
            link(dve.tensor_tensor(factor, shrink, tmp2, ALU.mult))
            for t in range(T):
                last = dve.scalar_tensor_tensor(x2[:, t], x2[:, t], factor[:, t:t + 1], x1[:, t],
                                                ALU.mult, ALU.add)
            link(last)
            statistics(chain, x2, stats_done)
            dve.wait_ge(inverse_done, 3 * b + 2)
            normalise(x2, x2, x2_done)
            for c in range(KC):
                dve.wait_ge(x2t_high, KC * b + c + 1)
                link(dve.tensor_tensor(x2t[LO][:, c], bank_of(X2T + c)[:], x2t[HI][:, c].bitcast(F32), ALU.subtract))
                dve.sem_inc(bank_taken[(X2T + c) % BANKS], 1)
                dve.sem_inc(x2t_split, 1)
            yield
            for t in range(T):
                dve.wait_ge(qk_copied, T * b + t + 1)
                dve.sem_inc(bank_taken[at(t, QK_) % BANKS], 1)
                c = cos[:, t, None, :].broadcast_to([P, 2 * H1, E1])
                link(dve.tensor_tensor(qk_pad[:, :, 0:E1], qk[:], c, ALU.mult))
                dve.wait_ge(swapped_done, T * b + t + 1)
                dve.tensor_tensor(qk_pad[:, :, 0:E1], qk_pad[:, :, 0:E1], swapped[:], ALU.add)\
                    .then_inc(rotated, 1)
                dve.wait_ge(v_copied, T * b + t + 1)
                dve.sem_inc(bank_taken[at(t, V_) % BANKS], 1)
                wait_bank(dve, b, at(t, KT))
                dve.tensor_copy(kt[:], bank_of(at(t, KT))[:]).then_inc(kt_done, 1)
                dve.wait_ge(kt_done, T * b + t + 1)
                dve.sem_inc(bank_taken[at(t, KT) % BANKS], 1)
                dve.wait_ge(qt_done, T * b + t + 1)
                dve.sem_inc(bank_taken[at(t, QT) % BANKS], 1)
                for j in range(PER_BLOCK):
                    wait_bank(dve, b, at(t, SCORES + j))
                    dve.tensor_tensor(masked[:, j], bank_of(at(t, SCORES + j))[:], decay[:, j], ALU.mult)\
                        .then_inc(masked_done, 1)
                    dve.wait_ge(masked_done, (T * b + t) * PER_BLOCK + j + 1)
                    dve.sem_inc(bank_taken[at(t, SCORES + j) % BANKS], 1)
                wait_bank(dve, b, at(t, MIXED))
                mixed = bank_of(at(t, MIXED))
                link(dve.tensor_tensor(attn[:].rearrange("p (h e) -> p h e", h=H1),
                                       mixed[:, D:2 * D].rearrange("p (h e) -> p h e", h=H1),
                                       q_decay[:, :, None].broadcast_to([P, H1, E1]), ALU.mult))
                dve.tensor_tensor(attn[:], mixed[:, 0:D], attn[:], ALU.add).then_inc(attn_done, 1)
                dve.wait_ge(attn_done, T * b + t + 1)
                dve.sem_inc(bank_taken[at(t, MIXED) % BANKS], 1)
                wait_bank(dve, b, at(t, UPDATE))
                dve.tensor_tensor(update[:], bank_of(at(t, UPDATE))[:, 0:D].rearrange("p (a b) -> p a b", a=BLOCKS),
                                  own_head[:, None, :].broadcast_to(list(update.shape)), ALU.mult)\
                    .then_inc(update_done, 1)
                dve.wait_ge(update_done, T * b + t + 1)
                dve.sem_inc(bank_taken[at(t, UPDATE) % BANKS], 1)
                dve.wait_ge(attn_t_done, T * b + t + 1)
                dve.sem_inc(bank_taken[at(t, ATTN_T) % BANKS], 1)
                wait_bank(dve, b, at(t, OUT))
                dve.wait_ge(attn_inverse_done, T * b + t + 1)
                link(dve.scalar_tensor_tensor(x1[:, t], bank_of(at(t, OUT))[:, 0:D], attn_inverse[:, t:t + 1],
                                              x2[:, t], ALU.mult, ALU.add))
                dve.sem_inc(bank_taken[at(t, OUT) % BANKS], 1)
                yield
            statistics(chain, x1, stats_done)
            dve.wait_ge(inverse_done, 3 * b + 3)
            dve.wait_ge(result_out, 16 * b + 1)
            normalise(x1, x3, x3_done)
            for c in range(KC):
                dve.wait_ge(x3t_high, KC * b + c + 1)
                link(dve.tensor_tensor(x3t[LO][:, c], bank_of(X3T + c)[:], x3t[HI][:, c].bitcast(F32), ALU.subtract))
                dve.sem_inc(bank_taken[(X3T + c) % BANKS], 1)
                dve.sem_inc(x3t_split, 1)
            wait_bank(dve, b, LOGITS)
            link(dve.tensor_copy(logits[:].rearrange("p t n -> p (t n)"), bank_of(LOGITS)[:, 0:T * ROUTER]))
            dve.sem_inc(bank_taken[LOGITS % BANKS], 1)
            level = logits[:, :, 0:EXPERTS]
            equal, rank, chosen1, rest, chosen2 = (pick[:, i] for i in range(5))
            m1, m2, first, gap, ratio, gate_exp, w1, w2 = (best[:, i] for i in range(8))

            def wide(x):
                return x[:, :, None].broadcast_to([P, T, EXPERTS])

            for source, top, chosen in ((level, m1, chosen1), (rest, m2, chosen2)):
                link(dve.tensor_reduce(top, source, AX.X, ALU.max))
                link(dve.tensor_tensor(equal, source, wide(top), ALU.is_equal))
                link(dve.tensor_tensor(rank, equal, descending[:], ALU.mult))
                link(dve.tensor_reduce(first, rank, AX.X, ALU.max))
                link(dve.tensor_tensor(chosen, descending[:], wide(first), ALU.is_equal))
                if chosen is chosen1:
                    link(dve.tensor_scalar(equal, chosen, -MASKED, None, ALU.mult))
                    link(dve.tensor_tensor(rest, equal, level, ALU.add))
            dve.tensor_tensor(gap, m2, m1, ALU.subtract).then_inc(gap_done, 1)
            dve.wait_ge(exp_done, b + 1)
            link(dve.tensor_scalar(first, ratio, 1.0, None, ALU.add))
            link(dve.reciprocal(w1, first))
            link(dve.tensor_scalar(w1, w1, 0.5, None, ALU.mult))
            link(dve.tensor_tensor(w2, w1, ratio, ALU.mult))
            link(dve.tensor_tensor(equal, chosen1, wide(w1), ALU.mult))
            link(dve.tensor_tensor(rank, chosen2, wide(w2), ALU.mult))
            link(dve.tensor_scalar(first, gate_exp, 1.0, None, ALU.add))
            link(dve.reciprocal(gap, first))
            dve.tensor_scalar(mix[:, :, EXPERTS], gap, 0.5, None, ALU.mult)
            dve.tensor_tensor(mix[:, :, 0:EXPERTS], equal, rank, ALU.add).then_inc(mix_done, 1)
            wait_bank(dve, b, MIX_T)
            dve.tensor_copy(mix_t[:], bank_of(MIX_T)[0:EXPERTS + 1, :]).then_inc(mix_t_done, 1)
            dve.wait_ge(mix_t_done, b + 1)
            dve.sem_inc(bank_taken[MIX_T % BANKS], 1)
            wait_bank(dve, b, SHARE + 1)
            link(dve.tensor_copy(share[1][:], bank_of(SHARE + 1)[:]))
            dve.sem_inc(bank_taken[(SHARE + 1) % BANKS], 1)
            dve.wait_ge(share_done, 2 * b + 1)
            dve.sem_inc(bank_taken[SHARE % BANKS], 1)
            dve.sem_inc(share_done, 1)
            chain.close()
            yield

        def back(b):
            chain = Chain(back_chain, b * BACK_LINKS, BACK_LINKS)
            link = chain.link

            def low(c):
                dve.wait_ge(hidden_high, CHUNKS * b + c + 1)
                dve.tensor_tensor(hidden_split[c % SLOTS][LO][:], hidden[c % SLOTS][:],
                                  hidden_split[c % SLOTS][HI][:].bitcast(F32), ALU.subtract).then_inc(hidden_low, 1)

            for c in range(CHUNKS):
                h = hidden[c % SLOTS][:]
                dve.wait_ge(tanh_gate, CHUNKS * b + c + 1)
                dve.scalar_tensor_tensor(h, h, 1.0, gate_bank[:], ALU.add, ALU.mult).then_inc(gate_taken, 1)
                if c:
                    low(c - 1)
                dve.wait_ge(gate_taken, CHUNKS * b + c + 2)
                dve.wait_ge(up_ready, CHUNKS * b + c + 1)
                link(dve.tensor_tensor(h, up_bank[:], h, ALU.mult))
                dve.sem_inc(up_taken, 1)
                dve.sem_inc(product_done, 1)
                yield
            low(CHUNKS - 1)
            dve.wait_ge(down_done, CHUNKS * b + CHUNKS)
            for half in range(2):
                part = x3[:, 2 * half:2 * half + 2]
                last = dve.tensor_tensor(part, out[half][:], part, ALU.add)
            link(last)
            dve.sem_inc(moe_done, 1)
            statistics(chain, x3, final_stats)
            dve.wait_ge(final_inverse, b + 1)
            normalise(x3, x3, result_ready)
            chain.close()

        with dve.Fori(0, batches) as b:
            run(front(b), back(b))


def two_block_kernel(nc, x_tokens, x_t, w_heads, slopes, *rest):
    result = rest[-1]
    weights = dict(zip(WEIGHTS, rest))
    tables = dict(zip(TABLES, rest[len(WEIGHTS):]))
    batches = result.shape[0]
    y_scratch = nc.dram_tensor("y_scratch", (batches, S, D), F32, kind="Internal").ap()
    softmax_attention(nc, x_tokens, x_t, w_heads, slopes, y_scratch)
    block_one(nc, y_scratch, weights, tables, result)


WEIGHTS = ("gate_up", "down", "qkv", "router", "ffn_w", "ffn_scale", "wo", "rms_w")
TABLES = ("cos", "sin", "decay", "q_decay", "k_decay", "own_head", "chunk_decay", "spread", "ident",
          "descending", "power")


def alibi_slopes(heads):
    return [2.0 ** (-8.0 * (h + 1) / heads) for h in range(heads)]


def shape_tables():
    f32 = np.float32
    slopes = np.array(alibi_slopes(H1), f32)
    r = np.exp(-slopes)
    freq = (f32(1.0 / 1024.0) ** np.linspace(0.0, 1.0, E1 // 4, dtype=f32)).astype(f32)
    freq = np.concatenate([freq, np.zeros(E1 // 4, f32)])
    theta = np.arange(S, dtype=f32)[:, None] * freq[None, :]
    cos = np.concatenate([np.cos(theta)] * 2, axis=1)
    sin = np.concatenate([np.sin(theta), -np.sin(theta)], axis=1)

    def tiles(a):
        return a.reshape(T, P, -1).transpose(1, 0, 2)

    i = np.arange(P, dtype=f32)
    diff = i[None, :] - i[:, None]
    by_head = np.where(diff >= 0, r[:, None, None] ** np.maximum(diff, 0), 0)
    decay = by_head.reshape(BLOCKS, PER_BLOCK, P, P).transpose(2, 1, 0, 3).reshape(P, PER_BLOCK, BLOCKS * P)
    row_head, column_head = np.arange(P) // PAD, np.arange(PER_BLOCK * E1) // E1
    own = (row_head[:, None] == column_head[None, :]) & (np.arange(P) % PAD < E1)[:, None]
    own = own.astype(f32)
    block_r = (r ** f32(P)).reshape(BLOCKS, PER_BLOCK)
    spread = np.zeros((P, 2, P), f32)
    for e in range(EXPERTS):
        spread[e, 0, e * ROWS:(e + 1) * ROWS] = 1.0
    spread[EXPERTS, 1] = 1.0
    tables = dict(
        cos=tiles(cos), sin=tiles(sin), decay=decay,
        q_decay=r[None, :] ** (i[:, None] + 1), k_decay=r[None, :] ** (P - 1 - i[:, None]),
        own_head=own, chunk_decay=own[:, None, :] * np.repeat(block_r, E1, axis=1)[None],
        spread=spread, ident=np.eye(P),
        descending=np.broadcast_to(EXPERTS - np.arange(EXPERTS), (P, T, EXPERTS)),
        power=np.broadcast_to(np.array([-0.5, 0.5])[None, :, None], (P, 2, T)))
    return [np.ascontiguousarray(tables[x], dtype=f32) for x in TABLES]


def by_row(a):
    return a.reshape(KC, P, -1).transpose(1, 0, 2)


def pack_attention(Wq, Wk, Wv, Wo):
    qkv = [w.reshape(H0, DH, KC, P).transpose(0, 3, 2, 1).reshape(H0, P, KC * DH) for w in (Wq, Wk, Wv)]
    return np.concatenate(qkv + [Wo.reshape(D, H0, DH).transpose(1, 2, 0)], axis=2)


def pack_experts(gate_up_proj, down_proj, sh_gate_w, sh_up_w, sh_down_w):
    def chunks(experts, shared):
        n = shared.shape[1]
        e = experts.reshape(EXPERTS, E_CHUNKS, ROWS, n).transpose(1, 0, 2, 3).reshape(E_CHUNKS, P, n)
        s = np.zeros((S_CHUNKS * P, n), shared.dtype)
        s[:I_SHARED] = shared
        s = iter(s.reshape(S_CHUNKS, P, n))
        e = iter(e)
        return np.stack([next(s if x else e) for x in SHARED])

    gate = chunks(gate_up_proj[:, :I_MOE], sh_gate_w)
    up = chunks(gate_up_proj[:, I_MOE:], sh_up_w)
    both = np.stack([gate, up], axis=1).reshape(CHUNKS, 2, P, KC, P)
    return both.transpose(0, 4, 1, 3, 2), chunks(down_proj.transpose(0, 2, 1), sh_down_w.T)


def kernel(**inputs):
    import concourse.bacc as bacc
    from concourse.bass_utils import run_bass_kernel_spmd

    a = {k: np.asarray(v) for k, v in inputs.items()}
    x = a["L0_attn_resid_pre"]
    batches = x.shape[0]
    padded = np.concatenate([x, x[:1]])
    gate_up, down = pack_experts(*(a["L1_ffn_" + n] for n in
                                   ("gate_up_proj", "down_proj", "sh_gate_w", "sh_up_w", "sh_down_w")))
    router = np.concatenate([a["L1_ffn_router_weight"].T, a["L1_ffn_shared_gate_w"].T,
                             np.zeros((D, 1), np.float32)], axis=1)
    arrays = [
        padded,
        padded.reshape(batches + 1, S, KC, P).transpose(0, 3, 2, 1),
        pack_attention(*(a["L0_attn_" + n] for n in ("Wq", "Wk", "Wv", "Wo"))),
        np.broadcast_to(np.array(alibi_slopes(H0), np.float32), (P, H0)),
        gate_up, down,
        by_row(np.concatenate([a["L1_attn_Wq"], a["L1_attn_Wk"], a["L1_attn_Wv"]], axis=1)),
        by_row(router),
        by_row(a["L0_ffn_weight"]),
        np.broadcast_to(a["L0_ffn_scale"], (P, D)),
        by_row(a["L1_attn_Wo"]),
        a["L1_attn_rms_w"].reshape(KC, P).T,
    ] + shape_tables()
    names = ["x_tokens", "x_t", "w_heads", "slopes", *WEIGHTS, *TABLES]
    arrays = {f"in_{n}": np.ascontiguousarray(v) for n, v in zip(names, arrays)}
    nc = bacc.Bacc("TRN2", target_bir_lowering=False, num_devices=1)
    args = [nc.dram_tensor(n, v.shape, F32, kind="ExternalInput").ap() for n, v in arrays.items()]
    result = nc.dram_tensor("out_result", (batches, S, D), F32, kind="ExternalOutput").ap()
    two_block_kernel(nc, *args, result)
    run = run_bass_kernel_spmd(nc, [arrays], core_ids=[0])
    return run.results[0]["out_result"]
```

```python
from contextlib import ExitStack

import numpy as np

import concourse.bass as bass
from concourse import mybir

F32 = mybir.dt.float32
F32R = mybir.dt.float32r
ALU = mybir.AluOpType
ACT = mybir.ActivationFunctionType
AX = mybir.AxisListType

P = 128
D = 256
KC = D // P
S = 512
T = S // P

H0 = 16
DH = 128
PAIRS = H0 // 2
CLIP = 1024.0
MASKED = 1e30
BIG = 3e38

PASSES = ((1, 0), (0, 1), (0, 0))
HI, LO = 0, 1


class Space:

    def __init__(self, nc, stack, prefix):
        self.nc, self.stack, self.prefix = nc, stack, prefix

    def sb(self, name, shape, dt=F32):
        return self.stack.enter_context(self.nc.sbuf_tensor(self.prefix + name, shape, dt))

    def ps(self, name, shape, dt=F32):
        return self.stack.enter_context(self.nc.psum_tensor(self.prefix + name, shape, dt))

    def sem(self, name):
        return self.stack.enter_context(self.nc.semaphore(self.prefix + name))


def softmax_attention(nc, x_tokens, x_t, w_heads, slopes, y_scratch):
    batches = x_tokens.shape[0] - 1
    with ExitStack() as stack:
        m = Space(nc, stack, "attention_")
        w_qk = m.sb("w_qk", [P, H0 * 2 * 2 * KC * DH], F32R)
        w_v = [m.sb(f"w_v_{x}", [P, KC, H0 * DH], F32R) for x in ("hi", "lo")]
        w_o = [m.sb(f"w_o_{x}", [P, H0 * D], F32R) for x in ("hi", "lo")]
        split_weights(nc, w_heads, w_qk, w_v, w_o)
        attend(nc, m, batches, x_tokens, x_t, slopes, y_scratch, w_qk, w_v, w_o)


def split_weights(nc, w_heads, w_qk, w_v, w_o):
    SLOTS = 4
    QK, V, O = 2 * KC * DH, KC * DH, D
    with ExitStack() as stack:
        m = Space(nc, stack, "attention_split_")
        raw = [m.sb(f"raw_{i}", [P, QK + V + O]) for i in range(SLOTS)]
        loaded = [m.sem(f"raw_loaded_{i}") for i in range(SLOTS)]
        high_done = m.sem("w_high_done")
        low_done = m.sem("w_low_done")
        block = stack.enter_context(nc.Block())

        def parts(h, part):
            yield w_qk[:, (2 * h + part) * QK:(2 * h + part + 1) * QK], 0, QK
            yield w_v[part][:, :, h * DH:(h + 1) * DH], QK, V
            yield w_o[part][:, h * O:(h + 1) * O], QK + V, O

        def piece(i, at, n):
            r = raw[i][:, at:at + n]
            return r.rearrange("p (c n) -> p c n", c=KC) if n == V and at == QK else r

        @block.sync
        def _(sp):
            for h in range(H0):
                if h >= SLOTS:
                    sp.wait_ge(low_done, h - SLOTS + 1)
                sp.dma_start(raw[h % SLOTS][:], w_heads[h]).then_inc(loaded[h % SLOTS], 16)

        @block.scalar
        def _(act):
            for h in range(H0):
                act.wait_ge(loaded[h % SLOTS], 16 * (h // SLOTS + 1))
                for n, (dst, at, size) in enumerate(parts(h, HI)):
                    last = act.activation(dst, piece(h % SLOTS, at, size), ACT.Copy)
                last.then_inc(high_done, 1)

        @block.vector
        def _(dve):
            for h in range(H0):
                dve.wait_ge(high_done, h + 1)
                for (dst, at, size), (high, _, _) in zip(parts(h, LO), parts(h, HI)):
                    last = dve.tensor_tensor(dst, piece(h % SLOTS, at, size), high.bitcast(F32), ALU.subtract)
                last.then_inc(low_done, 1)


def attend(nc, m, batches, x_tokens, x_t, slopes, y_scratch, w_qk, w_v, w_o):
    QK = 2 * KC * DH
    stage = [m.sb(f"w_stage_{s}", [P, 2, 2, KC, DH], F32R) for s in "ab"]
    xt_raw = m.sb("xt_raw", [P, KC, S])
    xt = [m.sb(f"xt_{x}", [P, KC, S], F32R) for x in ("hi", "lo")]
    y = m.sb("y_tokens", [P, T, D])
    q = [[m.sb(f"q_{s}_{x}", [P, S], F32R) for x in ("hi", "lo")] for s in "ab"]
    k = [[m.sb(f"k_{s}_{x}", [P, S], F32R) for x in ("hi", "lo")] for s in "ab"]
    v = [m.sb(f"v_{x}", [P, T, 2 * DH], F32R) for x in ("hi", "lo")]
    z = [m.sb(f"z_{x}", [P, S], F32R) for x in ("hi", "lo")]
    pt = [m.sb(f"probs_t_{x}", [P, T, S], F32R) for x in ("hi", "lo")]
    WIDTH = [(t + 1) * P for t in range(T)]
    AT = [sum(WIDTH[:t]) for t in range(T)]
    probs = m.sb("probs", [P, sum(WIDTH)])
    distance = m.sb("distance", [P, S])
    bias = [m.sb(f"bias_{s}", [P, S]) for s in "ab"]
    slope = m.sb("slope", [P, H0])
    ident = m.sb("ident", [P, P])
    count = bias[0][:].bitcast(mybir.dt.int32)
    zeros = m.sb("zeros", [P, 2], F32R)
    low = m.sb("lowest", [P, 2 * T])
    total = m.sb("total", [P, 2 * T])
    inverse = m.sb("inverse", [P, 2 * T])
    scores = [m.ps(f"scores_{i}", [P, S]) for i in range(2)]
    turned = [m.ps(f"turned_{i}", [P, S]) for i in range(2)]
    proj = [m.ps(f"proj_{i}", [P, S]) for i in range(2)]
    out = [m.ps(f"out_{i}", [P, 2, D]) for i in range(2)]

    consts = m.sem("consts")
    stage_in = [m.sem(f"stage_{s}_in") for s in "ab"]
    xt_in, x_in = m.sem("xt_in"), m.sem("x_in")
    xt_high, xt_split = m.sem("xt_high"), m.sem("xt_split")
    proj_ready, proj_high, proj_low = m.sem("proj_ready"), m.sem("proj_high"), m.sem("proj_low")
    scores_ready, scores_clipped = m.sem("scores_ready"), m.sem("scores_clipped")
    biased, exp_done, inverse_done = m.sem("biased"), m.sem("exp_done"), m.sem("inverse_done")
    dve_passed, pool_passed = m.sem("dve_passed"), m.sem("pool_passed")
    bias_ready, probs_ready = m.sem("bias_ready"), m.sem("probs_ready")
    turned_ready, turned_high, turned_low = m.sem("turned_ready"), m.sem("turned_high"), m.sem("turned_low")
    out_ready, y_ready, y_stored = m.sem("out_ready"), m.sem("y_ready"), m.sem("y_stored")

    STEP = 8
    Q_B, K_B, V_0, V_1, Z_A, Q_A, K_A, Z_B = range(STEP)
    AHEAD = 2
    FREE = 2
    HEAD_UNIT = STEP // 2

    block = m.stack.enter_context(nc.Block())

    def numbers(eng, b, i):
        return eng.snap(b * (PAIRS * STEP) + i * STEP)

    @block.sync
    def _(sp):
        def weights(head):
            return w_qk[:, bass.ds(head * (2 * QK), 2 * QK)]

        def load_stage(slot, src):
            dst = stage[slot][:].rearrange("p a b c d -> p (a b c d)")
            sp.dma_start(dst.bitcast(F32), src.bitcast(F32)).then_inc(stage_in[slot], 16)

        def tokens(dram):
            return dram.rearrange("(t p) d -> p t d", p=P)

        sp.dma_start(xt_raw[:], x_t[0]).then_inc(xt_in, 16)
        load_stage(0, weights(0))
        load_stage(1, weights(1))
        sp.dma_start(slope[:], slopes).then_inc(consts, 16)
        sp.dma_start(y[:], tokens(x_tokens[0])).then_inc(x_in, 16)

        def step(n, next_a, next_b):
            sp.wait_ge(proj_ready, n + 2)
            load_stage(0, weights(next_a))
            sp.wait_ge(proj_ready, n + AHEAD + K_B + 1)
            load_stage(1, weights(next_b))

        with sp.Fori(0, batches) as b:
            sp.wait_ge(xt_split, b + 1)
            sp.dma_start(xt_raw[:], x_t[b + 1]).then_inc(xt_in, 16)
            with sp.Fori(0, PAIRS - 1) as i:
                step(numbers(sp, b, i), 2 * i + 2, 2 * i + 3)
            step(numbers(sp, b, PAIRS - 1), 0, 1)
            sp.wait_ge(y_ready, b + 1)
            sp.dma_start(tokens(y_scratch[b]), y[:]).then_inc(y_stored, 16)
            sp.wait_ge(y_stored, 16 * b + 16)
            sp.dma_start(y[:], tokens(x_tokens[b + 1])).then_inc(x_in, 16)
        sp.wait_ge(xt_in, 16 * (batches + 1))
        sp.wait_ge(x_in, 16 * (batches + 1))
        for s in range(2):
            sp.wait_ge(stage_in[s], 16 * (batches * PAIRS + 1))

    @block.gpsimd
    def _(pool):
        pool.memset(ident[:], 0.0).then_inc(consts, 1)
        pool.memset(zeros[:].bitcast(F32), 0.0).then_inc(consts, 1)
        pool.iota(count[:], pattern=[[-1, S]], base=S - P, channel_multiplier=0).then_inc(consts, 1)
        pool.wait_ge(consts, 16 + 3)
        pool.affine_select(ident[:], ident[:], compare_op=ALU.not_equal, fill=1.0, base=0,
                           pattern=[[-1, P]], channel_multiplier=1).then_inc(consts, 1)
        pool.tensor_copy(distance[:], count[:]).then_inc(consts, 1)
        pool.wait_ge(consts, 16 + 5)
        pool.affine_select(distance[:], distance[:], compare_op=ALU.is_ge, fill=MASKED, base=S - P,
                           pattern=[[-1, S]], channel_multiplier=1).then_inc(consts, 1)
        pool.wait_ge(consts, 16 + 6)

        def head_bias(slot, head):
            s = slope[:, bass.ds(head, 1)].broadcast_to([P, S])
            pool.tensor_tensor(bias[slot][:], distance[:], s, ALU.mult).then_inc(bias_ready, HEAD_UNIT)

        def normalise(tile, slot):
            for t in range(T):
                pool.wait_ge(inverse_done, tile + t + 1)
                pool.sem_inc(pool_passed, 1)
                p = probs[:, AT[t]:AT[t] + WIDTH[t]]
                pool.tensor_scalar(p, p, inverse[:, slot * T + t:slot * T + t + 1], 1.0,
                                   ALU.mult, ALU.mult).then_inc(probs_ready, 1)

        head_bias(0, 0)
        head_bias(1, 1)
        normalise(0, 0)

        def step(n, next_a, next_b):
            pool.wait_ge(biased, n + T)
            head_bias(0, next_a)
            normalise(n + T, 1)
            pool.wait_ge(biased, n + 2 * T)
            head_bias(1, next_b)
            normalise(n + 2 * T, 0)

        with pool.Fori(0, batches) as b:
            with pool.Fori(0, PAIRS - 1) as i:
                step(numbers(pool, b, i), 2 * i + 2, 2 * i + 3)
            step(numbers(pool, b, PAIRS - 1), 0, 1)

    @block.tensor
    def _(pe):
        def projection(unit, slot, which):
            for n, (a, b) in enumerate((p, c) for c in range(KC) for p in PASSES):
                last = pe.matmul(proj[unit % 2][:], stage[slot][:, a[0], which, b], xt[a[1]][:, b],
                                 start=(n == 0), stop=(n == 3 * KC - 1))
            last.then_inc(proj_ready, 1)

        def values(half, col):
            for t in range(2):
                at = (2 * half + t) * P
                for n, (a, c) in enumerate((p, c) for c in range(KC) for p in PASSES):
                    last = pe.matmul(proj[half][:, t * 2 * DH:(t + 1) * 2 * DH], xt[a[0]][:, c, at:at + P],
                                     w_v[a[1]][:, c, bass.ds(col, 2 * DH)],
                                     start=(n == 0), stop=(n == 3 * KC - 1))
            last.then_inc(proj_ready, 1)

        def score_tile(slot, t):
            for n, a in enumerate(PASSES):
                last = pe.matmul(scores[t % 2][:, 0:WIDTH[t]], q[slot][a[0]][:, t * P:(t + 1) * P],
                                 k[slot][a[1]][:, 0:WIDTH[t]], start=(n == 0), stop=(n == 2))
            last.then_inc(scores_ready, 1)

        def turn(tile, tiles=range(T)):
            for t in tiles:
                pe.wait_ge(probs_ready, tile + t + 1)
                pe.wait_ge(turned_low, tile + t - 1 + FREE)
                for c in range(t + 1):
                    last = pe.transpose(turned[t % 2][:, c * P:(c + 1) * P],
                                        probs[:, AT[t] + c * P:AT[t] + (c + 1) * P], ident[:])
                last.then_inc(turned_ready, 1)

        def attended(unit, slot, number):
            for c in range(T):
                if unit == Z_A and c % 2 == 0:
                    pe.wait_ge(proj_low, number + AHEAD + (V_0 if c == 0 else V_1) + 1)
                for n, a in enumerate(PASSES):
                    last = pe.matmul(proj[unit % 2][:, c * P:S], v[a[0]][:, c, slot * DH:(slot + 1) * DH],
                                     pt[a[1]][:, c, c * P:S], start=(c == 0 and n == 0),
                                     stop=(c == T - 1 and n == 2))
            last.then_inc(proj_ready, 1)

        def project_out(col, tiles=range(T)):
            for t in tiles:
                for a in PASSES:
                    last = pe.matmul(out[t // 2][:, t % 2], z[a[0]][:, t * P:(t + 1) * P],
                                     w_o[a[1]][:, bass.ds(col, D)], start=False, stop=False,
                                     skip_group_check=True)
            return last

        def clear_out():
            for bank in out:
                pe.matmul(bank[:, 0, 0:2], w_qk[:, 0:P], zeros[:], start=True, stop=True,
                          skip_group_check=True)

        def free_bank(n, unit):
            pe.wait_ge(proj_low, n + AHEAD + unit - 1)

        pe.wait_ge(consts, 16 + 6)
        pe.wait_ge(xt_split, 1)
        pe.wait_ge(stage_in[0], 16)
        projection(0, 0, 0)
        projection(1, 0, 1)
        clear_out()
        pe.wait_ge(proj_low, 2)
        for t in range(T):
            if t >= 2:
                pe.wait_ge(scores_clipped, t - 1)
            score_tile(0, t)
        turn(0, (0, 1))

        def step(b, n, i, last_pair):
            def scores_of(slot, tile, tiles):
                for t in tiles:
                    pe.wait_ge(scores_clipped, tile + t - 1)
                    score_tile(slot, t)

            pe.wait_ge(stage_in[1], 2 * n + 16)
            for unit, which in ((Q_B, 0), (K_B, 1)):
                free_bank(n, unit)
                projection(unit, 1, which)
            turn(n, (2,))
            free_bank(n, V_0)
            values(0, i * (2 * DH))
            turn(n, (3,))
            free_bank(n, V_1)
            values(1, i * (2 * DH))
            pe.wait_ge(proj_low, n + AHEAD + K_B + 1)
            scores_of(1, n + T, (0, 1))
            free_bank(n, Z_A)
            pe.wait_ge(turned_low, n + T + FREE)
            attended(Z_A, 0, n)
            scores_of(1, n + T, (2, 3))
            turn(n + T, (0, 1))
            pe.wait_ge(stage_in[0], 2 * n + 32)
            if last_pair:
                pe.wait_ge(xt_split, b + 2)
            for unit, which in ((Q_A, 0), (K_A, 1)):
                free_bank(n, unit)
                projection(unit, 0, which)
            pe.wait_ge(proj_low, n + AHEAD + Z_A + 1)
            project_out(i * (2 * D), (0, 1))
            turn(n + T, (2, 3))
            project_out(i * (2 * D), (2, 3))
            pe.wait_ge(proj_low, n + AHEAD + K_A + 1)
            scores_of(0, n + 2 * T, (0, 1))
            free_bank(n, Z_B)
            pe.wait_ge(turned_low, n + 2 * T + FREE)
            attended(Z_B, 1, n)
            scores_of(0, n + 2 * T, (2, 3))
            turn(n + 2 * T, (0, 1))
            pe.wait_ge(proj_low, n + AHEAD + Z_B + 1)
            last = project_out(i * (2 * D) + D)
            if last_pair:
                last.then_inc(out_ready, 1)

        with pe.Fori(0, batches) as b:
            with pe.Fori(0, PAIRS - 1) as i:
                step(b, numbers(pe, b, i), i, False)
            step(b, numbers(pe, b, PAIRS - 1), PAIRS - 1, True)
            pe.wait_ge(y_ready, b + 1)
            clear_out()

    NEGATIVE_SCALE = -1.0 / DH ** 0.5

    def unit_target(number, unit):
        bank = proj[number % 2][:]
        if unit in (V_0, V_1):
            t = 2 * (unit - V_0)
            return bank.rearrange("p (t n) -> p t n", t=2), [x[:, t:t + 2] for x in v], 1.0
        if unit in (Q_A, Q_B):
            return bank, [x[:] for x in q[unit == Q_B]], NEGATIVE_SCALE
        if unit in (K_A, K_B):
            return bank, [x[:] for x in k[unit == K_B]], 1.0
        return bank, [x[:] for x in z], 1.0

    @block.scalar
    def _(act):
        def split_x(b):
            act.wait_ge(xt_in, 16 * b + 16)
            act.activation(xt[HI][:], xt_raw[:], ACT.Copy).then_inc(xt_high, 1)

        def unit_high(number, unit, before=0):
            bank, dst, scale = unit_target(number, unit)
            act.wait_ge(proj_ready, before + number + 1)
            act.activation(dst[HI], bank, ACT.Copy, scale=scale).then_inc(proj_high, 1)

        def exponentials(tile, slot, t):
            act.wait_ge(biased, tile + t + 1)
            p = probs[:, AT[t]:AT[t] + WIDTH[t]]
            c = slot * T + t
            act.activation(p, p, ACT.Exp, bias=low[:, c:c + 1], scale=-1.0,
                           accum_out=total[:, c:c + 1]).then_inc(exp_done, 1)

        def turned_to_high(tile, tiles):
            for t in tiles:
                act.wait_ge(turned_ready, tile + t + 1)
                act.activation(pt[HI][:, 0:t + 1, t * P:(t + 1) * P],
                               turned[t % 2][:, 0:WIDTH[t]].rearrange("p (c n) -> p c n", c=t + 1),
                               ACT.Copy).then_inc(turned_high, 1)

        split_x(0)
        for number, unit in enumerate((Q_A, K_A)):
            unit_high(number, unit)
        exponentials(0, 0, 0)
        exponentials(0, 0, 1)
        turned_to_high(0, (0, 1))
        exponentials(0, 0, 2)
        exponentials(0, 0, 3)

        def step(b, n, last_pair):
            unit_high(AHEAD + Q_B, Q_B, n)
            unit_high(AHEAD + K_B, K_B, n)
            turned_to_high(n, (2,))
            unit_high(AHEAD + V_0, V_0, n)
            turned_to_high(n, (3,))
            unit_high(AHEAD + V_1, V_1, n)
            if last_pair:
                split_x(b + 1)
            exponentials(n + T, 1, 0)
            exponentials(n + T, 1, 1)
            unit_high(AHEAD + Z_A, Z_A, n)
            turned_to_high(n + T, (0, 1))
            exponentials(n + T, 1, 2)
            exponentials(n + T, 1, 3)
            unit_high(AHEAD + Q_A, Q_A, n)
            unit_high(AHEAD + K_A, K_A, n)
            turned_to_high(n + T, (2, 3))
            exponentials(n + 2 * T, 0, 0)
            exponentials(n + 2 * T, 0, 1)
            unit_high(AHEAD + Z_B, Z_B, n)
            turned_to_high(n + 2 * T, (0, 1))
            exponentials(n + 2 * T, 0, 2)
            exponentials(n + 2 * T, 0, 3)

        with act.Fori(0, batches) as b:
            with act.Fori(0, PAIRS - 1) as i:
                step(b, numbers(act, b, i), False)
            step(b, numbers(act, b, PAIRS - 1), True)

    @block.vector
    def _(dve):
        def split_x(b):
            dve.wait_ge(xt_high, b + 1)
            dve.tensor_tensor(xt[LO][:], xt_raw[:], xt[HI][:].bitcast(F32), ALU.subtract).then_inc(xt_split, 1)

        def unit_low(number, unit, before=0):
            bank, dst, scale = unit_target(number, unit)
            dve.wait_ge(proj_high, before + number + 1)
            high = dst[HI].bitcast(F32)
            if scale == 1.0:
                dve.tensor_tensor(dst[LO], bank, high, ALU.subtract).then_inc(proj_low, 1)
            else:
                dve.scalar_tensor_tensor(dst[LO], bank, scale, high, ALU.mult, ALU.subtract).then_inc(proj_low, 1)

        def clip(tile, t, first=False):
            dve.wait_ge(scores_ready, tile + t + 1)
            if not first:
                dve.wait_ge(turned_ready, tile + t - T + 1)
            dve.tensor_scalar(probs[:, AT[t]:AT[t] + WIDTH[t]], scores[t % 2][:, 0:WIDTH[t]], CLIP, -CLIP,
                              ALU.min, ALU.max).then_inc(scores_clipped, 1)

        def add_bias(tile, slot, t, biases):
            if t == 0:
                dve.wait_ge(bias_ready, biases)
            dve.wait_ge(scores_clipped, tile + t + 1)
            dve.sem_inc(dve_passed, 1)
            p = probs[:, AT[t]:AT[t] + WIDTH[t]]
            c = slot * T + t
            dve.tensor_tensor_reduce(p, p, bias[slot][:, S - WIDTH[t]:S], 1.0, BIG, ALU.add, ALU.min,
                                     low[:, c:c + 1]).then_inc(biased, 1)

        def invert(tile, slot, t):
            dve.wait_ge(exp_done, tile + t + 1)
            c = slot * T + t
            dve.reciprocal(inverse[:, c:c + 1], total[:, c:c + 1]).then_inc(inverse_done, 1)

        def turned_to_low(tile, tiles):
            for t in tiles:
                dve.wait_ge(turned_high, tile + t + 1)
                dst = [x[:, 0:t + 1, t * P:(t + 1) * P] for x in pt]
                dve.tensor_tensor(dst[LO], turned[t % 2][:, 0:WIDTH[t]].rearrange("p (c n) -> p c n", c=t + 1),
                                  dst[HI].bitcast(F32), ALU.subtract).then_inc(turned_low, 1)

        def softmax(tile, slot, biases, between, first=False):
            clip(tile, 0, first)
            clip(tile, 1, first)
            add_bias(tile, slot, 0, biases)
            add_bias(tile, slot, 1, biases)
            invert(tile, slot, 0)
            invert(tile, slot, 1)
            between[0]()
            clip(tile, 2, first)
            clip(tile, 3, first)
            add_bias(tile, slot, 2, biases)
            add_bias(tile, slot, 3, biases)
            turned_to_low(tile, (0, 1))
            invert(tile, slot, 2)
            invert(tile, slot, 3)
            between[1]()
            between[2]()

        def nothing():
            pass

        dve.engine_nop().then_inc(turned_low, FREE)
        split_x(0)
        for number, unit in enumerate((Q_A, K_A)):
            unit_low(number, unit)
        softmax(0, 0, HEAD_UNIT, (nothing, nothing, nothing), first=True)

        def step(b, n, last_pair):
            unit_low(AHEAD + Q_B, Q_B, n)
            unit_low(AHEAD + K_B, K_B, n)
            turned_to_low(n, (2,))
            unit_low(AHEAD + V_0, V_0, n)
            turned_to_low(n, (3,))
            unit_low(AHEAD + V_1, V_1, n)
            if last_pair:
                split_x(b + 1)
            softmax(n + T, 1, n + 2 * HEAD_UNIT, (lambda: unit_low(AHEAD + Z_A, Z_A, n),
                                                  lambda: unit_low(AHEAD + Q_A, Q_A, n),
                                                  lambda: unit_low(AHEAD + K_A, K_A, n)))
            turned_to_low(n + T, (2, 3))
            softmax(n + 2 * T, 0, n + 3 * HEAD_UNIT, (lambda: unit_low(AHEAD + Z_B, Z_B, n), nothing, nothing))

        with dve.Fori(0, batches) as b:
            with dve.Fori(0, PAIRS - 1) as i:
                step(b, numbers(dve, b, i), False)
            step(b, numbers(dve, b, PAIRS - 1), True)
            dve.wait_ge(x_in, 16 * b + 16)
            dve.wait_ge(out_ready, b + 1)
            for half in range(2):
                part = y[:, 2 * half:2 * half + 2]
                last = dve.tensor_tensor(part, out[half][:], part, ALU.add)
            last.then_inc(y_ready, 1)


H1 = 16
E1 = D // H1
PAD = 32
BLOCKS = H1 * PAD // P
PER_BLOCK = H1 // BLOCKS
LN_EPS, RMS_EPS, NORM_EPS = 1e-5, 1e-5, 1e-7
MAX_NORM = 0.99
EXPERTS = 8
I_MOE, I_SHARED = 176, 704
ROWS = P // EXPERTS
E_CHUNKS = I_MOE // ROWS
S_CHUNKS = -(-I_SHARED // P)
CHUNKS = E_CHUNKS + S_CHUNKS
SHARED = [c % 3 == 2 or c == CHUNKS - 1 for c in range(CHUNKS)]
assert sum(SHARED) == S_CHUNKS
ROUTER = 10
GU = 2 * KC * P


def block_one(nc, y_scratch, weights, tables, result):
    with ExitStack() as stack:
        m = Space(nc, stack, "block_one_")
        resident = dict(
            gate_up=[m.sb(f"gate_up_{x}", [P, CHUNKS, 2, KC, P], F32R) for x in ("hi", "lo")],
            down=[m.sb(f"down_{x}", [P, CHUNKS, D], F32R) for x in ("hi", "lo")],
            qkv=[m.sb(f"qkv_{x}", [P, KC, 3 * D], F32R) for x in ("hi", "lo")],
            router=[m.sb(f"router_{x}", [P, KC, ROUTER], F32R) for x in ("hi", "lo")],
        )
        split_block_one(nc, weights, resident)
        block_one_layers(nc, m, y_scratch, weights, tables, resident, result)


def split_block_one(nc, weights, resident):
    SLOTS = 4
    pieces = []
    for c in range(CHUNKS):
        pieces.append((weights["gate_up"][c], *[x[:, c] for x in resident["gate_up"]]))
        pieces.append((weights["down"][c], *[x[:, c] for x in resident["down"]]))
    for c in range(KC):
        pieces.append((weights["qkv"][:, c], *[x[:, c] for x in resident["qkv"]]))
    pieces.append((weights["router"], *[x[:] for x in resident["router"]]))
    with ExitStack() as stack:
        m = Space(nc, stack, "block_one_split_")
        raw = [m.sb(f"raw_{i}", [P, 3 * D]) for i in range(SLOTS)]
        loaded = [m.sem(f"raw_loaded_{i}") for i in range(SLOTS)]
        high_done, low_done = m.sem("w_high_done"), m.sem("w_low_done")
        block = stack.enter_context(nc.Block())

        def flat(ap):
            names = "abcd"[:len(ap.shape) - 1]
            return ap if len(names) == 1 else ap.rearrange(f"p {' '.join(names)} -> p ({' '.join(names)})")

        @block.sync
        def _(sp):
            for n, (src, high, _) in enumerate(pieces):
                if n >= SLOTS:
                    sp.wait_ge(low_done, n - SLOTS + 1)
                src, size = flat(src), flat(high).shape[1]
                sp.dma_start(raw[n % SLOTS][:, 0:size], src).then_inc(loaded[n % SLOTS], 16)

        @block.scalar
        def _(act):
            for n, (_, high, _) in enumerate(pieces):
                high = flat(high)
                act.wait_ge(loaded[n % SLOTS], 16 * (n // SLOTS + 1))
                act.activation(high, raw[n % SLOTS][:, 0:high.shape[1]], ACT.Copy).then_inc(high_done, 1)

        @block.vector
        def _(dve):
            for n, (_, high, low) in enumerate(pieces):
                high, low = flat(high), flat(low)
                dve.wait_ge(high_done, n + 1)
                dve.tensor_tensor(low, raw[n % SLOTS][:, 0:high.shape[1]], high.bitcast(F32),
                                  ALU.subtract).then_inc(low_done, 1)


def block_one_layers(nc, m, y_scratch, weights, tables, resident, result):
    batches = result.shape[0]
    gate_up, down, qkv, router = (resident[x] for x in ("gate_up", "down", "qkv", "router"))
    ffn_w = m.sb("ffn_w", [P, KC, D])
    wo = m.sb("wo", [P, BLOCKS, D])
    rms_w = m.sb("rms_w", [P, BLOCKS])
    cos, sin = m.sb("cos", [P, T, E1]), m.sb("sin", [P, T, E1])
    decay = m.sb("decay", [P, PER_BLOCK, BLOCKS * P])
    q_decay = m.sb("q_decay", [P, BLOCKS * P])
    k_decay = m.sb("k_decay", [P, H1])
    own_head = m.sb("own_head", [P, P])
    chunk_decay = m.sb("chunk_decay", [P, BLOCKS])
    spread = m.sb("spread", [P, 2, P])
    ident = m.sb("ident", [P, P])
    descending = m.sb("descending", [P, T, EXPERTS])
    power = m.sb("power", [P, 2, T])
    x1 = m.sb("x1", [P, T, D])
    x2 = m.sb("x2", [P, T, D])
    x3 = m.sb("x3", [P, T, D])
    masked = m.sb("masked_scores", [P, PER_BLOCK, BLOCKS * P])
    x1t = masked[:, 0:KC]
    total = masked[:, KC:].rearrange("p a (b d) -> p (a b) d", d=D)
    x2_squares = total
    x2t = [m.sb(f"x2t_{x}", [P, KC, S], F32R) for x in ("hi", "lo")]
    x3t = [m.sb(f"x3t_{x}", [P, KC, S], F32R) for x in ("hi", "lo")]
    qk = m.sb("qk", [P, 2 * H1, E1])
    swapped = m.sb("swapped", [P, 2 * H1, E1])
    qk_pad = m.sb("qk_pad", [P, 2 * H1, PAD])
    kd_pad = m.sb("kd_pad", [P, H1, PAD])
    v_pad = m.sb("v_pad", [P, H1, PAD])
    qt, kt = m.sb("qt", [P, BLOCKS * P]), m.sb("kt", [P, BLOCKS * P])
    qt_decayed = kt
    attn_t = qt
    attn_t_squares = kt
    ffn_scale = masked[:, 0, 0:D]
    update = masked[:, 0]
    state = m.sb("state", [P, BLOCKS, P])
    ones = m.sb("ones", [P, 1])
    stats, moments = m.sb("stats", [P, T, 6]), m.sb("moments", [P, T, 2])
    variance, inverse = m.sb("variance", [P, T]), m.sb("inverse", [P, T])
    squares = m.sb("squares", [P, T])
    norm = m.sb("norm", [P, 8, T])
    attn_variance, attn_inverse = m.sb("attn_variance", [P, T]), m.sb("attn_inverse", [P, T])
    logits = m.sb("logits", [P, T, ROUTER])
    pick = m.sb("pick", [P, 5, T, EXPERTS])
    best = m.sb("best", [P, 8, T])
    mix = m.sb("mix", [P, T, EXPERTS + 1])
    mix_t = m.sb("mix_t", [EXPERTS + 1, S])
    share = [m.sb(f"share_{x}", [P, S]) for x in ("experts", "shared")]
    SLOTS = 2
    hidden = [m.sb(f"hidden_{i}", [P, S]) for i in range(SLOTS)]
    hidden_split = [[m.sb(f"hidden_{x}_{i}", [P, S], F32R) for x in ("hi", "lo")] for i in range(SLOTS)]
    BANKS = 4
    bank = [m.ps(f"bank_{i}", [P, 512]) for i in range(BANKS)]
    gate_bank, up_bank = m.ps("gate_bank", [P, S]), m.ps("up_bank", [P, S])
    out = [m.ps(f"out_{i}", [P, 2, D]) for i in range(2)]

    loaded, consts = m.sem("loaded"), m.sem("consts")
    bank_ready = [m.sem(f"bank_{i}_ready") for i in range(BANKS)]
    bank_taken = [m.sem(f"bank_{i}_taken") for i in range(BANKS)]
    gate_ready, gate_taken = m.sem("gate_ready"), m.sem("gate_taken")
    up_ready, up_taken = m.sem("up_ready"), m.sem("up_taken")
    y_in, result_out = m.sem("y_in"), m.sem("result_out")
    stats_done, inverse_done = m.sem("stats_done"), m.sem("inverse_done")
    x1_done, x2_done, x3_done = m.sem("x1_done"), m.sem("x2_done"), m.sem("x3_done")
    turned_x1 = m.sem("turned_x1")
    x2t_high, x2t_split, x3t_high, x3t_split = (m.sem(x) for x in ("x2t_high", "x2t_split", "x3t_high", "x3t_split"))
    scaled, squares_done, norms_done, norm_floored, tanh_done = (
        m.sem(x) for x in ("scaled", "squares_done", "norms_done", "norm_floored", "tanh_done"))
    qk_copied, v_copied, swapped_done, rotated, kd_done = (
        m.sem(x) for x in ("qk_copied", "v_copied", "swapped_done", "rotated", "kd_done"))
    qt_done, kt_done, masked_done = m.sem("qt_done"), m.sem("kt_done"), m.sem("masked_done")
    state_ready, state_faded, update_done = m.sem("state_ready"), m.sem("state_faded"), m.sem("update_done")
    decayed_done, attn_t_done, attn_squared, attn_variance_done, attn_inverse_done = (
        m.sem(x) for x in ("decayed_done", "attn_t_done", "attn_squared", "attn_variance_done", "attn_inverse_done"))
    gap_done, exp_done, mix_done, mix_t_done, share_done = (
        m.sem(x) for x in ("gap_done", "exp_done", "mix_done", "mix_t_done", "share_done"))
    tanh_gate, product_done, weighted, hidden_high, hidden_low = (
        m.sem(x) for x in ("tanh_gate", "product_done", "weighted", "hidden_high", "hidden_low"))
    x3_kept = m.sem("x3_kept")
    down_done, moe_done, result_ready = m.sem("down_done"), m.sem("moe_done"), m.sem("result_ready")
    front_chain, back_chain = m.sem("front_chain"), m.sem("back_chain")
    pool_chain, final_chain = m.sem("pool_chain"), m.sem("final_chain")
    final_stats, final_inverse = m.sem("final_stats"), m.sem("final_inverse")
    dve_passed, pool_passed = m.sem("dve_passed"), m.sem("pool_passed")

    X1T, FFN, X2T = 0, 2, 4
    TILE = 6
    QK_, V_, QT, KT, SCORES, MIXED, UPDATE, OUT = 0, 1, 2, 3, 4, 8, 9, 10
    PER_TILE = 11
    X3T = TILE + T * PER_TILE
    USES = X3T + KC
    PER_BANK = USES // BANKS
    RESULT_FREE = 17
    assert USES % BANKS == 0

    def at(t, use):
        return TILE + t * PER_TILE + use

    def bank_of(use):
        return bank[use % BANKS]

    def wait_bank(eng, b, use):
        eng.wait_ge(bank_ready[use % BANKS], b * PER_BANK + (use // BANKS + 1))

    def wait_free(eng, b, use):
        eng.wait_ge(bank_taken[use % BANKS], b * PER_BANK + (use // BANKS + 1))

    GATE_LOGITS, GATE_SHARE, UP_MIX, UP_SHARE = 0, 2, 1, 2
    MOE_USES = CHUNKS + 2

    def gate_use(c):
        return c + 2 if c else 1

    def up_use(c):
        return c + 2 if c else 0

    AHEAD_OF = [1, 6, 2, 8] + T * [0, 2, 2, 1, 3]
    ROUTING_STEPS = 5
    EXPERT_STEPS = ROUTING_STEPS + 3 * (CHUNKS - 1) + 1

    def interleave(layers, experts):
        for n in AHEAD_OF:
            for _ in range(n):
                next(experts)
            next(layers)
        for _ in range(EXPERT_STEPS - 1 - sum(AHEAD_OF)):
            next(experts)
        for part in (layers, experts):
            for _ in part:
                pass

    def alone(part):
        for _ in part:
            pass

    loads = [(ffn_w, weights["ffn_w"]), (ffn_scale, weights["ffn_scale"]), (wo, weights["wo"]),
             (rms_w, weights["rms_w"])] + \
            [(t, tables[x]) for x, t in dict(
                cos=cos, sin=sin, decay=decay, q_decay=q_decay, k_decay=k_decay, own_head=own_head,
                chunk_decay=chunk_decay, spread=spread, ident=ident, descending=descending,
                power=power).items()]
    LOADED = 16 * len(loads)

    block = m.stack.enter_context(nc.Block())

    @block.sync
    def _(sp):
        def tokens(dram):
            return dram.rearrange("(t p) d -> p t d", p=P)

        sp.dma_start(x1[:], tokens(y_scratch[0])).then_inc(y_in, 16)
        for dst, src in loads:
            sp.dma_start(dst[:], src).then_inc(loaded, 16)

        def store(b):
            sp.wait_ge(result_ready, b + 1)
            sp.dma_start(tokens(result[b]), total[:]).then_inc(result_out, 16)

        with sp.Fori(0, batches - 1) as b:
            sp.wait_ge(x3_kept, b + 1)
            sp.dma_start(x1[:], tokens(y_scratch[b + 1])).then_inc(y_in, 16)
            store(b)
        store(batches - 1)
        sp.wait_ge(result_out, 16 * batches + RESULT_FREE)


    @block.gpsimd
    def _(pool):
        pool.wait_ge(loaded, LOADED)
        pool.memset(qk_pad[:], 0.0).then_inc(consts, 1)
        pool.memset(kd_pad[:], 0.0).then_inc(consts, 1)
        pool.memset(v_pad[:], 0.0).then_inc(consts, 1)
        pool.memset(ones[:], 1.0).then_inc(consts, 1)
        pool.memset(state[:], 0.0).then_inc(state_ready, 1)

        def root(dst, src, which):
            return pool.tensor_tensor(dst, src, power[:, which, 0:dst.shape[1]], ALU.pow)

        def layer_inverse(stats_sem, count, chain, chain_value, signal):
            pool.wait_ge(stats_sem, count)
            pool.sem_inc(pool_passed, 1)
            pool.tensor_scalar(variance[:], moments[:, :, 1], LN_EPS, 1.0, ALU.add, ALU.mult)\
                .then_inc(chain, 1)
            pool.wait_ge(chain, chain_value)
            root(inverse[:], variance[:], 0).then_inc(signal, 1)

        CHAIN = 3

        def layers(b):
            layer_inverse(stats_done, 3 * b + 1, pool_chain, CHAIN * b + 1, inverse_done)
            yield
            yield
            pool.wait_ge(squares_done, b + 1)
            root(norm[:, 0], squares[:], 1).then_inc(norms_done, 1)
            layer_inverse(stats_done, 3 * b + 2, pool_chain, CHAIN * b + 2, inverse_done)
            yield
            yield
            for t in range(T):
                half = E1 // 2
                pool.wait_ge(qk_copied, T * b + t + 1)
                s = sin[:, t, None, :].broadcast_to([P, 2 * H1, E1])
                pool.tensor_tensor(swapped[:, :, 0:half], qk[:, :, half:E1], s[:, :, 0:half], ALU.mult)
                pool.tensor_tensor(swapped[:, :, half:E1], qk[:, :, 0:half], s[:, :, half:E1], ALU.mult)\
                    .then_inc(swapped_done, 1)
                yield
                pool.wait_ge(rotated, T * b + t + 1)
                pool.tensor_tensor(kd_pad[:, :, 0:E1], qk_pad[:, H1:, 0:E1],
                                   k_decay[:, :, None].broadcast_to([P, H1, E1]), ALU.mult).then_inc(kd_done, 1)
                yield
                wait_bank(pool, b, at(t, SCORES + PER_BLOCK - 1))
                pool.tensor_tensor(qt_decayed[:], qt[:], q_decay[:], ALU.mult).then_inc(decayed_done, 1)
                yield
                wait_bank(pool, b, at(t, MIXED))
                if t < T - 1:
                    pool.tensor_tensor(state[:], state[:], chunk_decay[:, :, None].broadcast_to([P, BLOCKS, P]),
                                       ALU.mult).then_inc(state_faded, 1)
                    pool.wait_ge(state_faded, (T - 1) * b + t + 1)
                    pool.wait_ge(update_done, (T - 1) * b + t + 1)
                    pool.tensor_tensor(state[:], state[:], update[:].rearrange("p (g n) -> p g n", g=BLOCKS),
                                       ALU.add).then_inc(state_ready, 1)
                else:
                    pool.sem_inc(pool_passed, 1)
                    pool.memset(state[:], 0.0).then_inc(state_ready, 1)
                yield
                pool.wait_ge(attn_variance_done, T * b + t + 1)
                root(attn_inverse[:, t:t + 1], attn_variance[:, t:t + 1], 0).then_inc(attn_inverse_done, 1)
                if t == T - 1:
                    layer_inverse(stats_done, 3 * b + 3, pool_chain, CHAIN * b + 3, inverse_done)
                yield

        def experts(b):
            for _ in range(ROUTING_STEPS - 1):
                yield
            pool.wait_ge(share_done, 2 * b + 2)
            weight(b, 0)
            yield
            for c in range(1, CHUNKS):
                yield
                weight(b, c)
                yield
                yield
            layer_inverse(final_stats, b + 1, final_chain, b + 1, final_inverse)

        def weight(b, c):
            pool.wait_ge(product_done, CHUNKS * b + c + 1)
            h = hidden[c % SLOTS][:]
            pool.tensor_tensor(h, h, share[SHARED[c]][:], ALU.mult).then_inc(weighted, 1)

        alone(layers(0))
        with pool.Fori(0, batches - 1) as b:
            interleave(layers(b + 1), experts(b))
        alone(experts(batches - 1))

    @block.tensor
    def _(pe):
        def transposes(b, use, src, col):
            wait_free(pe, b, use)
            for t in range(T):
                last = pe.transpose(bank_of(use)[:, t * P:(t + 1) * P], src[:, t, col:col + P], ident[:])
            last.then_inc(bank_ready[use % BANKS], 1)

        def layers(b):
            yield
            pe.wait_ge(x1_done, b + 1)
            for c in range(KC):
                transposes(b, X1T + c, x1, c * P)
            yield
            pe.wait_ge(turned_x1, 2 * b + 2)
            for half in range(2):
                wait_free(pe, b, FFN + half)
                for t in range(2):
                    row = (2 * half + t) * P
                    for c in range(KC):
                        last = pe.matmul(bank_of(FFN + half)[:, t * D:(t + 1) * D], x1t[:, c, row:row + P],
                                         ffn_w[:, c], start=(c == 0), stop=(c == KC - 1))
                last.then_inc(bank_ready[(FFN + half) % BANKS], 1)
            yield
            pe.wait_ge(x2_done, b + 1)
            for c in range(KC):
                transposes(b, X2T + c, x2, c * P)
            yield
            pe.wait_ge(x2t_split, 2 * b + 2)
            for t in range(T):
                row = t * P
                for use, lo, hi in ((QK_, 0, 2 * D), (V_, 2 * D, 3 * D)):
                    wait_free(pe, b, at(t, use))
                    for n, (p, c) in enumerate((p, c) for c in range(KC) for p in PASSES):
                        last = pe.matmul(bank_of(at(t, use))[:, 0:hi - lo], x2t[p[0]][:, c, row:row + P],
                                         qkv[p[1]][:, c, lo:hi], start=(n == 0), stop=(n == 3 * KC - 1))
                    last.then_inc(bank_ready[at(t, use) % BANKS], 1)
                yield
                pe.wait_ge(rotated, T * b + t + 1)
                for use, first in ((QT, 0), (KT, H1)):
                    wait_free(pe, b, at(t, use))
                    for g in range(BLOCKS):
                        heads = qk_pad[:, first + g * PER_BLOCK:first + (g + 1) * PER_BLOCK]
                        last = pe.transpose(bank_of(at(t, use))[:, g * P:(g + 1) * P],
                                            heads.rearrange("p a b -> p (a b)"), ident[:])
                    last.then_inc(bank_ready[at(t, use) % BANKS], 1)
                yield
                pe.wait_ge(qt_done, T * b + t + 1)
                pe.wait_ge(kt_done, T * b + t + 1)
                for j in range(PER_BLOCK):
                    wait_free(pe, b, at(t, SCORES + j))
                for g in range(BLOCKS):
                    for j in range(PER_BLOCK):
                        rows = slice(j * PAD, j * PAD + E1)
                        last = pe.matmul(bank_of(at(t, SCORES + j))[:, g * P:(g + 1) * P],
                                         kt[rows, g * P:(g + 1) * P], qt[rows, g * P:(g + 1) * P],
                                         start=True, stop=True)
                        if g == BLOCKS - 1:
                            last.then_inc(bank_ready[at(t, SCORES + j) % BANKS], 1)
                yield
                pe.wait_ge(v_copied, T * b + t + 1)
                wait_free(pe, b, at(t, MIXED))
                mixed = bank_of(at(t, MIXED))
                for j in range(PER_BLOCK):
                    pe.wait_ge(masked_done, (T * b + t) * PER_BLOCK + j + 1)
                    for g in range(BLOCKS):
                        pe.matmul(mixed[j * PAD:(j + 1) * PAD, g * P:(g + 1) * P],
                                  v_pad[:, g * PER_BLOCK + j], masked[:, j, g * P:(g + 1) * P],
                                  start=(g == 0), stop=False, skip_group_check=True)
                pe.wait_ge(state_ready, T * b + t + 1)
                pe.wait_ge(decayed_done, T * b + t + 1)
                for g in range(BLOCKS):
                    last = pe.matmul(mixed[:, g * P:(g + 1) * P], state[:, g], qt_decayed[:, g * P:(g + 1) * P],
                                     start=False, stop=True, skip_group_check=True)
                last.then_inc(bank_ready[at(t, MIXED) % BANKS], 1)
                pe.wait_ge(kd_done, T * b + t + 1)
                wait_free(pe, b, at(t, UPDATE))
                for g in range(BLOCKS):
                    keys, values = (x[:, g * PER_BLOCK:(g + 1) * PER_BLOCK].rearrange("p a b -> p (a b)")
                                    for x in (kd_pad, v_pad))
                    last = pe.matmul(bank_of(at(t, UPDATE))[:, g * P:(g + 1) * P], keys, values,
                                     start=True, stop=True)
                last.then_inc(bank_ready[at(t, UPDATE) % BANKS], 1)
                yield
                wait_free(pe, b, at(t, OUT))
                pe.wait_ge(attn_t_done, T * b + t + 1)
                for g in range(BLOCKS):
                    pe.matmul(bank_of(at(t, OUT))[:, 0:D], attn_t[:, g * P:(g + 1) * P], wo[:, g],
                              start=(g == 0), stop=(g == BLOCKS - 1))
                pe.wait_ge(attn_squared, T * b + t + 1)
                for g in range(BLOCKS):
                    last = pe.matmul(bank_of(at(t, OUT))[:, D:D + 1], attn_t_squares[:, g * P:(g + 1) * P], ones[:],
                                     start=(g == 0), stop=(g == BLOCKS - 1))
                last.then_inc(bank_ready[at(t, OUT) % BANKS], 1)
                yield
            pe.wait_ge(x3_done, b + 1)
            for c in range(KC):
                transposes(b, X3T + c, x1, c * P)

        def experts(b):
            def free(taken, use):
                pe.wait_ge(taken, MOE_USES * b + use + 1)

            def expand(c, which, target, use, taken, ready):
                free(taken, use)
                for n, (p, k) in enumerate((p, k) for k in range(KC) for p in PASSES):
                    last = pe.matmul(target[:], gate_up[p[0]][:, c, which, k], x3t[p[1]][:, k],
                                     start=(n == 0), stop=(n == 3 * KC - 1))
                last.then_inc(ready, 1)

            def gate(c):
                expand(c, 0, gate_bank, gate_use(c), gate_taken, gate_ready)

            def up(c):
                expand(c, 1, up_bank, up_use(c), up_taken, up_ready)

            def contract(c):
                pe.wait_ge(hidden_low, CHUNKS * b + c + 1)
                for t in range(T):
                    for n, p in enumerate(PASSES):
                        last = pe.matmul(out[t // 2][:, t % 2], hidden_split[c % SLOTS][p[0]][:, t * P:(t + 1) * P],
                                         down[p[1]][:, c], start=(c == 0 and n == 0 and t % 2 == 0),
                                         stop=(c == CHUNKS - 1 and n == 2), skip_group_check=True)
                last.then_inc(down_done, 1)

            pe.wait_ge(x3t_split, 2 * b + 2)
            free(gate_taken, GATE_LOGITS)
            for t in range(T):
                for n, (p, c) in enumerate((p, c) for c in range(KC) for p in PASSES):
                    last = pe.matmul(gate_bank[:, t * ROUTER:(t + 1) * ROUTER],
                                     x3t[p[0]][:, c, t * P:(t + 1) * P], router[p[1]][:, c],
                                     start=(n == 0), stop=(n == 3 * KC - 1))
            last.then_inc(gate_ready, 1)
            yield
            gate(0)
            yield
            up(0)
            yield
            pe.wait_ge(mix_done, b + 1)
            free(up_taken, UP_MIX)
            for t in range(T):
                last = pe.matmul(up_bank[0:EXPERTS + 1, t * P:(t + 1) * P], mix[:, t], ident[:],
                                 start=True, stop=True)
            last.then_inc(up_ready, 1)
            yield
            pe.wait_ge(mix_t_done, b + 1)
            free(gate_taken, GATE_SHARE)
            pe.matmul(gate_bank[:], spread[0:EXPERTS + 1, 0], mix_t[:], start=True, stop=True).then_inc(gate_ready, 1)
            free(up_taken, UP_SHARE)
            pe.matmul(up_bank[:], spread[0:EXPERTS + 1, 1], mix_t[:], start=True, stop=True).then_inc(up_ready, 1)
            yield
            for c in range(1, CHUNKS):
                gate(c)
                yield
                up(c)
                yield
                if c == 1:
                    pe.wait_ge(moe_done, b + 1)
                contract(c - 1)
                yield
            contract(CHUNKS - 1)

        pe.wait_ge(loaded, LOADED)
        pe.wait_ge(consts, 6)
        alone(layers(0))
        with pe.Fori(0, batches - 1) as b:
            interleave(layers(b + 1), experts(b))
        alone(experts(batches - 1))

    @block.scalar
    def _(act):
        def layers(b):
            yield
            wait_bank(act, b, X1T)
            act.activation(x1t[:, 0], bank_of(X1T)[:], ACT.Copy).then_inc(bank_taken[X1T % BANKS], 1)
            yield
            act.wait_ge(result_out, 16 * b + 1)
            act.wait_ge(scaled, b + 1)
            for t in range(T):
                last = act.activation(x2_squares[:, t], x2[:, t], ACT.Square, accum_out=squares[:, t:t + 1])
            last.then_inc(squares_done, 1)
            act.wait_ge(norm_floored, b + 1)
            act.activation(norm[:, 2], norm[:, 1], ACT.Tanh).then_inc(tanh_done, 1)
            yield
            for c in range(KC):
                wait_bank(act, b, X2T + c)
                act.activation(x2t[HI][:, c], bank_of(X2T + c)[:], ACT.Copy).then_inc(x2t_high, 1)
            yield
            for t in range(T):
                wait_bank(act, b, at(t, QK_))
                act.activation(qk[:].rearrange("p a b -> p (a b)"), bank_of(at(t, QK_))[:], ACT.Copy)\
                    .then_inc(qk_copied, 1)
                wait_bank(act, b, at(t, V_))
                act.activation(v_pad[:, :, 0:E1], bank_of(at(t, V_))[:, 0:D].rearrange("p (h e) -> p h e", h=H1),
                               ACT.Copy).then_inc(v_copied, 1)
                yield
                wait_bank(act, b, at(t, QT))
                act.activation(qt[:], bank_of(at(t, QT))[:], ACT.Copy).then_inc(qt_done, 1)
                yield
                yield
                wait_bank(act, b, at(t, MIXED))
                mixed = bank_of(at(t, MIXED))[:]
                act.activation(attn_t[:], mixed, ACT.Copy).then_inc(attn_t_done, 1)
                act.activation(attn_t_squares[:], mixed, ACT.Square).then_inc(attn_squared, 1)
                yield
                yield
            for c in range(KC):
                wait_bank(act, b, X3T + c)
                act.activation(x3t[HI][:, c], bank_of(X3T + c)[:], ACT.Copy).then_inc(x3t_high, 1)

        def experts(b):
            def tanh(c):
                act.wait_ge(gate_ready, MOE_USES * b + gate_use(c) + 1)
                act.activation(hidden[c % SLOTS][:], gate_bank[:], ACT.Tanh, scale=0.5).then_inc(tanh_gate, 1)

            def high(c):
                act.wait_ge(weighted, CHUNKS * b + c + 1)
                act.activation(hidden_split[c % SLOTS][HI][:], hidden[c % SLOTS][:], ACT.Copy)\
                    .then_inc(hidden_high, 1)

            act.wait_ge(x3_done, b + 1)
            act.wait_ge(moe_done, b + 1)
            act.activation(x3[:], x1[:], ACT.Copy).then_inc(x3_kept, 1)
            act.wait_ge(gap_done, b + 1)
            act.activation(best[:, 4], best[:, 3], ACT.Exp)
            act.activation(best[:, 5], logits[:, :, EXPERTS], ACT.Exp, scale=-1.0).then_inc(exp_done, 1)
            yield
            tanh(0)
            yield
            yield
            yield
            act.wait_ge(gate_ready, MOE_USES * b + GATE_SHARE + 1)
            act.activation(share[0][:], gate_bank[:], ACT.Copy).then_inc(share_done, 1)
            yield
            for c in range(1, CHUNKS):
                tanh(c)
                if c == 1:
                    high(0)
                yield
                yield
                high(c)
                yield

        act.wait_ge(loaded, LOADED)
        act.wait_ge(consts, 6)
        alone(layers(0))
        with act.Fori(0, batches - 1) as b:
            interleave(layers(b + 1), experts(b))
        alone(experts(batches - 1))

    @block.vector
    def _(dve):
        dve.wait_ge(loaded, LOADED)
        for g in range(BLOCKS):
            last = dve.tensor_scalar(wo[:, g], wo[:, g], rms_w[:, g:g + 1], None, ALU.mult)
        last.then_inc(consts, 1)
        dve.tensor_tensor(ffn_w[:], ffn_w[:], ffn_scale[:, None, :].broadcast_to([P, KC, D]), ALU.mult)\
            .then_inc(consts, 1)
        dve.wait_ge(consts, 6)
        for s in bank_taken + [gate_taken, up_taken, moe_done]:
            dve.sem_inc(s, 1)
        dve.sem_inc(result_out, RESULT_FREE)
        FRONT_LINKS, BACK_LINKS = 26, 58

        class Chain:

            def __init__(self, sem, base, links):
                self.sem, self.base, self.n, self.links = sem, base, 0, links

            def link(self, instruction):
                instruction.then_inc(self.sem, 1)
                self.n += 1
                dve.wait_ge(self.sem, self.base + self.n)

            def close(self):
                assert self.n == self.links, self.n

        def statistics(chain, src, signal):
            for t in range(T):
                last = dve.bn_stats(stats[:, t], src[:, t])
            chain.link(last)
            dve.sem_inc(dve_passed, 1)
            for t in range(T):
                last = dve.bn_aggr(moments[:, t], stats[:, t])
            last.then_inc(signal, 1)

        def normalise(src, dst, signal):
            for t in range(T):
                last = dve.tensor_scalar(dst[:, t], src[:, t], moments[:, t, 0:1], inverse[:, t:t + 1],
                                         ALU.subtract, ALU.mult)
            last.then_inc(signal, 1)

        def layers(b):
            chain = Chain(front_chain, b * FRONT_LINKS, FRONT_LINKS)
            link = chain.link
            dve.wait_ge(y_in, 16 * b + 16)
            statistics(chain, x1, stats_done)
            dve.wait_ge(inverse_done, 3 * b + 1)
            normalise(x1, x1, x1_done)
            yield
            wait_bank(dve, b, X1T + 1)
            last = dve.tensor_copy(x1t[:, 1], bank_of(X1T + 1)[:])
            last.then_inc(turned_x1, 1)
            dve.wait_ge(bank_taken[X1T % BANKS], b * PER_BANK + 2)
            dve.sem_inc(turned_x1, 1)
            dve.wait_ge(turned_x1, 2 * b + 1)
            dve.sem_inc(bank_taken[(X1T + 1) % BANKS], 1)
            yield
            for half in range(2):
                wait_bank(dve, b, FFN + half)
                link(dve.tensor_copy(x2[:, 2 * half:2 * half + 2],
                                     bank_of(FFN + half)[:].rearrange("p (t n) -> p t n", t=2)))
                dve.sem_inc(bank_taken[(FFN + half) % BANKS], 1)
            dve.sem_inc(scaled, 1)
            dve.wait_ge(norms_done, b + 1)
            root, floored, tanh, shrink = norm[:, 0], norm[:, 1], norm[:, 2], norm[:, 3]
            tmp, tmp2, factor = norm[:, 4], norm[:, 5], norm[:, 6]
            dve.tensor_scalar(floored, root, NORM_EPS, None, ALU.max).then_inc(norm_floored, 1)
            dve.wait_ge(norm_floored, b + 1)
            link(dve.tensor_scalar(tmp, floored, NORM_EPS, None, ALU.add))
            link(dve.reciprocal(tmp2, tmp))
            dve.wait_ge(tanh_done, b + 1)
            link(dve.tensor_tensor(shrink, tanh, tmp2, ALU.mult))
            link(dve.tensor_tensor(tmp, shrink, root, ALU.mult))
            link(dve.tensor_scalar(tmp2, tmp, NORM_EPS, None, ALU.max))
            link(dve.reciprocal(tmp, tmp2))
            link(dve.tensor_scalar(tmp2, tmp, MAX_NORM, 1.0, ALU.mult, ALU.min))
            link(dve.tensor_tensor(factor, shrink, tmp2, ALU.mult))
            for t in range(T):
                last = dve.scalar_tensor_tensor(x2[:, t], x2[:, t], factor[:, t:t + 1], x1[:, t],
                                                ALU.mult, ALU.add)
            link(last)
            statistics(chain, x2, stats_done)
            dve.wait_ge(inverse_done, 3 * b + 2)
            normalise(x2, x2, x2_done)
            yield
            for c in range(KC):
                dve.wait_ge(x2t_high, KC * b + c + 1)
                link(dve.tensor_tensor(x2t[LO][:, c], bank_of(X2T + c)[:], x2t[HI][:, c].bitcast(F32), ALU.subtract))
                dve.sem_inc(bank_taken[(X2T + c) % BANKS], 1)
                dve.sem_inc(x2t_split, 1)
            yield
            for t in range(T):
                dve.wait_ge(qk_copied, T * b + t + 1)
                dve.sem_inc(bank_taken[at(t, QK_) % BANKS], 1)
                c = cos[:, t, None, :].broadcast_to([P, 2 * H1, E1])
                link(dve.tensor_tensor(qk_pad[:, :, 0:E1], qk[:], c, ALU.mult))
                dve.wait_ge(swapped_done, T * b + t + 1)
                dve.tensor_tensor(qk_pad[:, :, 0:E1], qk_pad[:, :, 0:E1], swapped[:], ALU.add)\
                    .then_inc(rotated, 1)
                dve.wait_ge(v_copied, T * b + t + 1)
                dve.sem_inc(bank_taken[at(t, V_) % BANKS], 1)
                yield
                wait_bank(dve, b, at(t, KT))
                dve.tensor_copy(kt[:], bank_of(at(t, KT))[:]).then_inc(kt_done, 1)
                dve.wait_ge(kt_done, T * b + t + 1)
                dve.sem_inc(bank_taken[at(t, KT) % BANKS], 1)
                dve.wait_ge(qt_done, T * b + t + 1)
                dve.sem_inc(bank_taken[at(t, QT) % BANKS], 1)
                yield
                dve.wait_ge(state_ready, T * b + t + 1)
                for j in range(PER_BLOCK):
                    wait_bank(dve, b, at(t, SCORES + j))
                    dve.tensor_tensor(masked[:, j], bank_of(at(t, SCORES + j))[:], decay[:, j], ALU.mult)\
                        .then_inc(masked_done, 1)
                    dve.wait_ge(masked_done, (T * b + t) * PER_BLOCK + j + 1)
                    dve.sem_inc(bank_taken[at(t, SCORES + j) % BANKS], 1)
                yield
                wait_bank(dve, b, at(t, UPDATE))
                if t < T - 1:
                    dve.tensor_tensor(update[:].rearrange("p (g n) -> p g n", g=BLOCKS),
                                      bank_of(at(t, UPDATE))[:].rearrange("p (g n) -> p g n", g=BLOCKS),
                                      own_head[:, None, :].broadcast_to([P, BLOCKS, P]), ALU.mult)\
                        .then_inc(update_done, 1)
                    dve.wait_ge(update_done, (T - 1) * b + t + 1)
                dve.sem_inc(bank_taken[at(t, UPDATE) % BANKS], 1)
                dve.wait_ge(attn_squared, T * b + t + 1)
                dve.sem_inc(bank_taken[at(t, MIXED) % BANKS], 1)
                yield
                wait_bank(dve, b, at(t, OUT))
                dve.tensor_scalar(attn_variance[:, t:t + 1], bank_of(at(t, OUT))[:, D:D + 1], 1.0 / D, RMS_EPS,
                                  ALU.mult, ALU.add).then_inc(attn_variance_done, 1)
                dve.wait_ge(attn_inverse_done, T * b + t + 1)
                link(dve.scalar_tensor_tensor(x1[:, t], bank_of(at(t, OUT))[:, 0:D], attn_inverse[:, t:t + 1],
                                              x2[:, t], ALU.mult, ALU.add))
                dve.sem_inc(bank_taken[at(t, OUT) % BANKS], 1)
                if t == T - 1:
                    statistics(chain, x1, stats_done)
                    dve.wait_ge(inverse_done, 3 * b + 3)
                    normalise(x1, x1, x3_done)
                yield
            for c in range(KC):
                dve.wait_ge(x3t_high, KC * b + c + 1)
                link(dve.tensor_tensor(x3t[LO][:, c], bank_of(X3T + c)[:], x3t[HI][:, c].bitcast(F32), ALU.subtract))
                dve.sem_inc(bank_taken[(X3T + c) % BANKS], 1)
                dve.sem_inc(x3t_split, 1)
            chain.close()

        def experts(b):
            chain = Chain(back_chain, b * BACK_LINKS, BACK_LINKS)
            link = chain.link
            dve.wait_ge(gate_ready, MOE_USES * b + GATE_LOGITS + 1)
            link(dve.tensor_copy(logits[:].rearrange("p t n -> p (t n)"), gate_bank[:, 0:T * ROUTER]))
            dve.sem_inc(gate_taken, 1)
            level = logits[:, :, 0:EXPERTS]
            equal, rank, chosen1, rest, chosen2 = (pick[:, i] for i in range(5))
            m1, m2, first, gap, ratio, gate_exp, w1, w2 = (best[:, i] for i in range(8))

            def wide(x):
                return x[:, :, None].broadcast_to([P, T, EXPERTS])

            for source, top, chosen in ((level, m1, chosen1), (rest, m2, chosen2)):
                link(dve.tensor_reduce(top, source, AX.X, ALU.max))
                link(dve.tensor_tensor(equal, source, wide(top), ALU.is_equal))
                link(dve.tensor_tensor(rank, equal, descending[:], ALU.mult))
                link(dve.tensor_reduce(first, rank, AX.X, ALU.max))
                link(dve.tensor_tensor(chosen, descending[:], wide(first), ALU.is_equal))
                if chosen is chosen1:
                    link(dve.tensor_scalar(equal, chosen, -MASKED, None, ALU.mult))
                    link(dve.tensor_tensor(rest, equal, level, ALU.add))
            dve.tensor_tensor(gap, m2, m1, ALU.subtract).then_inc(gap_done, 1)
            dve.wait_ge(exp_done, b + 1)
            link(dve.tensor_scalar(first, ratio, 1.0, None, ALU.add))
            link(dve.reciprocal(w1, first))
            link(dve.tensor_scalar(w1, w1, 0.5, None, ALU.mult))
            link(dve.tensor_tensor(w2, w1, ratio, ALU.mult))
            link(dve.tensor_tensor(equal, chosen1, wide(w1), ALU.mult))
            link(dve.tensor_tensor(rank, chosen2, wide(w2), ALU.mult))
            link(dve.tensor_scalar(first, gate_exp, 1.0, None, ALU.add))
            link(dve.reciprocal(gap, first))
            dve.tensor_scalar(mix[:, :, EXPERTS], gap, 0.5, None, ALU.mult)
            dve.tensor_tensor(mix[:, :, 0:EXPERTS], equal, rank, ALU.add).then_inc(mix_done, 1)
            yield

            def activated(c):
                h = hidden[c % SLOTS][:]
                dve.wait_ge(tanh_gate, CHUNKS * b + c + 1)
                link(dve.scalar_tensor_tensor(h, h, 1.0, gate_bank[:], ALU.add, ALU.mult))
                dve.sem_inc(gate_taken, 1)

            def product(c):
                h = hidden[c % SLOTS][:]
                dve.wait_ge(up_ready, MOE_USES * b + up_use(c) + 1)
                link(dve.tensor_tensor(h, up_bank[:], h, ALU.mult))
                dve.sem_inc(up_taken, 1)
                dve.sem_inc(product_done, 1)

            def low(c):
                dve.wait_ge(hidden_high, CHUNKS * b + c + 1)
                dve.tensor_tensor(hidden_split[c % SLOTS][LO][:], hidden[c % SLOTS][:],
                                  hidden_split[c % SLOTS][HI][:].bitcast(F32), ALU.subtract).then_inc(hidden_low, 1)

            activated(0)
            yield
            product(0)
            yield
            dve.wait_ge(up_ready, MOE_USES * b + UP_MIX + 1)
            dve.tensor_copy(mix_t[:], up_bank[0:EXPERTS + 1, :]).then_inc(mix_t_done, 1)
            dve.wait_ge(mix_t_done, b + 1)
            dve.sem_inc(up_taken, 1)
            yield
            dve.wait_ge(up_ready, MOE_USES * b + UP_SHARE + 1)
            link(dve.tensor_copy(share[1][:], up_bank[:]))
            dve.sem_inc(up_taken, 1)
            dve.wait_ge(share_done, 2 * b + 1)
            dve.sem_inc(gate_taken, 1)
            dve.sem_inc(share_done, 1)
            yield
            for c in range(1, CHUNKS):
                activated(c)
                if c == 1:
                    low(0)
                yield
                product(c)
                yield
                low(c)
                yield
            dve.wait_ge(down_done, CHUNKS * b + CHUNKS)
            dve.wait_ge(result_out, 16 * b + RESULT_FREE)
            for half in range(2):
                part = slice(2 * half, 2 * half + 2)
                last = dve.tensor_tensor(total[:, part], out[half][:], x3[:, part], ALU.add)
            link(last)
            dve.sem_inc(moe_done, 1)
            statistics(chain, total, final_stats)
            dve.wait_ge(final_inverse, b + 1)
            normalise(total, total, result_ready)
            chain.close()

        alone(layers(0))
        with dve.Fori(0, batches - 1) as b:
            interleave(layers(b + 1), experts(b))
        alone(experts(batches - 1))


def two_block_kernel(nc, x_tokens, x_t, w_heads, slopes, *rest):
    result = rest[-1]
    weights = dict(zip(WEIGHTS, rest))
    tables = dict(zip(TABLES, rest[len(WEIGHTS):]))
    batches = result.shape[0]
    y_scratch = nc.dram_tensor("y_scratch", (batches, S, D), F32, kind="Internal").ap()
    softmax_attention(nc, x_tokens, x_t, w_heads, slopes, y_scratch)
    block_one(nc, y_scratch, weights, tables, result)


WEIGHTS = ("gate_up", "down", "qkv", "router", "ffn_w", "ffn_scale", "wo", "rms_w")
TABLES = ("cos", "sin", "decay", "q_decay", "k_decay", "own_head", "chunk_decay", "spread", "ident",
          "descending", "power")


def alibi_slopes(heads):
    return [2.0 ** (-8.0 * (h + 1) / heads) for h in range(heads)]


def shape_tables():
    f32 = np.float32
    slopes = np.array(alibi_slopes(H1), f32)
    r = np.exp(-slopes)
    freq = (f32(1.0 / 1024.0) ** np.linspace(0.0, 1.0, E1 // 4, dtype=f32)).astype(f32)
    freq = np.concatenate([freq, np.zeros(E1 // 4, f32)])
    theta = np.arange(S, dtype=f32)[:, None] * freq[None, :]
    cos = np.concatenate([np.cos(theta)] * 2, axis=1)
    sin = np.concatenate([np.sin(theta), -np.sin(theta)], axis=1)

    def tiles(a):
        return a.reshape(T, P, -1).transpose(1, 0, 2)

    i = np.arange(P, dtype=f32)
    diff = i[None, :] - i[:, None]
    by_head = np.where(diff >= 0, r[:, None, None] ** np.maximum(diff, 0), 0)
    decay = by_head.reshape(BLOCKS, PER_BLOCK, P, P).transpose(2, 1, 0, 3).reshape(P, PER_BLOCK, BLOCKS * P)
    row = np.arange(P)
    own = (row[:, None] // PAD == row[None, :] // PAD) & ((row % PAD < E1)[:, None] & (row % PAD < E1)[None, :])
    row_r = np.repeat(r.reshape(BLOCKS, PER_BLOCK), PAD, axis=1).T
    spread = np.zeros((P, 2, P), f32)
    for e in range(EXPERTS):
        spread[e, 0, e * ROWS:(e + 1) * ROWS] = 1.0
    spread[EXPERTS, 1] = 1.0
    tables = dict(
        cos=tiles(cos), sin=tiles(sin), decay=decay,
        q_decay=(row_r[:, :, None] ** (i[None, None, :] + 1)).reshape(P, BLOCKS * P),
        k_decay=r[None, :] ** (P - 1 - i[:, None]),
        own_head=own, chunk_decay=row_r ** f32(P),
        spread=spread, ident=np.eye(P),
        descending=np.broadcast_to(EXPERTS - np.arange(EXPERTS), (P, T, EXPERTS)),
        power=np.broadcast_to(np.array([-0.5, 0.5])[None, :, None], (P, 2, T)))
    return [np.ascontiguousarray(tables[x], dtype=f32) for x in TABLES]


def by_row(a):
    return a.reshape(KC, P, -1).transpose(1, 0, 2)


def by_head(a):
    padded = np.zeros((H1, PAD, a.shape[1]), a.dtype)
    padded[:, :E1] = a.reshape(H1, E1, -1)
    return padded.reshape(BLOCKS, P, -1).transpose(1, 0, 2)


def pack_attention(Wq, Wk, Wv, Wo):
    qkv = [w.reshape(H0, DH, KC, P).transpose(0, 3, 2, 1).reshape(H0, P, KC * DH) for w in (Wq, Wk, Wv)]
    return np.concatenate(qkv + [Wo.reshape(D, H0, DH).transpose(1, 2, 0)], axis=2)


def pack_experts(gate_up_proj, down_proj, sh_gate_w, sh_up_w, sh_down_w):
    def chunks(experts, shared):
        n = shared.shape[1]
        e = experts.reshape(EXPERTS, E_CHUNKS, ROWS, n).transpose(1, 0, 2, 3).reshape(E_CHUNKS, P, n)
        s = np.zeros((S_CHUNKS * P, n), shared.dtype)
        s[:I_SHARED] = shared
        s = iter(s.reshape(S_CHUNKS, P, n))
        e = iter(e)
        return np.stack([next(s if x else e) for x in SHARED])

    gate = chunks(gate_up_proj[:, :I_MOE], sh_gate_w)
    up = chunks(gate_up_proj[:, I_MOE:], sh_up_w)
    both = np.stack([gate, up], axis=1).reshape(CHUNKS, 2, P, KC, P)
    return both.transpose(0, 4, 1, 3, 2), chunks(down_proj.transpose(0, 2, 1), sh_down_w.T)


def kernel(**inputs):
    import concourse.bacc as bacc
    from concourse.bass_utils import run_bass_kernel_spmd

    a = {k: np.asarray(v) for k, v in inputs.items()}
    x = a["L0_attn_resid_pre"]
    batches = x.shape[0]
    padded = np.concatenate([x, x[:1]])
    gate_up, down = pack_experts(*(a["L1_ffn_" + n] for n in
                                   ("gate_up_proj", "down_proj", "sh_gate_w", "sh_up_w", "sh_down_w")))
    router = np.concatenate([a["L1_ffn_router_weight"].T, a["L1_ffn_shared_gate_w"].T,
                             np.zeros((D, 1), np.float32)], axis=1)
    arrays = [
        padded,
        padded.reshape(batches + 1, S, KC, P).transpose(0, 3, 2, 1),
        pack_attention(*(a["L0_attn_" + n] for n in ("Wq", "Wk", "Wv", "Wo"))),
        np.broadcast_to(np.array(alibi_slopes(H0), np.float32), (P, H0)),
        gate_up, down,
        by_row(np.concatenate([a["L1_attn_Wq"], a["L1_attn_Wk"], a["L1_attn_Wv"]], axis=1)),
        by_row(router),
        by_row(a["L0_ffn_weight"]),
        np.broadcast_to(a["L0_ffn_scale"], (P, D)),
        by_head(a["L1_attn_Wo"]),
        by_head(a["L1_attn_rms_w"][:, None])[:, :, 0],
    ] + shape_tables()
    names = ["x_tokens", "x_t", "w_heads", "slopes", *WEIGHTS, *TABLES]
    arrays = {f"in_{n}": np.ascontiguousarray(v) for n, v in zip(names, arrays)}
    nc = bacc.Bacc("TRN2", target_bir_lowering=False, num_devices=1)
    args = [nc.dram_tensor(n, v.shape, F32, kind="ExternalInput").ap() for n, v in arrays.items()]
    result = nc.dram_tensor("out_result", (batches, S, D), F32, kind="ExternalOutput").ap()
    two_block_kernel(nc, *args, result)
    run = run_bass_kernel_spmd(nc, [arrays], core_ids=[0])
    return run.results[0]["out_result"]
```

```python
from contextlib import ExitStack

import numpy as np

import concourse.bass as bass
from concourse import mybir

F32 = mybir.dt.float32
F32R = mybir.dt.float32r
ALU = mybir.AluOpType
ACT = mybir.ActivationFunctionType
AX = mybir.AxisListType

P = 128
D = 256
KC = D // P
S = 512
T = S // P

H0 = 16
DH = 128
PAIRS = H0 // 2
CLIP = 1024.0
MASKED = 1e30
BIG = 3e38

PASSES = ((1, 0), (0, 1), (0, 0))
HI, LO = 0, 1


class Space:

    def __init__(self, nc, stack, prefix):
        self.nc, self.stack, self.prefix = nc, stack, prefix

    def sb(self, name, shape, dt=F32):
        return self.stack.enter_context(self.nc.sbuf_tensor(self.prefix + name, shape, dt))

    def ps(self, name, shape, dt=F32):
        return self.stack.enter_context(self.nc.psum_tensor(self.prefix + name, shape, dt))

    def sem(self, name):
        return self.stack.enter_context(self.nc.semaphore(self.prefix + name))


def softmax_attention(nc, x_tokens, x_t, w_heads, slopes, y_scratch):
    batches = x_tokens.shape[0] - 1
    with ExitStack() as stack:
        m = Space(nc, stack, "attention_")
        w_qk = m.sb("w_qk", [P, H0 * 2 * 2 * KC * DH], F32R)
        w_v = [m.sb(f"w_v_{x}", [P, KC, H0 * DH], F32R) for x in ("hi", "lo")]
        w_o = [m.sb(f"w_o_{x}", [P, H0 * D], F32R) for x in ("hi", "lo")]
        split_weights(nc, w_heads, w_qk, w_v, w_o)
        attend(nc, m, batches, x_tokens, x_t, slopes, y_scratch, w_qk, w_v, w_o)


def split_weights(nc, w_heads, w_qk, w_v, w_o):
    SLOTS = 4
    QK, V, O = 2 * KC * DH, KC * DH, D
    with ExitStack() as stack:
        m = Space(nc, stack, "attention_split_")
        raw = [m.sb(f"raw_{i}", [P, QK + V + O]) for i in range(SLOTS)]
        loaded = [m.sem(f"raw_loaded_{i}") for i in range(SLOTS)]
        high_done = m.sem("w_high_done")
        low_done = m.sem("w_low_done")
        block = stack.enter_context(nc.Block())

        def parts(h, part):
            yield w_qk[:, (2 * h + part) * QK:(2 * h + part + 1) * QK], 0, QK
            yield w_v[part][:, :, h * DH:(h + 1) * DH], QK, V
            yield w_o[part][:, h * O:(h + 1) * O], QK + V, O

        def piece(i, at, n):
            r = raw[i][:, at:at + n]
            return r.rearrange("p (c n) -> p c n", c=KC) if n == V and at == QK else r

        @block.sync
        def _(sp):
            for h in range(H0):
                if h >= SLOTS:
                    sp.wait_ge(low_done, h - SLOTS + 1)
                sp.dma_start(raw[h % SLOTS][:], w_heads[h]).then_inc(loaded[h % SLOTS], 16)

        @block.scalar
        def _(act):
            for h in range(H0):
                act.wait_ge(loaded[h % SLOTS], 16 * (h // SLOTS + 1))
                for n, (dst, at, size) in enumerate(parts(h, HI)):
                    last = act.activation(dst, piece(h % SLOTS, at, size), ACT.Copy)
                last.then_inc(high_done, 1)

        @block.vector
        def _(dve):
            for h in range(H0):
                dve.wait_ge(high_done, h + 1)
                for (dst, at, size), (high, _, _) in zip(parts(h, LO), parts(h, HI)):
                    last = dve.tensor_tensor(dst, piece(h % SLOTS, at, size), high.bitcast(F32), ALU.subtract)
                last.then_inc(low_done, 1)


def attend(nc, m, batches, x_tokens, x_t, slopes, y_scratch, w_qk, w_v, w_o):
    QK = 2 * KC * DH
    stage = [m.sb(f"w_stage_{s}", [P, 2, 2, KC, DH], F32R) for s in "ab"]
    xt_raw = m.sb("xt_raw", [P, KC, S])
    xt = [m.sb(f"xt_{x}", [P, KC, S], F32R) for x in ("hi", "lo")]
    y = m.sb("y_tokens", [P, T, D])
    q = [[m.sb(f"q_{s}_{x}", [P, S], F32R) for x in ("hi", "lo")] for s in "ab"]
    k = [[m.sb(f"k_{s}_{x}", [P, S], F32R) for x in ("hi", "lo")] for s in "ab"]
    v = [m.sb(f"v_{x}", [P, T, 2 * DH], F32R) for x in ("hi", "lo")]
    z = [m.sb(f"z_{x}", [P, S], F32R) for x in ("hi", "lo")]
    pt = [m.sb(f"probs_t_{x}", [P, T, S], F32R) for x in ("hi", "lo")]
    WIDTH = [(t + 1) * P for t in range(T)]
    AT = [sum(WIDTH[:t]) for t in range(T)]
    probs = m.sb("probs", [P, sum(WIDTH)])
    distance = m.sb("distance", [P, S])
    bias = [m.sb(f"bias_{s}", [P, S]) for s in "ab"]
    slope = m.sb("slope", [P, H0])
    ident = m.sb("ident", [P, P])
    count = bias[0][:].bitcast(mybir.dt.int32)
    zeros = m.sb("zeros", [P, 2], F32R)
    low = m.sb("lowest", [P, 2 * T])
    total = m.sb("total", [P, 2 * T])
    inverse = m.sb("inverse", [P, 2 * T])
    scores = [m.ps(f"scores_{i}", [P, S]) for i in range(2)]
    turned = [m.ps(f"turned_{i}", [P, S]) for i in range(2)]
    proj = [m.ps(f"proj_{i}", [P, S]) for i in range(2)]
    out = [m.ps(f"out_{i}", [P, 2, D]) for i in range(2)]

    consts = m.sem("consts")
    stage_in = [m.sem(f"stage_{s}_in") for s in "ab"]
    xt_in, x_in = m.sem("xt_in"), m.sem("x_in")
    xt_high, xt_split = m.sem("xt_high"), m.sem("xt_split")
    proj_ready, proj_high, proj_low = m.sem("proj_ready"), m.sem("proj_high"), m.sem("proj_low")
    scores_ready, scores_clipped = m.sem("scores_ready"), m.sem("scores_clipped")
    biased, exp_done, inverse_done = m.sem("biased"), m.sem("exp_done"), m.sem("inverse_done")
    dve_passed, pool_passed = m.sem("dve_passed"), m.sem("pool_passed")
    bias_ready, probs_ready = m.sem("bias_ready"), m.sem("probs_ready")
    turned_ready, turned_high, turned_low = m.sem("turned_ready"), m.sem("turned_high"), m.sem("turned_low")
    out_ready, y_ready, y_stored = m.sem("out_ready"), m.sem("y_ready"), m.sem("y_stored")

    STEP = 8
    Q_B, K_B, V_0, V_1, Z_A, Q_A, K_A, Z_B = range(STEP)
    AHEAD = 2
    FREE = 2
    HEAD_UNIT = STEP // 2

    block = m.stack.enter_context(nc.Block())

    def numbers(eng, b, i):
        return eng.snap(b * (PAIRS * STEP) + i * STEP)

    @block.sync
    def _(sp):
        def weights(head):
            return w_qk[:, bass.ds(head * (2 * QK), 2 * QK)]

        def load_stage(slot, src):
            dst = stage[slot][:].rearrange("p a b c d -> p (a b c d)")
            sp.dma_start(dst.bitcast(F32), src.bitcast(F32)).then_inc(stage_in[slot], 16)

        def tokens(dram):
            return dram.rearrange("(t p) d -> p t d", p=P)

        sp.dma_start(xt_raw[:], x_t[0]).then_inc(xt_in, 16)
        load_stage(0, weights(0))
        load_stage(1, weights(1))
        sp.dma_start(slope[:], slopes).then_inc(consts, 16)
        sp.sem_inc(y_stored, 1)

        def step(n, next_a, next_b):
            sp.wait_ge(proj_ready, n + 2)
            load_stage(0, weights(next_a))
            sp.wait_ge(proj_ready, n + AHEAD + K_B + 1)
            load_stage(1, weights(next_b))

        with sp.Fori(0, batches) as b:
            sp.wait_ge(xt_split, b + 1)
            sp.dma_start(xt_raw[:], x_t[b + 1]).then_inc(xt_in, 16)
            step(numbers(sp, b, 0), 2, 3)
            sp.wait_ge(y_stored, 16 * b + 1)
            sp.dma_start(y[:], tokens(x_tokens[b])).then_inc(x_in, 16)
            with sp.Fori(1, PAIRS - 1) as i:
                step(numbers(sp, b, i), 2 * i + 2, 2 * i + 3)
            step(numbers(sp, b, PAIRS - 1), 0, 1)
            sp.wait_ge(y_ready, b + 2)
            sp.dma_start(tokens(y_scratch[b]), y[:]).then_inc(y_stored, 16)
        sp.wait_ge(y_stored, 16 * batches + 1)
        sp.wait_ge(xt_in, 16 * (batches + 1))
        for s in range(2):
            sp.wait_ge(stage_in[s], 16 * (batches * PAIRS + 1))

    @block.gpsimd
    def _(pool):
        pool.memset(ident[:], 0.0).then_inc(consts, 1)
        pool.memset(zeros[:].bitcast(F32), 0.0).then_inc(consts, 1)
        pool.iota(count[:], pattern=[[-1, S]], base=S - P, channel_multiplier=0).then_inc(consts, 1)
        pool.wait_ge(consts, 16 + 3)
        pool.affine_select(ident[:], ident[:], compare_op=ALU.not_equal, fill=1.0, base=0,
                           pattern=[[-1, P]], channel_multiplier=1).then_inc(consts, 1)
        pool.tensor_copy(distance[:], count[:]).then_inc(consts, 1)
        pool.wait_ge(consts, 16 + 5)
        pool.affine_select(distance[:], distance[:], compare_op=ALU.is_ge, fill=MASKED, base=S - P,
                           pattern=[[-1, S]], channel_multiplier=1).then_inc(consts, 1)
        pool.wait_ge(consts, 16 + 6)

        def head_bias(slot, head):
            s = slope[:, bass.ds(head, 1)].broadcast_to([P, S])
            pool.tensor_tensor(bias[slot][:], distance[:], s, ALU.mult).then_inc(bias_ready, HEAD_UNIT)

        def normalise(tile, slot):
            for t in range(T):
                pool.wait_ge(inverse_done, tile + t + 1)
                pool.sem_inc(pool_passed, 1)
                p = probs[:, AT[t]:AT[t] + WIDTH[t]]
                pool.tensor_scalar(p, p, inverse[:, slot * T + t:slot * T + t + 1], 1.0,
                                   ALU.mult, ALU.mult).then_inc(probs_ready, 1)

        head_bias(0, 0)
        head_bias(1, 1)
        normalise(0, 0)

        def step(n, next_a, next_b):
            pool.wait_ge(biased, n + T)
            head_bias(0, next_a)
            normalise(n + T, 1)
            pool.wait_ge(biased, n + 2 * T)
            head_bias(1, next_b)
            normalise(n + 2 * T, 0)

        with pool.Fori(0, batches) as b:
            with pool.Fori(0, PAIRS - 1) as i:
                step(numbers(pool, b, i), 2 * i + 2, 2 * i + 3)
            step(numbers(pool, b, PAIRS - 1), 0, 1)

    @block.tensor
    def _(pe):
        def projection(unit, slot, which):
            for n, (a, b) in enumerate((p, c) for c in range(KC) for p in PASSES):
                last = pe.matmul(proj[unit % 2][:], stage[slot][:, a[0], which, b], xt[a[1]][:, b],
                                 start=(n == 0), stop=(n == 3 * KC - 1))
            last.then_inc(proj_ready, 1)

        def values(half, col):
            for t in range(2):
                at = (2 * half + t) * P
                for n, (a, c) in enumerate((p, c) for c in range(KC) for p in PASSES):
                    last = pe.matmul(proj[half][:, t * 2 * DH:(t + 1) * 2 * DH], xt[a[0]][:, c, at:at + P],
                                     w_v[a[1]][:, c, bass.ds(col, 2 * DH)],
                                     start=(n == 0), stop=(n == 3 * KC - 1))
            last.then_inc(proj_ready, 1)

        def score_tile(slot, t):
            for n, a in enumerate(PASSES):
                last = pe.matmul(scores[t % 2][:, 0:WIDTH[t]], q[slot][a[0]][:, t * P:(t + 1) * P],
                                 k[slot][a[1]][:, 0:WIDTH[t]], start=(n == 0), stop=(n == 2))
            last.then_inc(scores_ready, 1)

        def turn(tile, tiles=range(T)):
            for t in tiles:
                pe.wait_ge(probs_ready, tile + t + 1)
                pe.wait_ge(turned_low, tile + t - 1 + FREE)
                for c in range(t + 1):
                    last = pe.transpose(turned[t % 2][:, c * P:(c + 1) * P],
                                        probs[:, AT[t] + c * P:AT[t] + (c + 1) * P], ident[:])
                last.then_inc(turned_ready, 1)

        def attended(unit, slot, number):
            for c in range(T):
                if unit == Z_A and c % 2 == 0:
                    pe.wait_ge(proj_low, number + AHEAD + (V_0 if c == 0 else V_1) + 1)
                for n, a in enumerate(PASSES):
                    last = pe.matmul(proj[unit % 2][:, c * P:S], v[a[0]][:, c, slot * DH:(slot + 1) * DH],
                                     pt[a[1]][:, c, c * P:S], start=(c == 0 and n == 0),
                                     stop=(c == T - 1 and n == 2))
            last.then_inc(proj_ready, 1)

        def project_out(col, tiles=range(T)):
            for t in tiles:
                for a in PASSES:
                    last = pe.matmul(out[t // 2][:, t % 2], z[a[0]][:, t * P:(t + 1) * P],
                                     w_o[a[1]][:, bass.ds(col, D)], start=False, stop=False,
                                     skip_group_check=True)
            return last

        def clear_out():
            for bank in out:
                pe.matmul(bank[:, 0, 0:2], w_qk[:, 0:P], zeros[:], start=True, stop=True,
                          skip_group_check=True)

        def free_bank(n, unit):
            pe.wait_ge(proj_low, n + AHEAD + unit - 1)

        pe.wait_ge(consts, 16 + 6)
        pe.wait_ge(xt_split, 1)
        pe.wait_ge(stage_in[0], 16)
        projection(0, 0, 0)
        projection(1, 0, 1)
        pe.wait_ge(proj_low, 2)
        for t in range(T):
            if t >= 2:
                pe.wait_ge(scores_clipped, t - 1)
            score_tile(0, t)
        turn(0, (0, 1))

        def step(b, n, i, first_pair=False, last_pair=False):
            def scores_of(slot, tile, tiles):
                for t in tiles:
                    pe.wait_ge(scores_clipped, tile + t - 1)
                    score_tile(slot, t)

            pe.wait_ge(stage_in[1], 2 * n + 16)
            for unit, which in ((Q_B, 0), (K_B, 1)):
                free_bank(n, unit)
                projection(unit, 1, which)
            turn(n, (2,))
            free_bank(n, V_0)
            values(0, i * (2 * DH))
            turn(n, (3,))
            free_bank(n, V_1)
            values(1, i * (2 * DH))
            pe.wait_ge(proj_low, n + AHEAD + K_B + 1)
            scores_of(1, n + T, (0, 1))
            free_bank(n, Z_A)
            pe.wait_ge(turned_low, n + T + FREE)
            attended(Z_A, 0, n)
            scores_of(1, n + T, (2, 3))
            turn(n + T, (0, 1))
            if first_pair:
                pe.wait_ge(y_ready, b + 1)
                clear_out()
            pe.wait_ge(stage_in[0], 2 * n + 32)
            if last_pair:
                pe.wait_ge(xt_split, b + 2)
            for unit, which in ((Q_A, 0), (K_A, 1)):
                free_bank(n, unit)
                projection(unit, 0, which)
            pe.wait_ge(proj_low, n + AHEAD + Z_A + 1)
            project_out(i * (2 * D), (0, 1))
            turn(n + T, (2, 3))
            project_out(i * (2 * D), (2, 3))
            pe.wait_ge(proj_low, n + AHEAD + K_A + 1)
            scores_of(0, n + 2 * T, (0, 1))
            free_bank(n, Z_B)
            pe.wait_ge(turned_low, n + 2 * T + FREE)
            attended(Z_B, 1, n)
            scores_of(0, n + 2 * T, (2, 3))
            turn(n + 2 * T, (0, 1))
            pe.wait_ge(proj_low, n + AHEAD + Z_B + 1)
            last = project_out(i * (2 * D) + D)
            if last_pair:
                last.then_inc(out_ready, 1)

        with pe.Fori(0, batches) as b:
            step(b, numbers(pe, b, 0), 0, first_pair=True)
            with pe.Fori(1, PAIRS - 1) as i:
                step(b, numbers(pe, b, i), i)
            step(b, numbers(pe, b, PAIRS - 1), PAIRS - 1, last_pair=True)

    NEGATIVE_SCALE = -1.0 / DH ** 0.5

    def unit_target(number, unit):
        bank = proj[number % 2][:]
        if unit in (V_0, V_1):
            t = 2 * (unit - V_0)
            return bank.rearrange("p (t n) -> p t n", t=2), [x[:, t:t + 2] for x in v], 1.0
        if unit in (Q_A, Q_B):
            return bank, [x[:] for x in q[unit == Q_B]], NEGATIVE_SCALE
        if unit in (K_A, K_B):
            return bank, [x[:] for x in k[unit == K_B]], 1.0
        return bank, [x[:] for x in z], 1.0

    @block.scalar
    def _(act):
        def split_x(b):
            act.wait_ge(xt_in, 16 * b + 16)
            act.activation(xt[HI][:], xt_raw[:], ACT.Copy).then_inc(xt_high, 1)

        def unit_high(number, unit, before=0):
            bank, dst, scale = unit_target(number, unit)
            act.wait_ge(proj_ready, before + number + 1)
            act.activation(dst[HI], bank, ACT.Copy, scale=scale).then_inc(proj_high, 1)

        def exponentials(tile, slot, t):
            act.wait_ge(biased, tile + t + 1)
            p = probs[:, AT[t]:AT[t] + WIDTH[t]]
            c = slot * T + t
            act.activation(p, p, ACT.Exp, bias=low[:, c:c + 1], scale=-1.0,
                           accum_out=total[:, c:c + 1]).then_inc(exp_done, 1)

        def turned_to_high(tile, tiles):
            for t in tiles:
                act.wait_ge(turned_ready, tile + t + 1)
                act.activation(pt[HI][:, 0:t + 1, t * P:(t + 1) * P],
                               turned[t % 2][:, 0:WIDTH[t]].rearrange("p (c n) -> p c n", c=t + 1),
                               ACT.Copy).then_inc(turned_high, 1)

        split_x(0)
        for number, unit in enumerate((Q_A, K_A)):
            unit_high(number, unit)
        exponentials(0, 0, 0)
        exponentials(0, 0, 1)
        turned_to_high(0, (0, 1))
        exponentials(0, 0, 2)
        exponentials(0, 0, 3)

        def step(b, n, last_pair):
            unit_high(AHEAD + Q_B, Q_B, n)
            unit_high(AHEAD + K_B, K_B, n)
            turned_to_high(n, (2,))
            unit_high(AHEAD + V_0, V_0, n)
            turned_to_high(n, (3,))
            unit_high(AHEAD + V_1, V_1, n)
            if last_pair:
                split_x(b + 1)
            exponentials(n + T, 1, 0)
            exponentials(n + T, 1, 1)
            unit_high(AHEAD + Z_A, Z_A, n)
            turned_to_high(n + T, (0, 1))
            exponentials(n + T, 1, 2)
            exponentials(n + T, 1, 3)
            unit_high(AHEAD + Q_A, Q_A, n)
            unit_high(AHEAD + K_A, K_A, n)
            turned_to_high(n + T, (2, 3))
            exponentials(n + 2 * T, 0, 0)
            exponentials(n + 2 * T, 0, 1)
            unit_high(AHEAD + Z_B, Z_B, n)
            turned_to_high(n + 2 * T, (0, 1))
            exponentials(n + 2 * T, 0, 2)
            exponentials(n + 2 * T, 0, 3)

        with act.Fori(0, batches) as b:
            with act.Fori(0, PAIRS - 1) as i:
                step(b, numbers(act, b, i), False)
            step(b, numbers(act, b, PAIRS - 1), True)

    @block.vector
    def _(dve):
        def split_x(b):
            dve.wait_ge(xt_high, b + 1)
            dve.tensor_tensor(xt[LO][:], xt_raw[:], xt[HI][:].bitcast(F32), ALU.subtract).then_inc(xt_split, 1)

        def unit_low(number, unit, before=0):
            bank, dst, scale = unit_target(number, unit)
            dve.wait_ge(proj_high, before + number + 1)
            high = dst[HI].bitcast(F32)
            if scale == 1.0:
                dve.tensor_tensor(dst[LO], bank, high, ALU.subtract).then_inc(proj_low, 1)
            else:
                dve.scalar_tensor_tensor(dst[LO], bank, scale, high, ALU.mult, ALU.subtract).then_inc(proj_low, 1)

        def clip(tile, t, first=False):
            dve.wait_ge(scores_ready, tile + t + 1)
            if not first:
                dve.wait_ge(turned_ready, tile + t - T + 1)
            dve.tensor_scalar(probs[:, AT[t]:AT[t] + WIDTH[t]], scores[t % 2][:, 0:WIDTH[t]], CLIP, -CLIP,
                              ALU.min, ALU.max).then_inc(scores_clipped, 1)

        def add_bias(tile, slot, t, biases):
            if t == 0:
                dve.wait_ge(bias_ready, biases)
            dve.wait_ge(scores_clipped, tile + t + 1)
            dve.sem_inc(dve_passed, 1)
            p = probs[:, AT[t]:AT[t] + WIDTH[t]]
            c = slot * T + t
            dve.tensor_tensor_reduce(p, p, bias[slot][:, S - WIDTH[t]:S], 1.0, BIG, ALU.add, ALU.min,
                                     low[:, c:c + 1]).then_inc(biased, 1)

        def invert(tile, slot, t):
            dve.wait_ge(exp_done, tile + t + 1)
            c = slot * T + t
            dve.reciprocal(inverse[:, c:c + 1], total[:, c:c + 1]).then_inc(inverse_done, 1)

        def turned_to_low(tile, tiles):
            for t in tiles:
                dve.wait_ge(turned_high, tile + t + 1)
                dst = [x[:, 0:t + 1, t * P:(t + 1) * P] for x in pt]
                dve.tensor_tensor(dst[LO], turned[t % 2][:, 0:WIDTH[t]].rearrange("p (c n) -> p c n", c=t + 1),
                                  dst[HI].bitcast(F32), ALU.subtract).then_inc(turned_low, 1)

        def softmax(tile, slot, biases, between, first=False):
            clip(tile, 0, first)
            clip(tile, 1, first)
            add_bias(tile, slot, 0, biases)
            add_bias(tile, slot, 1, biases)
            invert(tile, slot, 0)
            invert(tile, slot, 1)
            between[0]()
            clip(tile, 2, first)
            clip(tile, 3, first)
            add_bias(tile, slot, 2, biases)
            add_bias(tile, slot, 3, biases)
            turned_to_low(tile, (0, 1))
            invert(tile, slot, 2)
            invert(tile, slot, 3)
            between[1]()
            between[2]()

        def nothing():
            pass

        dve.engine_nop().then_inc(turned_low, FREE)
        dve.sem_inc(y_ready, 1)
        split_x(0)
        for number, unit in enumerate((Q_A, K_A)):
            unit_low(number, unit)
        softmax(0, 0, HEAD_UNIT, (nothing, nothing, nothing), first=True)

        def step(b, n, last_pair):
            unit_low(AHEAD + Q_B, Q_B, n)
            unit_low(AHEAD + K_B, K_B, n)
            turned_to_low(n, (2,))
            unit_low(AHEAD + V_0, V_0, n)
            turned_to_low(n, (3,))
            unit_low(AHEAD + V_1, V_1, n)
            if last_pair:
                split_x(b + 1)
            softmax(n + T, 1, n + 2 * HEAD_UNIT, (lambda: unit_low(AHEAD + Z_A, Z_A, n),
                                                  lambda: unit_low(AHEAD + Q_A, Q_A, n),
                                                  lambda: unit_low(AHEAD + K_A, K_A, n)))
            turned_to_low(n + T, (2, 3))
            softmax(n + 2 * T, 0, n + 3 * HEAD_UNIT, (lambda: unit_low(AHEAD + Z_B, Z_B, n), nothing, nothing))

        with dve.Fori(0, batches) as b:
            with dve.Fori(0, PAIRS - 1) as i:
                step(b, numbers(dve, b, i), False)
            step(b, numbers(dve, b, PAIRS - 1), True)
            dve.wait_ge(x_in, 16 * b + 16)
            dve.wait_ge(out_ready, b + 1)
            for half in range(2):
                part = y[:, 2 * half:2 * half + 2]
                last = dve.tensor_tensor(part, out[half][:], part, ALU.add)
            last.then_inc(y_ready, 1)


H1 = 16
E1 = D // H1
PAD = 32
BLOCKS = H1 * PAD // P
PER_BLOCK = H1 // BLOCKS
LN_EPS, RMS_EPS, NORM_EPS = 1e-5, 1e-5, 1e-7
MAX_NORM = 0.99
EXPERTS = 8
I_MOE, I_SHARED = 176, 704
ROWS = P // EXPERTS
E_CHUNKS = I_MOE // ROWS
S_CHUNKS = -(-I_SHARED // P)
CHUNKS = E_CHUNKS + S_CHUNKS
SHARED = [c % 3 == 0 for c in range(CHUNKS)]
assert sum(SHARED) == S_CHUNKS
REST = I_SHARED % P
ROUTER = EXPERTS + 1
LOGIT_ROWS = slice(REST, REST + 32)
assert REST % 32 == 0 and REST + 32 <= P
GU = 2 * KC * P


def block_one(nc, y_scratch, weights, tables, result):
    with ExitStack() as stack:
        m = Space(nc, stack, "block_one_")
        resident = dict(
            gate_up=[m.sb(f"gate_up_{x}", [P, CHUNKS, 2, KC, P], F32R) for x in ("hi", "lo")],
            down=[m.sb(f"down_{x}", [P, CHUNKS, D], F32R) for x in ("hi", "lo")],
            qkv=[m.sb(f"qkv_{x}", [P, KC, 3 * D], F32R) for x in ("hi", "lo")],
        )
        block_one_layers(nc, m, y_scratch, weights, tables, resident, result)


def block_one_layers(nc, m, y_scratch, weights, tables, resident, result):
    batches = result.shape[0]
    gate_up, down, qkv = (resident[x] for x in ("gate_up", "down", "qkv"))
    ffn_w = m.sb("ffn_w", [P, KC, D])
    wo = m.sb("wo", [P, BLOCKS, D])
    rms_w = m.sb("rms_w", [P, BLOCKS])
    cos, sin = m.sb("cos", [P, T, E1]), m.sb("sin", [P, T, E1])
    decay = m.sb("decay", [P, PER_BLOCK, BLOCKS * P])
    q_decay = m.sb("q_decay", [P, BLOCKS * P])
    k_decay = m.sb("k_decay", [P, H1])
    own_head = m.sb("own_head", [P, P])
    chunk_decay = m.sb("chunk_decay", [P, BLOCKS])
    spread = m.sb("spread", [P, 2, P])
    ident = m.sb("ident", [P, P])
    descending = m.sb("descending", [P, T, EXPERTS])
    power = m.sb("power", [P, 2, T])
    x1 = m.sb("x1", [P, T, D])
    x2 = m.sb("x2", [P, T, D])
    x3 = m.sb("x3", [P, T, D])
    masked = m.sb("masked_scores", [P, PER_BLOCK, BLOCKS * P])
    x1t = masked[:, 0:KC]
    total = masked[:, KC:].rearrange("p a (b d) -> p (a b) d", d=D)
    x2_squares = total
    x2t = [m.sb(f"x2t_{x}", [P, KC, S], F32R) for x in ("hi", "lo")]
    x3t = [m.sb(f"x3t_{x}", [P, KC, S], F32R) for x in ("hi", "lo")]
    qk = m.sb("qk", [P, 2 * H1, E1])
    swapped = m.sb("swapped", [P, 2 * H1, E1])
    qk_pad = m.sb("qk_pad", [P, 2 * H1, PAD])
    kd_pad = m.sb("kd_pad", [P, H1, PAD])
    v_pad = m.sb("v_pad", [P, H1, PAD])
    qt, kt = m.sb("qt", [P, BLOCKS * P]), m.sb("kt", [P, BLOCKS * P])
    qt_decayed = kt
    attn_t = qt
    attn_t_squares = kt
    ffn_scale = masked[:, 0, 0:D]
    update = masked[:, 0]
    state = m.sb("state", [P, BLOCKS, P])
    ones = m.sb("ones", [P, 1])
    stats, moments = m.sb("stats", [P, T, 6]), m.sb("moments", [P, T, 2])
    variance, inverse = m.sb("variance", [P, T]), m.sb("inverse", [P, T])
    squares = m.sb("squares", [P, T])
    norm = m.sb("norm", [P, 8, T])
    attn_variance, attn_inverse = m.sb("attn_variance", [P, T]), m.sb("attn_inverse", [P, T])
    logits = m.sb("logits", [P, T, ROUTER])
    pick = m.sb("pick", [P, 5, T, EXPERTS])
    best = m.sb("best", [P, 8, T])
    mix = m.sb("mix", [P, T, EXPERTS + 1])
    transposed = m.sb("transposed", [P, S])
    mix_t, logits_t = transposed[0:EXPERTS + 1], transposed[LOGIT_ROWS]
    share = [m.sb(f"share_{x}", [P, S]) for x in ("experts", "shared")]
    SLOTS = 2
    hidden = [m.sb(f"hidden_{i}", [P, S]) for i in range(SLOTS)]
    hidden_split = [[m.sb(f"hidden_{x}_{i}", [P, S], F32R) for x in ("hi", "lo")] for i in range(SLOTS)]
    BANKS = 4
    bank = [m.ps(f"bank_{i}", [P, 512]) for i in range(BANKS)]
    gate_bank, up_bank = m.ps("gate_bank", [P, S]), m.ps("up_bank", [P, S])
    out = [m.ps(f"out_{i}", [P, 2, D]) for i in range(2)]

    first_loaded, loaded = m.sem("first_loaded"), m.sem("loaded")
    ffn_scaled, consts = m.sem("ffn_scaled"), m.sem("consts")
    raw_loaded = [m.sem(f"raw_{i}_loaded") for i in range(6)]
    weights_high, weights_low = m.sem("weights_high"), m.sem("weights_low")
    bank_ready = [m.sem(f"bank_{i}_ready") for i in range(BANKS)]
    bank_taken = [m.sem(f"bank_{i}_taken") for i in range(BANKS)]
    gate_ready, gate_taken = m.sem("gate_ready"), m.sem("gate_taken")
    up_ready, up_taken = m.sem("up_ready"), m.sem("up_taken")
    y_in, result_out = m.sem("y_in"), m.sem("result_out")
    stats_done, inverse_done = m.sem("stats_done"), m.sem("inverse_done")
    x1_done, x2_done, x3_done = m.sem("x1_done"), m.sem("x2_done"), m.sem("x3_done")
    x2t_high, x3t_high = m.sem("x2t_high"), m.sem("x3t_high")
    squares_done, norms_done, norm_floored, tanh_done = (
        m.sem(x) for x in ("squares_done", "norms_done", "norm_floored", "tanh_done"))
    swapped_done, rotated, kd_done = (m.sem(x) for x in ("swapped_done", "rotated", "kd_done"))
    state_ready, state_faded = m.sem("state_ready"), m.sem("state_faded")
    decayed_done, attn_t_done, attn_variance_done, attn_inverse_done = (
        m.sem(x) for x in ("decayed_done", "attn_t_done", "attn_variance_done", "attn_inverse_done"))
    logits_t_done = m.sem("logits_t_done")
    gap_done, tanh_mix, mix_done = (m.sem(x) for x in ("gap_done", "tanh_mix", "mix_done"))
    tanh_gate, weighted, hidden_high, hidden_low = (
        m.sem(x) for x in ("tanh_gate", "weighted", "hidden_high", "hidden_low"))
    x3_kept = m.sem("x3_kept")
    down_done, moe_done, result_ready = m.sem("down_done"), m.sem("moe_done"), m.sem("result_ready")
    front_chain, opening_chain, experts_chain = (m.sem(x) for x in ("front_chain", "opening_chain", "experts_chain"))
    pool_chain, final_chain = m.sem("pool_chain"), m.sem("final_chain")
    final_stats, final_inverse = m.sem("final_stats"), m.sem("final_inverse")
    dve_passed, pool_passed = m.sem("dve_passed"), m.sem("pool_passed")

    X1T, FFN, X2T = 0, 2, 4
    TILE = 6
    QK_, V_, QT, KT, SCORES, MIXED, UPDATE, OUT = 0, 1, 2, 3, 4, 8, 9, 10
    PER_TILE = 11
    X3T = TILE + T * PER_TILE
    USES = X3T + KC
    PER_BANK = USES // BANKS
    RESULT_FREE = 17
    assert USES % BANKS == 0

    def at(t, use):
        return TILE + t * PER_TILE + use

    def bank_of(use):
        return bank[use % BANKS]

    def wait_bank(eng, b, use):
        eng.wait_ge(bank_ready[use % BANKS], b * PER_BANK + (use // BANKS + 1))

    def wait_free(eng, b, use):
        eng.wait_ge(bank_taken[use % BANKS], b * PER_BANK + (use // BANKS + 1))

    def wait_taken(eng, b, use):
        eng.wait_ge(bank_taken[use % BANKS], b * PER_BANK + (use // BANKS + 2))

    GATE_SHARE = 1
    UP_LOGITS, UP_MIX, UP_SHARE = 0, 2, 3
    GATE_USES, UP_USES = CHUNKS + 1, CHUNKS + 3

    def gate_use(c):
        return c + 1 if c else 0

    def up_use(c):
        return c + 3 if c else 1

    def wait_gate_taken(eng, b, use):
        eng.wait_ge(gate_taken, GATE_USES * b + use + 2)

    def wait_up_taken(eng, b, use):
        eng.wait_ge(up_taken, UP_USES * b + use + 2)

    ORDER = "LEELEELEELEEELEELEELEELEELEELEELEELELLELELEELEELELEELEELELELLELEEELELELEELEELEOOOEOEOE"
    STEPS = dict(L=30, E=3 * CHUNKS, O=5)
    assert all(ORDER.count(part) == n for part, n in STEPS.items())

    def interleave(layers, experts, opening):
        parts = dict(L=layers, E=experts, O=opening)
        for part in ORDER:
            next(parts[part], None)

    def alone(part):
        for _ in part:
            pass

    RAW = 512
    raw = [h[:] for h in hidden] + [s[:] for s in share] + \
        [x3[:, 2 * half:2 * half + 2].rearrange("p t d -> p (t d)") for half in range(2)]

    def flat(ap):
        names = "abcd"[:len(ap.shape) - 1]
        return ap if len(names) == 1 else ap.rearrange(f"p {' '.join(names)} -> p ({' '.join(names)})")

    pieces = []
    for c in range(KC):
        for lo, hi in ((0, 2 * D), (2 * D, 3 * D)):
            pieces.append((weights["qkv"][:, c, lo:hi], *[x[:, c, lo:hi] for x in qkv]))
    EARLY = len(pieces)
    for c in range(CHUNKS):
        pieces.append((flat(weights["gate_up"][c]), *[flat(x[:, c]) for x in gate_up]))
        pieces.append((weights["down"][c], *[x[:, c] for x in down]))

    def raw_piece(n):
        return raw[n % len(raw)][:, 0:pieces[n][1].shape[1]]

    def between(splitting, layers):
        for _ in layers:
            for _ in range(2):
                next(splitting, None)

    first_loads = [(power, tables["power"]), (ident, tables["ident"]), (ffn_w, weights["ffn_w"]),
                   (ffn_scale, weights["ffn_scale"])]
    loads = [(wo, weights["wo"]), (rms_w, weights["rms_w"])] + \
            [(t, tables[x]) for x, t in dict(
                cos=cos, sin=sin, decay=decay, q_decay=q_decay, k_decay=k_decay, own_head=own_head,
                chunk_decay=chunk_decay, spread=spread, descending=descending).items()]
    FIRST_LOADED, LOADED = 16 * len(first_loads), 16 * len(loads)
    BEFORE_TILES = 8

    def begin(layers):
        for _ in range(BEFORE_TILES):
            next(layers)
            yield

    block = m.stack.enter_context(nc.Block())

    @block.sync
    def _(sp):
        def tokens(dram):
            return dram.rearrange("(t p) d -> p t d", p=P)

        sp.dma_start(x1[:], tokens(y_scratch[0])).then_inc(y_in, 16)
        for dst, src in first_loads:
            sp.dma_start(dst[:], src).then_inc(first_loaded, 16)
        for n, (src, _, _) in enumerate(pieces):
            if n == EARLY:
                for dst, constant in loads:
                    sp.dma_start(dst[:], constant).then_inc(loaded, 16)
            if n >= len(raw):
                sp.wait_ge(weights_low, n - len(raw) + 1)
            sp.dma_start(raw_piece(n), src).then_inc(raw_loaded[n % len(raw)], 16)

        def store(b):
            sp.wait_ge(result_ready, b + 1)
            sp.dma_start(tokens(result[b]), total[:]).then_inc(result_out, 16)

        def load(b):
            sp.wait_ge(x3_done, b)
            sp.dma_start(x1[:], tokens(y_scratch[b])).then_inc(y_in, 16)

        load(1)
        with sp.Fori(0, batches - 2) as b:
            load(b + 2)
            store(b)
        store(batches - 2)
        store(batches - 1)
        sp.wait_ge(result_out, 16 * batches + RESULT_FREE)


    @block.gpsimd
    def _(pool):
        pool.wait_ge(first_loaded, FIRST_LOADED)
        pool.memset(qk_pad[:], 0.0).then_inc(consts, 1)
        pool.memset(kd_pad[:], 0.0).then_inc(consts, 1)
        pool.memset(v_pad[:], 0.0).then_inc(consts, 1)
        pool.memset(ones[:], 1.0).then_inc(consts, 1)
        pool.memset(state[:], 0.0).then_inc(state_ready, 1)

        def root(dst, src, which):
            return pool.tensor_tensor(dst, src, power[:, which, 0:dst.shape[1]], ALU.pow)

        def layer_inverse(stats_sem, count, chain, chain_value, signal):
            pool.wait_ge(stats_sem, count)
            pool.sem_inc(pool_passed, 1)
            pool.tensor_scalar(variance[:], moments[:, :, 1], LN_EPS, 1.0, ALU.add, ALU.mult)\
                .then_inc(chain, 1)
            pool.wait_ge(chain, chain_value)
            root(inverse[:], variance[:], 0).then_inc(signal, 1)

        CHAIN = 3

        def layers(b):
            layer_inverse(stats_done, 3 * b + 1, pool_chain, CHAIN * b + 1, inverse_done)
            yield
            yield
            yield
            pool.wait_ge(squares_done, b + 1)
            root(norm[:, 0], squares[:], 1).then_inc(norms_done, 1)
            yield
            yield
            layer_inverse(stats_done, 3 * b + 2, pool_chain, CHAIN * b + 2, inverse_done)
            yield
            yield
            yield
            for t in range(T):
                half = E1 // 2
                wait_taken(pool, b, at(t, QK_))
                s = sin[:, t, None, :].broadcast_to([P, 2 * H1, E1])
                pool.tensor_tensor(swapped[:, :, 0:half], qk[:, :, half:E1], s[:, :, 0:half], ALU.mult)
                pool.tensor_tensor(swapped[:, :, half:E1], qk[:, :, 0:half], s[:, :, half:E1], ALU.mult)\
                    .then_inc(swapped_done, 1)
                yield
                pool.wait_ge(rotated, T * b + t + 1)
                pool.tensor_tensor(kd_pad[:, :, 0:E1], qk_pad[:, H1:, 0:E1],
                                   k_decay[:, :, None].broadcast_to([P, H1, E1]), ALU.mult).then_inc(kd_done, 1)
                yield
                wait_bank(pool, b, at(t, SCORES + PER_BLOCK - 1))
                pool.tensor_tensor(qt_decayed[:], qt[:], q_decay[:], ALU.mult).then_inc(decayed_done, 1)
                yield
                wait_bank(pool, b, at(t, MIXED))
                if t < T - 1:
                    pool.tensor_tensor(state[:], state[:], chunk_decay[:, :, None].broadcast_to([P, BLOCKS, P]),
                                       ALU.mult).then_inc(state_faded, 1)
                    pool.wait_ge(state_faded, (T - 1) * b + t + 1)
                    wait_taken(pool, b, at(t, UPDATE))
                    pool.tensor_tensor(state[:], state[:], update[:].rearrange("p (g n) -> p g n", g=BLOCKS),
                                       ALU.add).then_inc(state_ready, 1)
                else:
                    pool.sem_inc(pool_passed, 1)
                    pool.memset(state[:], 0.0).then_inc(state_ready, 1)
                yield
                pool.wait_ge(attn_variance_done, T * b + t + 1)
                root(attn_inverse[:, t:t + 1], attn_variance[:, t:t + 1], 0).then_inc(attn_inverse_done, 1)
                if t == T - 1:
                    layer_inverse(stats_done, 3 * b + 3, pool_chain, CHAIN * b + 3, inverse_done)
                yield
            yield

        def opening(b, first=False):
            for _ in range(4):
                yield
            wait_gate_taken(pool, b, GATE_SHARE)
            wait_up_taken(pool, b, UP_SHARE)
            weight(b, 0)

        def experts(b):
            for c in range(1, CHUNKS):
                yield
                weight(b, c)
                yield
                yield
            yield
            layer_inverse(final_stats, b + 1, final_chain, b + 1, final_inverse)
            yield

        def weight(b, c):
            wait_up_taken(pool, b, up_use(c))
            h = hidden[c % SLOTS][:]
            pool.tensor_tensor(h, h, share[SHARED[c]][:], ALU.mult).then_inc(weighted, 1)

        first = layers(0)
        alone(begin(first))
        pool.wait_ge(loaded, LOADED)
        alone(first)
        alone(opening(0, first=True))
        with pool.Fori(0, batches - 1) as b:
            interleave(layers(b + 1), experts(b), opening(b + 1))
        alone(experts(batches - 1))

    @block.tensor
    def _(pe):
        def transposes(b, use, src, col):
            wait_free(pe, b, use)
            for t in range(T):
                last = pe.transpose(bank_of(use)[:, t * P:(t + 1) * P], src[:, t, col:col + P], ident[:])
            last.then_inc(bank_ready[use % BANKS], 1)

        def layers(b):
            yield
            yield
            pe.wait_ge(x1_done, b + 1)
            for c in range(KC):
                transposes(b, X1T + c, x1, c * P)
            yield
            for c in range(KC):
                wait_taken(pe, b, X1T + c)
            for half in range(2):
                wait_free(pe, b, FFN + half)
                for t in range(2):
                    row = (2 * half + t) * P
                    for c in range(KC):
                        last = pe.matmul(bank_of(FFN + half)[:, t * D:(t + 1) * D], x1t[:, c, row:row + P],
                                         ffn_w[:, c], start=(c == 0), stop=(c == KC - 1))
                last.then_inc(bank_ready[(FFN + half) % BANKS], 1)
            yield
            yield
            yield
            yield
            pe.wait_ge(x2_done, b + 1)
            for c in range(KC):
                transposes(b, X2T + c, x2, c * P)
            yield
            for c in range(KC):
                wait_taken(pe, b, X2T + c)
            for t in range(T):
                row = t * P
                for use, lo, hi in ((QK_, 0, 2 * D), (V_, 2 * D, 3 * D)):
                    wait_free(pe, b, at(t, use))
                    for n, (p, c) in enumerate((p, c) for c in range(KC) for p in PASSES):
                        last = pe.matmul(bank_of(at(t, use))[:, 0:hi - lo], x2t[p[0]][:, c, row:row + P],
                                         qkv[p[1]][:, c, lo:hi], start=(n == 0), stop=(n == 3 * KC - 1))
                    last.then_inc(bank_ready[at(t, use) % BANKS], 1)
                yield
                pe.wait_ge(rotated, T * b + t + 1)
                for use, first in ((QT, 0), (KT, H1)):
                    wait_free(pe, b, at(t, use))
                    for g in range(BLOCKS):
                        heads = qk_pad[:, first + g * PER_BLOCK:first + (g + 1) * PER_BLOCK]
                        last = pe.transpose(bank_of(at(t, use))[:, g * P:(g + 1) * P],
                                            heads.rearrange("p a b -> p (a b)"), ident[:])
                    last.then_inc(bank_ready[at(t, use) % BANKS], 1)
                yield
                for use in (QT, KT):
                    wait_taken(pe, b, at(t, use))
                for j in range(PER_BLOCK):
                    wait_free(pe, b, at(t, SCORES + j))
                for g in range(BLOCKS):
                    for j in range(PER_BLOCK):
                        rows = slice(j * PAD, j * PAD + E1)
                        last = pe.matmul(bank_of(at(t, SCORES + j))[:, g * P:(g + 1) * P],
                                         kt[rows, g * P:(g + 1) * P], qt[rows, g * P:(g + 1) * P],
                                         start=True, stop=True)
                        if g == BLOCKS - 1:
                            last.then_inc(bank_ready[at(t, SCORES + j) % BANKS], 1)
                yield
                wait_taken(pe, b, at(t, V_))
                wait_free(pe, b, at(t, MIXED))
                mixed = bank_of(at(t, MIXED))
                for j in range(PER_BLOCK):
                    wait_taken(pe, b, at(t, SCORES + j))
                    for g in range(BLOCKS):
                        pe.matmul(mixed[j * PAD:(j + 1) * PAD, g * P:(g + 1) * P],
                                  v_pad[:, g * PER_BLOCK + j], masked[:, j, g * P:(g + 1) * P],
                                  start=(g == 0), stop=False, skip_group_check=True)
                pe.wait_ge(state_ready, T * b + t + 1)
                pe.wait_ge(decayed_done, T * b + t + 1)
                for g in range(BLOCKS):
                    last = pe.matmul(mixed[:, g * P:(g + 1) * P], state[:, g], qt_decayed[:, g * P:(g + 1) * P],
                                     start=False, stop=True, skip_group_check=True)
                last.then_inc(bank_ready[at(t, MIXED) % BANKS], 1)
                pe.wait_ge(kd_done, T * b + t + 1)
                wait_free(pe, b, at(t, UPDATE))
                for g in range(BLOCKS):
                    keys, values = (x[:, g * PER_BLOCK:(g + 1) * PER_BLOCK].rearrange("p a b -> p (a b)")
                                    for x in (kd_pad, v_pad))
                    last = pe.matmul(bank_of(at(t, UPDATE))[:, g * P:(g + 1) * P], keys, values,
                                     start=True, stop=True)
                last.then_inc(bank_ready[at(t, UPDATE) % BANKS], 1)
                yield
                wait_free(pe, b, at(t, OUT))
                pe.wait_ge(attn_t_done, T * b + t + 1)
                for g in range(BLOCKS):
                    pe.matmul(bank_of(at(t, OUT))[:, 0:D], attn_t[:, g * P:(g + 1) * P], wo[:, g],
                              start=(g == 0), stop=(g == BLOCKS - 1))
                wait_taken(pe, b, at(t, MIXED))
                for g in range(BLOCKS):
                    last = pe.matmul(bank_of(at(t, OUT))[:, D:D + 1], attn_t_squares[:, g * P:(g + 1) * P], ones[:],
                                     start=(g == 0), stop=(g == BLOCKS - 1))
                last.then_inc(bank_ready[at(t, OUT) % BANKS], 1)
                yield
            yield
            pe.wait_ge(x3_done, b + 1)
            for c in range(KC):
                transposes(b, X3T + c, x2, c * P)

        def free(taken, number):
            pe.wait_ge(taken, number + 1)

        def expand(b, c, which, target, use, taken, ready):
            free(taken, use)
            for n, (p, k) in enumerate((p, k) for k in range(KC) for p in PASSES):
                last = pe.matmul(target[:], gate_up[p[0]][:, c, which, k], x3t[p[1]][:, k],
                                 start=(n == 0), stop=(n == 3 * KC - 1))
            last.then_inc(ready, 1)

        def gate(b, c):
            expand(b, c, 0, gate_bank, GATE_USES * b + gate_use(c), gate_taken, gate_ready)

        def up(b, c):
            expand(b, c, 1, up_bank, UP_USES * b + up_use(c), up_taken, up_ready)

        def contract(b, c):
            pe.wait_ge(hidden_low, CHUNKS * b + c + 1)
            for t in range(T):
                for n, p in enumerate(PASSES):
                    last = pe.matmul(out[t // 2][:, t % 2], hidden_split[c % SLOTS][p[0]][:, t * P:(t + 1) * P],
                                     down[p[1]][:, c], start=(c == 0 and n == 0 and t % 2 == 0),
                                     stop=(c == CHUNKS - 1 and n == 2), skip_group_check=True)
            last.then_inc(down_done, 1)

        def opening(b, first=False):
            for c in range(KC):
                wait_taken(pe, b, X3T + c)
            gate(b, 0)
            yield
            pe.wait_ge(logits_t_done, b + 1)
            free(up_taken, UP_USES * b + UP_LOGITS)
            for t in range(T):
                last = pe.matmul(up_bank[:, t * ROUTER:(t + 1) * ROUTER], logits_t[:, t * P:(t + 1) * P],
                                 ident[LOGIT_ROWS, REST:REST + ROUTER], start=True, stop=True)
            last.then_inc(up_ready, 1)
            yield
            up(b, 0)
            yield
            pe.wait_ge(mix_done, b + 1)
            free(up_taken, UP_USES * b + UP_MIX)
            for t in range(T):
                last = pe.matmul(up_bank[0:EXPERTS + 1, t * P:(t + 1) * P], mix[:, t], ident[:],
                                 start=True, stop=True)
            last.then_inc(up_ready, 1)
            yield
            wait_up_taken(pe, b, UP_MIX)
            free(gate_taken, GATE_USES * b + GATE_SHARE)
            pe.matmul(gate_bank[:], spread[0:EXPERTS + 1, 0], mix_t, start=True, stop=True).then_inc(gate_ready, 1)
            free(up_taken, UP_USES * b + UP_SHARE)
            pe.matmul(up_bank[:], spread[0:EXPERTS + 1, 1], mix_t, start=True, stop=True).then_inc(up_ready, 1)

        def experts(b):
            for c in range(1, CHUNKS):
                gate(b, c)
                yield
                up(b, c)
                yield
                if c == 1:
                    pe.wait_ge(moe_done, b + 1)
                contract(b, c - 1)
                yield
            contract(b, CHUNKS - 1)
            yield
            yield

        pe.wait_ge(first_loaded, FIRST_LOADED)
        pe.wait_ge(ffn_scaled, 1)
        first = layers(0)
        alone(begin(first))
        pe.wait_ge(loaded, LOADED)
        pe.wait_ge(consts, 5)
        pe.wait_ge(weights_low, EARLY)
        alone(first)
        pe.wait_ge(weights_low, len(pieces))
        alone(opening(0, first=True))
        with pe.Fori(0, batches - 1) as b:
            interleave(layers(b + 1), experts(b), opening(b + 1))
        alone(experts(batches - 1))

    @block.scalar
    def _(act):
        def layers(b):
            yield
            yield
            wait_bank(act, b, X1T)
            act.activation(x1t[:, 0], bank_of(X1T)[:], ACT.Copy).then_inc(bank_taken[X1T % BANKS], 1)
            yield
            act.wait_ge(result_out, 16 * b + 1)
            for half in range(2):
                wait_bank(act, b, FFN + half)
                act.activation(x2[:, 2 * half:2 * half + 2], bank_of(FFN + half)[:].rearrange("p (t n) -> p t n", t=2),
                               ACT.Copy).then_inc(bank_taken[(FFN + half) % BANKS], 1)
            for half in range(2):
                wait_taken(act, b, FFN + half)
            for t in range(T):
                last = act.activation(x2_squares[:, t], x2[:, t], ACT.Square, accum_out=squares[:, t:t + 1])
            last.then_inc(squares_done, 1)
            yield
            act.wait_ge(norm_floored, b + 1)
            act.activation(norm[:, 2], norm[:, 1], ACT.Tanh).then_inc(tanh_done, 1)
            yield
            yield
            yield
            for c in range(KC):
                wait_bank(act, b, X2T + c)
                act.activation(x2t[HI][:, c], bank_of(X2T + c)[:], ACT.Copy).then_inc(x2t_high, 1)
            yield
            for t in range(T):
                wait_bank(act, b, at(t, QK_))
                act.activation(qk[:].rearrange("p a b -> p (a b)"), bank_of(at(t, QK_))[:], ACT.Copy)\
                    .then_inc(bank_taken[at(t, QK_) % BANKS], 1)
                wait_bank(act, b, at(t, V_))
                act.activation(v_pad[:, :, 0:E1], bank_of(at(t, V_))[:, 0:D].rearrange("p (h e) -> p h e", h=H1),
                               ACT.Copy).then_inc(bank_taken[at(t, V_) % BANKS], 1)
                yield
                for use, dst in ((QT, qt), (KT, kt)):
                    wait_bank(act, b, at(t, use))
                    act.activation(dst[:], bank_of(at(t, use))[:], ACT.Copy).then_inc(bank_taken[at(t, use) % BANKS], 1)
                yield
                yield
                wait_bank(act, b, at(t, MIXED))
                mixed = bank_of(at(t, MIXED))[:]
                act.activation(attn_t[:], mixed, ACT.Copy).then_inc(attn_t_done, 1)
                act.activation(attn_t_squares[:], mixed, ACT.Square).then_inc(bank_taken[at(t, MIXED) % BANKS], 1)
                yield
                yield
            yield
            for c in range(KC):
                wait_bank(act, b, X3T + c)
                act.activation(x3t[HI][:, c], bank_of(X3T + c)[:], ACT.Copy).then_inc(x3t_high, 1)

        def tanh(b, c):
            act.wait_ge(gate_ready, GATE_USES * b + gate_use(c) + 1)
            act.activation(hidden[c % SLOTS][:], gate_bank[:], ACT.Tanh, scale=0.5).then_inc(tanh_gate, 1)

        def high(b, c):
            act.wait_ge(weighted, CHUNKS * b + c + 1)
            act.activation(hidden_split[c % SLOTS][HI][:], hidden[c % SLOTS][:], ACT.Copy)\
                .then_inc(hidden_high, 1)

        def opening(b, first=False):
            if not first:
                act.wait_ge(hidden_low, CHUNKS * b)
            act.wait_ge(gate_ready, GATE_USES * b + 1)
            act.activation(logits_t, gate_bank[LOGIT_ROWS], ACT.Copy).then_inc(logits_t_done, 1)
            tanh(b, 0)
            yield
            act.wait_ge(gap_done, b + 1)
            act.activation(best[:, 4], best[:, 3], ACT.Tanh, scale=0.5)
            act.activation(best[:, 5], logits[:, :, EXPERTS], ACT.Tanh, scale=0.5).then_inc(tanh_mix, 1)
            yield
            act.wait_ge(x3_done, b + 1)
            act.wait_ge(moe_done, b + 1)
            act.activation(x3[:], x2[:], ACT.Copy).then_inc(x3_kept, 1)
            yield
            yield
            act.wait_ge(gate_ready, GATE_USES * b + GATE_SHARE + 1)
            act.activation(share[0][:], gate_bank[:], ACT.Copy).then_inc(gate_taken, 1)

        def experts(b):
            for c in range(1, CHUNKS):
                tanh(b, c)
                high(b, c - 1)
                yield
                yield
                if c == CHUNKS - 1:
                    high(b, c)
                yield
            yield
            yield

        def splitting(numbers):
            for n in numbers:
                act.wait_ge(raw_loaded[n % len(raw)], 16 * (n // len(raw) + 1))
                act.activation(pieces[n][1], raw_piece(n), ACT.Copy).then_inc(weights_high, 1)
                yield

        act.wait_ge(ffn_scaled, 1)
        alone(splitting(range(EARLY)))
        first, later = layers(0), splitting(range(EARLY, len(pieces)))
        alone(begin(first))
        act.wait_ge(consts, 5)
        between(later, first)
        alone(later)
        act.wait_ge(weights_low, len(pieces))
        alone(opening(0, first=True))
        with act.Fori(0, batches - 1) as b:
            interleave(layers(b + 1), experts(b), opening(b + 1))
        alone(experts(batches - 1))

    @block.vector
    def _(dve):
        dve.wait_ge(first_loaded, FIRST_LOADED)
        dve.tensor_tensor(ffn_w[:], ffn_w[:], ffn_scale[:, None, :].broadcast_to([P, KC, D]), ALU.mult)\
            .then_inc(ffn_scaled, 1)
        for s in bank_taken + [gate_taken, up_taken, moe_done]:
            dve.sem_inc(s, 1)
        dve.sem_inc(result_out, RESULT_FREE)
        FRONT_LINKS, OPENING_LINKS, EXPERTS_LINKS = 20, 13, 2

        class Chain:

            def __init__(self, sem, base, links):
                self.sem, self.base, self.n, self.links = sem, base, 0, links

            def link(self, instruction):
                instruction.then_inc(self.sem, 1)
                self.n += 1
                dve.wait_ge(self.sem, self.base + self.n)

            def close(self):
                assert self.n == self.links, self.n

        def statistics(chain, src, signal, tiles=range(T)):
            for t in tiles:
                last = dve.bn_stats(stats[:, t], src[:, t])
            chain.link(last)
            dve.sem_inc(dve_passed, 1)
            for t in range(T):
                last = dve.bn_aggr(moments[:, t], stats[:, t])
            last.then_inc(signal, 1)

        def normalise(src, dst, signal):
            for t in range(T):
                last = dve.tensor_scalar(dst[:, t], src[:, t], moments[:, t, 0:1], inverse[:, t:t + 1],
                                         ALU.subtract, ALU.mult)
            last.then_inc(signal, 1)

        def layers(b):
            chain = Chain(front_chain, b * FRONT_LINKS, FRONT_LINKS)
            link = chain.link
            dve.wait_ge(y_in, 16 * b + 16)
            statistics(chain, x1, stats_done)
            yield
            dve.wait_ge(inverse_done, 3 * b + 1)
            normalise(x1, x1, x1_done)
            yield
            wait_bank(dve, b, X1T + 1)
            dve.tensor_copy(x1t[:, 1], bank_of(X1T + 1)[:]).then_inc(bank_taken[(X1T + 1) % BANKS], 1)
            yield
            yield
            dve.wait_ge(norms_done, b + 1)
            root, floored, tanh, shrink = norm[:, 0], norm[:, 1], norm[:, 2], norm[:, 3]
            tmp, tmp2, factor = norm[:, 4], norm[:, 5], norm[:, 6]
            dve.tensor_scalar(floored, root, NORM_EPS, None, ALU.max).then_inc(norm_floored, 1)
            dve.wait_ge(norm_floored, b + 1)
            link(dve.tensor_scalar(tmp, floored, NORM_EPS, None, ALU.add))
            link(dve.reciprocal(tmp2, tmp))
            dve.wait_ge(tanh_done, b + 1)
            link(dve.tensor_tensor(shrink, tanh, tmp2, ALU.mult))
            link(dve.tensor_tensor(tmp, shrink, root, ALU.mult))
            link(dve.tensor_scalar(tmp2, tmp, NORM_EPS, None, ALU.max))
            link(dve.reciprocal(tmp, tmp2))
            link(dve.tensor_scalar(tmp2, tmp, MAX_NORM, 1.0, ALU.mult, ALU.min))
            link(dve.tensor_tensor(factor, shrink, tmp2, ALU.mult))
            for t in range(T):
                last = dve.scalar_tensor_tensor(x2[:, t], x2[:, t], factor[:, t:t + 1], x1[:, t],
                                                ALU.mult, ALU.add)
            link(last)
            yield
            statistics(chain, x2, stats_done)
            yield
            dve.wait_ge(inverse_done, 3 * b + 2)
            normalise(x2, x2, x2_done)
            yield
            for c in range(KC):
                dve.wait_ge(x2t_high, KC * b + c + 1)
                dve.tensor_tensor(x2t[LO][:, c], bank_of(X2T + c)[:], x2t[HI][:, c].bitcast(F32), ALU.subtract)\
                    .then_inc(bank_taken[(X2T + c) % BANKS], 1)
            yield
            for t in range(T):
                wait_taken(dve, b, at(t, QK_))
                c = cos[:, t, None, :].broadcast_to([P, 2 * H1, E1])
                link(dve.tensor_tensor(qk_pad[:, :, 0:E1], qk[:], c, ALU.mult))
                dve.wait_ge(swapped_done, T * b + t + 1)
                dve.tensor_tensor(qk_pad[:, :, 0:E1], qk_pad[:, :, 0:E1], swapped[:], ALU.add)\
                    .then_inc(rotated, 1)
                yield
                yield
                dve.wait_ge(state_ready, T * b + t + 1)
                for j in range(PER_BLOCK):
                    wait_bank(dve, b, at(t, SCORES + j))
                    dve.tensor_tensor(masked[:, j], bank_of(at(t, SCORES + j))[:], decay[:, j], ALU.mult)\
                        .then_inc(bank_taken[at(t, SCORES + j) % BANKS], 1)
                yield
                wait_bank(dve, b, at(t, UPDATE))
                if t < T - 1:
                    dve.tensor_tensor(update[:].rearrange("p (g n) -> p g n", g=BLOCKS),
                                      bank_of(at(t, UPDATE))[:].rearrange("p (g n) -> p g n", g=BLOCKS),
                                      own_head[:, None, :].broadcast_to([P, BLOCKS, P]), ALU.mult)\
                        .then_inc(bank_taken[at(t, UPDATE) % BANKS], 1)
                else:
                    dve.sem_inc(bank_taken[at(t, UPDATE) % BANKS], 1)
                yield
                wait_bank(dve, b, at(t, OUT))
                dve.tensor_scalar(attn_variance[:, t:t + 1], bank_of(at(t, OUT))[:, D:D + 1], 1.0 / D, RMS_EPS,
                                  ALU.mult, ALU.add).then_inc(attn_variance_done, 1)
                dve.wait_ge(attn_inverse_done, T * b + t + 1)
                link(dve.scalar_tensor_tensor(x1[:, t], bank_of(at(t, OUT))[:, 0:D], attn_inverse[:, t:t + 1],
                                              x2[:, t], ALU.mult, ALU.add))
                dve.sem_inc(bank_taken[at(t, OUT) % BANKS], 1)
                if t < T - 1:
                    dve.bn_stats(stats[:, t], x1[:, t])
                else:
                    statistics(chain, x1, stats_done, (t,))
                yield
            dve.wait_ge(inverse_done, 3 * b + 3)
            normalise(x1, x2, x3_done)
            yield
            for c in range(KC):
                dve.wait_ge(x3t_high, KC * b + c + 1)
                dve.tensor_tensor(x3t[LO][:, c], bank_of(X3T + c)[:], x3t[HI][:, c].bitcast(F32), ALU.subtract)\
                    .then_inc(bank_taken[(X3T + c) % BANKS], 1)
            chain.close()

        def activated(b, c):
            h = hidden[c % SLOTS][:]
            dve.wait_ge(tanh_gate, CHUNKS * b + c + 1)
            dve.scalar_tensor_tensor(h, h, 1.0, gate_bank[:], ALU.add, ALU.mult).then_inc(gate_taken, 1)

        def product(b, c):
            h = hidden[c % SLOTS][:]
            wait_gate_taken(dve, b, gate_use(c))
            dve.wait_ge(up_ready, UP_USES * b + up_use(c) + 1)
            dve.tensor_tensor(h, up_bank[:], h, ALU.mult).then_inc(up_taken, 1)

        def low(b, c):
            dve.wait_ge(hidden_high, CHUNKS * b + c + 1)
            dve.tensor_tensor(hidden_split[c % SLOTS][LO][:], hidden[c % SLOTS][:],
                              hidden_split[c % SLOTS][HI][:].bitcast(F32), ALU.subtract).then_inc(hidden_low, 1)

        def opening(b, first=False):
            chain = Chain(opening_chain, b * OPENING_LINKS, OPENING_LINKS)
            link = chain.link
            activated(b, 0)
            yield
            dve.wait_ge(up_ready, UP_USES * b + UP_LOGITS + 1)
            dve.tensor_copy(logits[:].rearrange("p t n -> p (t n)"), up_bank[:, 0:T * ROUTER]).then_inc(up_taken, 1)
            wait_up_taken(dve, b, UP_LOGITS)
            level = logits[:, :, 0:EXPERTS]
            equal, rank, chosen1, rest, chosen2 = (pick[:, i] for i in range(5))
            m1, m2, first, gap, gap_tanh, gate_tanh, w1, w2 = (best[:, i] for i in range(8))

            def wide(x):
                return x[:, :, None].broadcast_to([P, T, EXPERTS])

            for source, top, chosen in ((level, m1, chosen1), (rest, m2, chosen2)):
                link(dve.tensor_reduce(top, source, AX.X, ALU.max))
                if chosen is chosen2:
                    dve.tensor_tensor(gap, m1, m2, ALU.subtract).then_inc(gap_done, 1)
                link(dve.tensor_tensor(equal, source, wide(top), ALU.is_equal))
                link(dve.tensor_tensor(rank, equal, descending[:], ALU.mult))
                link(dve.tensor_reduce(first, rank, AX.X, ALU.max))
                link(dve.tensor_tensor(chosen, descending[:], wide(first), ALU.is_equal))
                if chosen is chosen1:
                    link(dve.scalar_tensor_tensor(rest, chosen, -MASKED, level, ALU.mult, ALU.add))
            dve.wait_ge(tanh_mix, b + 1)
            dve.tensor_scalar(w1, gap_tanh, 0.25, 0.25, ALU.mult, ALU.add)
            link(dve.tensor_scalar(w2, gap_tanh, -0.25, 0.25, ALU.mult, ALU.add))
            dve.tensor_tensor(equal, chosen1, wide(w1), ALU.mult)
            dve.tensor_scalar(mix[:, :, EXPERTS], gate_tanh, 0.25, 0.25, ALU.mult, ALU.add)
            link(dve.tensor_tensor(rank, chosen2, wide(w2), ALU.mult))
            dve.tensor_tensor(mix[:, :, 0:EXPERTS], equal, rank, ALU.add).then_inc(mix_done, 1)
            yield
            product(b, 0)
            yield
            dve.wait_ge(up_ready, UP_USES * b + UP_MIX + 1)
            dve.tensor_copy(mix_t, up_bank[0:EXPERTS + 1, :]).then_inc(up_taken, 1)
            yield
            dve.wait_ge(up_ready, UP_USES * b + UP_SHARE + 1)
            dve.tensor_copy(share[1][:], up_bank[:]).then_inc(up_taken, 1)
            chain.close()

        def experts(b):
            chain = Chain(experts_chain, b * EXPERTS_LINKS, EXPERTS_LINKS)
            link = chain.link
            for c in range(1, CHUNKS):
                activated(b, c)
                low(b, c - 1)
                yield
                product(b, c)
                yield
                if c == CHUNKS - 1:
                    low(b, c)
                yield
            dve.wait_ge(x3_kept, b + 1)
            dve.wait_ge(down_done, CHUNKS * b + CHUNKS)
            dve.wait_ge(result_out, 16 * b + RESULT_FREE)
            for half in range(2):
                part = slice(2 * half, 2 * half + 2)
                last = dve.tensor_tensor(total[:, part], out[half][:], x3[:, part], ALU.add)
            link(last)
            dve.sem_inc(moe_done, 1)
            yield
            statistics(chain, total, final_stats)
            yield
            dve.wait_ge(final_inverse, b + 1)
            normalise(total, total, result_ready)
            chain.close()

        def splitting(numbers):
            for n in numbers:
                _, high, low_part = pieces[n]
                dve.wait_ge(weights_high, n + 1)
                dve.tensor_tensor(low_part, raw_piece(n), high.bitcast(F32), ALU.subtract).then_inc(weights_low, 1)
                yield

        alone(splitting(range(EARLY)))
        first, later = layers(0), splitting(range(EARLY, len(pieces)))
        alone(begin(first))
        dve.wait_ge(loaded, LOADED)
        for g in range(BLOCKS):
            last = dve.tensor_scalar(wo[:, g], wo[:, g], rms_w[:, g:g + 1], None, ALU.mult)
        last.then_inc(consts, 1)
        dve.wait_ge(consts, 5)
        between(later, first)
        alone(later)
        alone(opening(0, first=True))
        with dve.Fori(0, batches - 1) as b:
            interleave(layers(b + 1), experts(b), opening(b + 1))
        alone(experts(batches - 1))


def two_block_kernel(nc, x_tokens, x_t, w_heads, slopes, *rest):
    result = rest[-1]
    weights = dict(zip(WEIGHTS, rest))
    tables = dict(zip(TABLES, rest[len(WEIGHTS):]))
    batches = result.shape[0]
    y_scratch = nc.dram_tensor("y_scratch", (batches, S, D), F32, kind="Internal").ap()
    softmax_attention(nc, x_tokens, x_t, w_heads, slopes, y_scratch)
    block_one(nc, y_scratch, weights, tables, result)


WEIGHTS = ("gate_up", "down", "qkv", "ffn_w", "ffn_scale", "wo", "rms_w")
TABLES = ("cos", "sin", "decay", "q_decay", "k_decay", "own_head", "chunk_decay", "spread", "ident",
          "descending", "power")


def alibi_slopes(heads):
    return [2.0 ** (-8.0 * (h + 1) / heads) for h in range(heads)]


def shape_tables():
    f32 = np.float32
    slopes = np.array(alibi_slopes(H1), f32)
    r = np.exp(-slopes)
    freq = (f32(1.0 / 1024.0) ** np.linspace(0.0, 1.0, E1 // 4, dtype=f32)).astype(f32)
    freq = np.concatenate([freq, np.zeros(E1 // 4, f32)])
    theta = np.arange(S, dtype=f32)[:, None] * freq[None, :]
    cos = np.concatenate([np.cos(theta)] * 2, axis=1)
    sin = np.concatenate([np.sin(theta), -np.sin(theta)], axis=1)

    def tiles(a):
        return a.reshape(T, P, -1).transpose(1, 0, 2)

    i = np.arange(P, dtype=f32)
    diff = i[None, :] - i[:, None]
    by_head = np.where(diff >= 0, r[:, None, None] ** np.maximum(diff, 0), 0)
    decay = by_head.reshape(BLOCKS, PER_BLOCK, P, P).transpose(2, 1, 0, 3).reshape(P, PER_BLOCK, BLOCKS * P)
    row = np.arange(P)
    own = (row[:, None] // PAD == row[None, :] // PAD) & ((row % PAD < E1)[:, None] & (row % PAD < E1)[None, :])
    row_r = np.repeat(r.reshape(BLOCKS, PER_BLOCK), PAD, axis=1).T
    spread = np.zeros((P, 2, P), f32)
    for e in range(EXPERTS):
        spread[e, 0, e * ROWS:(e + 1) * ROWS] = 1.0
    spread[EXPERTS, 1] = 1.0
    tables = dict(
        cos=tiles(cos), sin=tiles(sin), decay=decay,
        q_decay=(row_r[:, :, None] ** (i[None, None, :] + 1)).reshape(P, BLOCKS * P),
        k_decay=r[None, :] ** (P - 1 - i[:, None]),
        own_head=own, chunk_decay=row_r ** f32(P),
        spread=spread, ident=np.eye(P),
        descending=np.broadcast_to(EXPERTS - np.arange(EXPERTS), (P, T, EXPERTS)),
        power=np.broadcast_to(np.array([-0.5, 0.5])[None, :, None], (P, 2, T)))
    return [np.ascontiguousarray(tables[x], dtype=f32) for x in TABLES]


def by_row(a):
    return a.reshape(KC, P, -1).transpose(1, 0, 2)


def by_head(a):
    padded = np.zeros((H1, PAD, a.shape[1]), a.dtype)
    padded[:, :E1] = a.reshape(H1, E1, -1)
    return padded.reshape(BLOCKS, P, -1).transpose(1, 0, 2)


def pack_attention(Wq, Wk, Wv, Wo):
    qkv = [w.reshape(H0, DH, KC, P).transpose(0, 3, 2, 1).reshape(H0, P, KC * DH) for w in (Wq, Wk, Wv)]
    return np.concatenate(qkv + [Wo.reshape(D, H0, DH).transpose(1, 2, 0)], axis=2)


EXPERT_WEIGHTS = ("gate_up_proj", "down_proj", "sh_gate_w", "sh_up_w", "sh_down_w", "router_weight",
                  "shared_gate_w")


def pack_experts(gate_up_proj, down_proj, sh_gate_w, sh_up_w, sh_down_w, router_weight, shared_gate_w):
    def chunks(experts, shared, after=()):
        n = shared.shape[1]
        e = iter(experts.reshape(EXPERTS, E_CHUNKS, ROWS, n).transpose(1, 0, 2, 3).reshape(E_CHUNKS, P, n))
        last = np.concatenate([shared[-REST:], *after])
        last = np.concatenate([last, np.zeros((P - len(last), n), shared.dtype)])
        s = iter([last, *shared[:-REST].reshape(-1, P, n)])
        return np.stack([next(s if x else e) for x in SHARED])

    gate = chunks(gate_up_proj[:, :I_MOE], sh_gate_w, (router_weight, shared_gate_w))
    up = chunks(gate_up_proj[:, I_MOE:], sh_up_w)
    both = np.stack([gate, up], axis=1).reshape(CHUNKS, 2, P, KC, P)
    return both.transpose(0, 4, 1, 3, 2), chunks(down_proj.transpose(0, 2, 1), sh_down_w.T)


def kernel(**inputs):
    import concourse.bacc as bacc
    from concourse.bass_utils import run_bass_kernel_spmd

    a = {k: np.asarray(v) for k, v in inputs.items()}
    x = a["L0_attn_resid_pre"]
    batches = x.shape[0]
    padded = np.concatenate([x, x[:1]])
    gate_up, down = pack_experts(*(a["L1_ffn_" + n] for n in EXPERT_WEIGHTS))
    arrays = [
        padded,
        padded.reshape(batches + 1, S, KC, P).transpose(0, 3, 2, 1),
        pack_attention(*(a["L0_attn_" + n] for n in ("Wq", "Wk", "Wv", "Wo"))),
        np.broadcast_to(np.array(alibi_slopes(H0), np.float32), (P, H0)),
        gate_up, down,
        by_row(np.concatenate([a["L1_attn_Wq"], a["L1_attn_Wk"], a["L1_attn_Wv"]], axis=1)),
        by_row(a["L0_ffn_weight"]),
        np.broadcast_to(a["L0_ffn_scale"], (P, D)),
        by_head(a["L1_attn_Wo"]),
        by_head(a["L1_attn_rms_w"][:, None])[:, :, 0],
    ] + shape_tables()
    names = ["x_tokens", "x_t", "w_heads", "slopes", *WEIGHTS, *TABLES]
    arrays = {f"in_{n}": np.ascontiguousarray(v) for n, v in zip(names, arrays)}
    nc = bacc.Bacc("TRN2", target_bir_lowering=False, num_devices=1)
    args = [nc.dram_tensor(n, v.shape, F32, kind="ExternalInput").ap() for n, v in arrays.items()]
    result = nc.dram_tensor("out_result", (batches, S, D), F32, kind="ExternalOutput").ap()
    two_block_kernel(nc, *args, result)
    run = run_bass_kernel_spmd(nc, [arrays], core_ids=[0])
    return run.results[0]["out_result"]
```
